# Optimizing a Trainium2 kernel written in Bass

```python
import numpy as np
import jax
import jax.numpy as jnp

def _softmax(x, axis=-1):
    return jax.nn.softmax(x, axis=axis)

def _gelu(x):
    return jax.nn.gelu(x, approximate=True)

def _silu(x):
    return jax.nn.silu(x)

def _sigmoid(x):
    return jax.nn.sigmoid(x)

def _layernorm(x, axis=-1, eps=1e-05):
    m = jnp.mean(x, axis=axis, keepdims=True)
    v = jnp.var(x, axis=axis, keepdims=True)
    return (x - m) / jnp.sqrt(v + eps)

def _scatter_add(tgt, idx, src, axis=0):
    return tgt.at[idx].add(src)

def _segment_sum(src, seg, n):
    return jax.ops.segment_sum(src, seg, n)
kernel_name = 'mk_flamingo_gated_d2_seqx_r8_d89b05'

def setup_inputs(seed: int=0):
    np.random.seed(seed)
    _w = jnp.asarray

    def _rec_inputs():
        import jax
        import jax.numpy as jnp
        _rk = jax.random.key(seed)
        x = -0.0003929 + 0.9999 * jax.random.normal(jax.random.fold_in(_rk, 1), (16, 64, 256), jnp.float32)
        _lenS = 64 - jax.random.randint(jax.random.fold_in(_rk, 7), (16,), 0, max(1, 64 // 4) + 1, jnp.int32)
        _lenS2 = 64 - jax.random.randint(jax.random.fold_in(_rk, 8), (16,), 0, max(1, 64 // 4) + 1, jnp.int32)
        _ctx_2048P = jax.random.normal(jax.random.fold_in(_rk, 11), (16, 16, 256), jnp.float32)
        _ctx_2048c = jax.random.dirichlet(jax.random.fold_in(_rk, 511), 0.3 * jnp.ones((16,), jnp.float32), (16, 64))
        _ctx_2048t = jnp.einsum('bsk,bkd->bsd', _ctx_2048c, _ctx_2048P)
        _ctx_2048t = _ctx_2048t * jax.lax.rsqrt(jnp.mean(jnp.square(_ctx_2048t)) + 1e-12) * 0.953939
        ctx_2048 = -0.000514642 + 1.00011 * (_ctx_2048t + 0.3 * jax.random.normal(jax.random.fold_in(_rk, 611), (16, 64, 256), jnp.float32))
        _validS = jnp.arange(64)[None, :] < _lenS[:, None]
        _validS2 = jnp.arange(64)[None, :] < _lenS2[:, None]
        _causal = jnp.tril(jnp.ones((64, 64), dtype=bool))
        mask_BxS2_ik0 = jnp.where(jnp.broadcast_to(_validS2[:, :], (16, 64)), 0, 1).astype(jnp.int32)
        _g = jax.random.normal(jax.random.fold_in(_rk, 9001), (2, 2), jnp.float32)
        _g = jnp.sign(_g) * jnp.maximum(jnp.abs(_g), 1.0) + (_g == 0) * 1.0
        g_xattn = _g[0]
        g_ffn = _g[1]
        return (x, ctx_2048, mask_BxS2_ik0, g_xattn, g_ffn)
    x, ctx_2048, mask_BxS2_ik0, g_xattn, g_ffn = _rec_inputs()

    def _L0_xattn_setup():
        import jax, jax.numpy as jnp
        import numpy as np
        import math
        H = 256
        NH = 16
        HD = H // NH
        EPS_LN = 1e-05
        RES_SCALE_MAX = 0.3

        def _nan_clean(x, lim=10000.0):
            return jnp.nan_to_num(x, nan=0.0, posinf=lim, neginf=-lim)
        key = jax.random.key(seed)
        ks = jax.random.split(key, 12)
        B, S, T = (4, 256, 32)
        std = 1.0 / math.sqrt(H)
        return {'hidden_states': jax.random.normal(ks[0], (B, S, H), jnp.float32), 'audio_tokens': jax.random.normal(ks[1], (B, T, H), jnp.float32), 'attention_mask': jax.random.randint(ks[2], (B, T), 0, 2, jnp.int32), 'Wq': jax.random.normal(ks[3], (H, H), jnp.float32) * std, 'bq': jnp.zeros((H,), jnp.float32), 'Wk': jax.random.normal(ks[4], (H, H), jnp.float32) * std, 'bk': jnp.zeros((H,), jnp.float32), 'Wv': jax.random.normal(ks[5], (H, H), jnp.float32) * std, 'bv': jnp.zeros((H,), jnp.float32), 'Wo': jax.random.normal(ks[6], (H, H), jnp.float32) * std, 'bo': jnp.zeros((H,), jnp.float32), 'ln_gamma': jnp.ones((H,), jnp.float32), 'ln_beta': jnp.zeros((H,), jnp.float32), 'residual_scale': jnp.float32(0.05)}
    _L0_xattn_all = _L0_xattn_setup()
    _L0_xattn_in = {k: v for k, v in _L0_xattn_all.items() if k in ('Wq', 'bq', 'Wk', 'bk', 'Wv', 'bv', 'Wo', 'bo', 'ln_gamma', 'ln_beta', 'residual_scale')}
    del _L0_xattn_all

    def _L0_ffn_setup():
        import jax, jax.numpy as jnp
        import numpy as np
        TOP_K = 2

        def _gelu(v):
            return jax.nn.gelu(v, approximate=False)
        key = jax.random.key(seed)
        ks = jax.random.split(key, 7)
        B, T, D, I, E = (2, 256, 256, 1024, 8)
        s = 0.02
        return {'x': jax.random.normal(ks[0], (B, T, D), jnp.float32), 'rw1': jax.random.normal(ks[1], (D, D // 2), jnp.float32) * s, 'rw2': jax.random.normal(ks[2], (D // 2, E), jnp.float32) * s, 'w1': jax.random.normal(ks[3], (E, D, I), jnp.float32) * s, 'b1': jax.random.normal(ks[4], (E, I), jnp.float32) * s, 'w2': jax.random.normal(ks[5], (E, I, D), jnp.float32) * s, 'b2': jax.random.normal(ks[6], (E, D), jnp.float32) * s}
    _L0_ffn_all = _L0_ffn_setup()
    _L0_ffn_in = {k: v for k, v in _L0_ffn_all.items() if k in ('rw1', 'rw2', 'w1', 'b1', 'w2', 'b2')}
    del _L0_ffn_all

    def _L1_xattn_setup():
        import math
        import jax, jax.numpy as jnp
        import numpy as np
        HEADS = 16
        MASKED_BIAS = -10000.0

        def _mha(q, k, v):
            B, Sq, D = q.shape
            Sk = k.shape[-2]
            hd = D // HEADS
            qh = q.reshape(B, Sq, HEADS, hd).transpose(0, 2, 1, 3)
            kh = k.reshape(B, Sk, HEADS, hd).transpose(0, 2, 1, 3)
            vh = v.reshape(B, Sk, HEADS, hd).transpose(0, 2, 1, 3)
            scores = jnp.einsum('bhqd,bhkd->bhqk', qh, kh) / math.sqrt(hd)
            qi = jnp.arange(Sq)[:, None] + (Sk - Sq)
            ki = jnp.arange(Sk)[None, :]
            causal = ki <= qi
            scores = jnp.where(causal[None, None], scores, jnp.asarray(MASKED_BIAS, scores.dtype))
            attn = jax.nn.softmax(scores, axis=-1)
            out = jnp.einsum('bhqk,bhkd->bhqd', attn, vh)
            return out.transpose(0, 2, 1, 3).reshape(B, Sq, D)
        key = jax.random.key(seed)
        kq, kk, kv = jax.random.split(key, 3)
        B, S, D = (4, 128, 256)
        q = jax.random.normal(kq, (B, S, D), dtype=jnp.float32)
        k = jax.random.normal(kk, (B, S, D), dtype=jnp.float32)
        v = jax.random.normal(kv, (B, S, D), dtype=jnp.float32)
        return {'q': q, 'k': k, 'v': v}
    _L1_xattn_all = _L1_xattn_setup()
    _L1_xattn_in = {k: v for k, v in _L1_xattn_all.items() if k in ()}
    del _L1_xattn_all

    def _L1_ffn_setup():
        import jax, jax.numpy as jnp
        import numpy as np
        B, S, H, I, E, F, K, R, TOPK = (1, 128, 256, 176, 64, 8, 8, 8, 6)
        ISH = 2 * I

        def _fused_linear(x, W, qa, qb, scale, w):
            out = x @ W.T
            a = jnp.einsum('th,krh->tkr', x, qa)
            b = jnp.einsum('tkr,khr->tkh', a, qb)
            mix = jnp.einsum('tkh,tk->th', b, w)
            return out + scale[None, :] * mix

        def _moe_forward(hidden_states, gate_weight, inv_mapping, mask_up_W, gate_W, gate_qa, gate_qb, gate_scale, up_W, up_qa, up_qb, up_scale, down_W, down_qa, down_qb, down_scale, sh_gate_W, sh_up_W, sh_down_W):
            b, s, h = hidden_states.shape
            x = hidden_states.reshape(-1, h)
            T = x.shape[0]
            scores = jax.nn.softmax(x @ gate_weight.T, axis=-1)
            topk_w, topk_idx = jax.lax.top_k(scores, TOPK)
            w_dense = jnp.zeros((T, E), x.dtype).at[jnp.arange(T)[:, None], topk_idx].add(topk_w)
            flat = w_dense[:, inv_mapping]
            scalar = flat.sum(-1)
            soft = jax.nn.softmax(jnp.where(flat == 0, -1000000000.0, flat), axis=-1)

            def expert(muW, gW, gqa, gqb, gs, uW, uqa, uqb, us, dW, dqa, dqb, ds, w):
                xe = x + w @ muW.T
                gate = jax.nn.silu(_fused_linear(xe, gW, gqa, gqb, gs, w))
                up = _fused_linear(xe, uW, uqa, uqb, us, w)
                return _fused_linear(gate * up, dW, dqa, dqb, ds, w)
            outs = jax.vmap(expert, in_axes=(0,) * 13 + (1,))(mask_up_W, gate_W, gate_qa, gate_qb, gate_scale, up_W, up_qa, up_qb, up_scale, down_W, down_qa, down_qb, down_scale, soft)
            y = jnp.einsum('fth,tf->th', outs, scalar).reshape(b, s, h)
            sh = jax.nn.silu(hidden_states @ sh_gate_W.T) * (hidden_states @ sh_up_W.T) @ sh_down_W.T
            return y + sh
        key = jax.random.key(seed)
        ks = jax.random.split(key, 20)
        g = lambda k, shape, s=0.02: jax.random.normal(k, shape, jnp.float32) * s
        return {'hidden_states': jax.random.normal(ks[0], (B, S, H), jnp.float32), 'gate_weight': g(ks[1], (E, H)), 'inv_mapping': jnp.arange(E, dtype=jnp.int32).reshape(F, K), 'mask_up_W': g(ks[2], (F, H, K)), 'gate_W': g(ks[3], (F, I, H)), 'gate_qa': g(ks[4], (F, K, R, H)), 'gate_qb': g(ks[5], (F, K, I, R)), 'gate_scale': jnp.full((F, I), 0.1, jnp.float32), 'up_W': g(ks[6], (F, I, H)), 'up_qa': g(ks[7], (F, K, R, H)), 'up_qb': g(ks[8], (F, K, I, R)), 'up_scale': jnp.full((F, I), 0.1, jnp.float32), 'down_W': g(ks[9], (F, H, I)), 'down_qa': g(ks[10], (F, K, R, I)), 'down_qb': g(ks[11], (F, K, H, R)), 'down_scale': jnp.full((F, H), 0.1, jnp.float32), 'sh_gate_W': g(ks[12], (ISH, H)), 'sh_up_W': g(ks[13], (ISH, H)), 'sh_down_W': g(ks[14], (H, ISH))}
    _L1_ffn_all = _L1_ffn_setup()
    _L1_ffn_in = {k: v for k, v in _L1_ffn_all.items() if k in ('gate_weight', 'inv_mapping', 'mask_up_W', 'gate_W', 'gate_qa', 'gate_qb', 'gate_scale', 'up_W', 'up_qa', 'up_qb', 'up_scale', 'down_W', 'down_qa', 'down_qb', 'down_scale', 'sh_gate_W', 'sh_up_W', 'sh_down_W')}
    del _L1_ffn_all
    return {'x': x, 'ctx_2048': ctx_2048, 'mask_BxS2_ik0': mask_BxS2_ik0, 'g_xattn': g_xattn, 'g_ffn': g_ffn, 'L0_xattn_Wq': _L0_xattn_in['Wq'], 'L0_xattn_bq': _L0_xattn_in['bq'], 'L0_xattn_Wk': _L0_xattn_in['Wk'], 'L0_xattn_bk': _L0_xattn_in['bk'], 'L0_xattn_Wv': _L0_xattn_in['Wv'], 'L0_xattn_bv': _L0_xattn_in['bv'], 'L0_xattn_Wo': _L0_xattn_in['Wo'], 'L0_xattn_bo': _L0_xattn_in['bo'], 'L0_xattn_ln_gamma': _L0_xattn_in['ln_gamma'], 'L0_xattn_ln_beta': _L0_xattn_in['ln_beta'], 'L0_xattn_residual_scale': _L0_xattn_in['residual_scale'], 'L0_ffn_rw1': _L0_ffn_in['rw1'], 'L0_ffn_rw2': _L0_ffn_in['rw2'], 'L0_ffn_w1': _L0_ffn_in['w1'], 'L0_ffn_b1': _L0_ffn_in['b1'], 'L0_ffn_w2': _L0_ffn_in['w2'], 'L0_ffn_b2': _L0_ffn_in['b2'], 'L1_ffn_gate_weight': _L1_ffn_in['gate_weight'], 'L1_ffn_inv_mapping': _L1_ffn_in['inv_mapping'], 'L1_ffn_mask_up_W': _L1_ffn_in['mask_up_W'], 'L1_ffn_gate_W': _L1_ffn_in['gate_W'], 'L1_ffn_gate_qa': _L1_ffn_in['gate_qa'], 'L1_ffn_gate_qb': _L1_ffn_in['gate_qb'], 'L1_ffn_gate_scale': _L1_ffn_in['gate_scale'], 'L1_ffn_up_W': _L1_ffn_in['up_W'], 'L1_ffn_up_qa': _L1_ffn_in['up_qa'], 'L1_ffn_up_qb': _L1_ffn_in['up_qb'], 'L1_ffn_up_scale': _L1_ffn_in['up_scale'], 'L1_ffn_down_W': _L1_ffn_in['down_W'], 'L1_ffn_down_qa': _L1_ffn_in['down_qa'], 'L1_ffn_down_qb': _L1_ffn_in['down_qb'], 'L1_ffn_down_scale': _L1_ffn_in['down_scale'], 'L1_ffn_sh_gate_W': _L1_ffn_in['sh_gate_W'], 'L1_ffn_sh_up_W': _L1_ffn_in['sh_up_W'], 'L1_ffn_sh_down_W': _L1_ffn_in['sh_down_W']}

def reference(x, ctx_2048, mask_BxS2_ik0, g_xattn, g_ffn, L0_xattn_Wq, L0_xattn_bq, L0_xattn_Wk, L0_xattn_bk, L0_xattn_Wv, L0_xattn_bv, L0_xattn_Wo, L0_xattn_bo, L0_xattn_ln_gamma, L0_xattn_ln_beta, L0_xattn_residual_scale, L0_ffn_rw1, L0_ffn_rw2, L0_ffn_w1, L0_ffn_b1, L0_ffn_w2, L0_ffn_b2, L1_ffn_gate_weight, L1_ffn_inv_mapping, L1_ffn_mask_up_W, L1_ffn_gate_W, L1_ffn_gate_qa, L1_ffn_gate_qb, L1_ffn_gate_scale, L1_ffn_up_W, L1_ffn_up_qa, L1_ffn_up_qb, L1_ffn_up_scale, L1_ffn_down_W, L1_ffn_down_qa, L1_ffn_down_qb, L1_ffn_down_scale, L1_ffn_sh_gate_W, L1_ffn_sh_up_W, L1_ffn_sh_down_W):
    import jax
    import jax.numpy as jnp

    def _L0_xattn_ref(hidden_states, audio_tokens, attention_mask, Wq, bq, Wk, bk, Wv, bv, Wo, bo, ln_gamma, ln_beta, residual_scale):
        import jax, jax.numpy as jnp
        import numpy as np
        import math
        H = 256
        NH = 16
        HD = H // NH
        EPS_LN = 1e-05
        RES_SCALE_MAX = 0.3

        def _nan_clean(x, lim=10000.0):
            return jnp.nan_to_num(x, nan=0.0, posinf=lim, neginf=-lim)
        B, S, _ = hidden_states.shape
        T = audio_tokens.shape[1]
        hs = _nan_clean(hidden_states).astype(jnp.float32)
        at = _nan_clean(audio_tokens).astype(jnp.float32)

        def proj(x, W, b, L):
            y = x @ W.T + b
            return y.reshape(B, L, NH, HD).transpose(0, 2, 1, 3)
        q = _nan_clean(proj(hs, Wq, bq, S))
        k = _nan_clean(proj(at, Wk, bk, T))
        v = _nan_clean(proj(at, Wv, bv, T))
        scale = max(math.sqrt(HD), 1e-08)
        scores = jnp.einsum('bhsd,bhtd->bhst', q, k) / scale
        scores = jnp.clip(scores, -50.0, 50.0)
        scores = jnp.nan_to_num(scores, nan=0.0, posinf=50.0, neginf=-50.0)
        attend = (attention_mask.astype(jnp.float32) > 0.5)[:, None, None, :]
        scores = jnp.where(attend, scores, -10000.0)
        scores = jnp.clip(scores, -50.0, 50.0)
        probs = jax.nn.softmax(scores, axis=-1)
        probs = jnp.nan_to_num(probs, nan=0.0, posinf=1.0, neginf=0.0)
        probs = probs / (probs.sum(axis=-1, keepdims=True) + 1e-08)
        ctx = jnp.einsum('bhst,bhtd->bhsd', probs, v)
        ctx = ctx.transpose(0, 2, 1, 3).reshape(B, S, H)
        delta = _nan_clean(ctx @ Wo.T + bo)
        rs = jnp.clip(residual_scale, 0.0, RES_SCALE_MAX)
        delta = rs * delta
        mu = delta.mean(axis=-1, keepdims=True)
        var = jnp.mean((delta - mu) ** 2, axis=-1, keepdims=True)
        delta = (delta - mu) / jnp.sqrt(var + EPS_LN) * ln_gamma + ln_beta
        return delta

    def _L0_ffn_ref(x, rw1, rw2, w1, b1, w2, b2):
        import jax, jax.numpy as jnp
        import numpy as np
        TOP_K = 2

        def _gelu(v):
            return jax.nn.gelu(v, approximate=False)
        logits = _gelu(x @ rw1) @ rw2
        probs = jax.nn.softmax(logits, axis=-1)
        wgt, idx = jax.lax.top_k(probs, TOP_K)
        E = w1.shape[0]
        out = jnp.zeros_like(x)
        for e in range(E):
            Ye = _gelu(x @ w1[e] + b1[e]) @ w2[e] + b2[e]
            Ce = _gelu(b1[e]) @ w2[e] + b2[e]
            for k in range(TOP_K):
                mask = idx[..., k] == e
                active = jnp.any(mask).astype(x.dtype)
                term = jnp.where(mask[..., None], Ye, Ce)
                out = out + active * wgt[..., k:k + 1] * term
        return out

    def _L1_xattn_ref(q, k, v):
        import math
        import jax, jax.numpy as jnp
        import numpy as np
        HEADS = 16
        MASKED_BIAS = -10000.0

        def _mha(q, k, v):
            B, Sq, D = q.shape
            Sk = k.shape[-2]
            hd = D // HEADS
            qh = q.reshape(B, Sq, HEADS, hd).transpose(0, 2, 1, 3)
            kh = k.reshape(B, Sk, HEADS, hd).transpose(0, 2, 1, 3)
            vh = v.reshape(B, Sk, HEADS, hd).transpose(0, 2, 1, 3)
            scores = jnp.einsum('bhqd,bhkd->bhqk', qh, kh) / math.sqrt(hd)
            qi = jnp.arange(Sq)[:, None] + (Sk - Sq)
            ki = jnp.arange(Sk)[None, :]
            causal = ki <= qi
            scores = jnp.where(causal[None, None], scores, jnp.asarray(MASKED_BIAS, scores.dtype))
            attn = jax.nn.softmax(scores, axis=-1)
            out = jnp.einsum('bhqk,bhkd->bhqd', attn, vh)
            return out.transpose(0, 2, 1, 3).reshape(B, Sq, D)
        return _mha(q, k, v)

    def _L1_ffn_ref(hidden_states, gate_weight, inv_mapping, mask_up_W, gate_W, gate_qa, gate_qb, gate_scale, up_W, up_qa, up_qb, up_scale, down_W, down_qa, down_qb, down_scale, sh_gate_W, sh_up_W, sh_down_W):
        import jax, jax.numpy as jnp
        import numpy as np
        B, S, H, I, E, F, K, R, TOPK = (1, 128, 256, 176, 64, 8, 8, 8, 6)
        ISH = 2 * I

        def _fused_linear(x, W, qa, qb, scale, w):
            out = x @ W.T
            a = jnp.einsum('th,krh->tkr', x, qa)
            b = jnp.einsum('tkr,khr->tkh', a, qb)
            mix = jnp.einsum('tkh,tk->th', b, w)
            return out + scale[None, :] * mix

        def _moe_forward(hidden_states, gate_weight, inv_mapping, mask_up_W, gate_W, gate_qa, gate_qb, gate_scale, up_W, up_qa, up_qb, up_scale, down_W, down_qa, down_qb, down_scale, sh_gate_W, sh_up_W, sh_down_W):
            b, s, h = hidden_states.shape
            x = hidden_states.reshape(-1, h)
            T = x.shape[0]
            scores = jax.nn.softmax(x @ gate_weight.T, axis=-1)
            topk_w, topk_idx = jax.lax.top_k(scores, TOPK)
            w_dense = jnp.zeros((T, E), x.dtype).at[jnp.arange(T)[:, None], topk_idx].add(topk_w)
            flat = w_dense[:, inv_mapping]
            scalar = flat.sum(-1)
            soft = jax.nn.softmax(jnp.where(flat == 0, -1000000000.0, flat), axis=-1)

            def expert(muW, gW, gqa, gqb, gs, uW, uqa, uqb, us, dW, dqa, dqb, ds, w):
                xe = x + w @ muW.T
                gate = jax.nn.silu(_fused_linear(xe, gW, gqa, gqb, gs, w))
                up = _fused_linear(xe, uW, uqa, uqb, us, w)
                return _fused_linear(gate * up, dW, dqa, dqb, ds, w)
            outs = jax.vmap(expert, in_axes=(0,) * 13 + (1,))(mask_up_W, gate_W, gate_qa, gate_qb, gate_scale, up_W, up_qa, up_qb, up_scale, down_W, down_qa, down_qb, down_scale, soft)
            y = jnp.einsum('fth,tf->th', outs, scalar).reshape(b, s, h)
            sh = jax.nn.silu(hidden_states @ sh_gate_W.T) * (hidden_states @ sh_up_W.T) @ sh_down_W.T
            return y + sh
        return _moe_forward(hidden_states, gate_weight, inv_mapping, mask_up_W, gate_W, gate_qa, gate_qb, gate_scale, up_W, up_qa, up_qb, up_scale, down_W, down_qa, down_qb, down_scale, sh_gate_W, sh_up_W, sh_down_W)
    x = x + jnp.tanh(g_xattn[0]) * _L0_xattn_ref(_layernorm(x, axis=-1), ctx_2048, mask_BxS2_ik0, L0_xattn_Wq, L0_xattn_bq, L0_xattn_Wk, L0_xattn_bk, L0_xattn_Wv, L0_xattn_bv, L0_xattn_Wo, L0_xattn_bo, L0_xattn_ln_gamma, L0_xattn_ln_beta, L0_xattn_residual_scale)
    x = x + jnp.tanh(g_ffn[0]) * _L0_ffn_ref(_layernorm(x, axis=-1), L0_ffn_rw1, L0_ffn_rw2, L0_ffn_w1, L0_ffn_b1, L0_ffn_w2, L0_ffn_b2)
    x = x + jnp.tanh(g_xattn[1]) * _L1_xattn_ref(_layernorm(x, axis=-1), ctx_2048, ctx_2048)
    x = x + jnp.tanh(g_ffn[1]) * _L1_ffn_ref(_layernorm(x, axis=-1), L1_ffn_gate_weight, L1_ffn_inv_mapping, L1_ffn_mask_up_W, L1_ffn_gate_W, L1_ffn_gate_qa, L1_ffn_gate_qb, L1_ffn_gate_scale, L1_ffn_up_W, L1_ffn_up_qa, L1_ffn_up_qb, L1_ffn_up_scale, L1_ffn_down_W, L1_ffn_down_qa, L1_ffn_down_qb, L1_ffn_down_scale, L1_ffn_sh_gate_W, L1_ffn_sh_up_W, L1_ffn_sh_down_W)
    return x

_drawn_inputs = setup_inputs


def setup_inputs(seed=0):
    import zlib

    import numpy as np

    out = dict(_drawn_inputs(seed))
    spreads = {'g_ffn': (-1.0, 0.6),
     'L0_xattn_bq': (0.0, 0.306),
     'L0_xattn_bk': (0.0, 0.8),
     'L0_xattn_bv': (0.0, 0.1),
     'L0_xattn_bo': (0.0, 0.1),
     'L0_xattn_ln_gamma': (1.0, 0.2),
     'L0_xattn_ln_beta': (0.0, 0.1),
     'L1_ffn_gate_scale': (0.10000000149011612, 0.6),
     'L1_ffn_up_scale': (0.10000000149011612, 0.6),
     'L1_ffn_down_scale': (0.10000000149011612, 0.6)}
    factors = {'L0_ffn_rw1': 6.01,
     'L0_ffn_rw2': 5.882,
     'L0_ffn_w1': 5.233,
     'L0_ffn_b1': 8.0,
     'L0_ffn_w2': 4.956,
     'L0_ffn_b2': 7.134,
     'L1_ffn_gate_weight': 8.0,
     'L1_ffn_mask_up_W': 8.0,
     'L1_ffn_gate_W': 8.0,
     'L1_ffn_gate_qa': 8.0,
     'L1_ffn_gate_qb': 8.0,
     'L1_ffn_up_W': 8.0,
     'L1_ffn_up_qa': 8.0,
     'L1_ffn_up_qb': 8.0,
     'L1_ffn_down_W': 8.0,
     'L1_ffn_down_qa': 8.0,
     'L1_ffn_down_qb': 8.0,
     'L1_ffn_sh_gate_W': 4.416,
     'L1_ffn_sh_up_W': 4.354,
     'L1_ffn_sh_down_W': 4.337}
    for name, (base, spread) in spreads.items():
        noise = np.random.default_rng([zlib.crc32(name.encode()), seed]).standard_normal(out[name].shape)
        drawn = base * np.exp(spread * noise) if base else spread * noise
        out[name] = jnp.asarray(drawn.astype(out[name].dtype))
    for name, factor in factors.items():
        out[name] = (out[name] * factor).astype(out[name].dtype)
    return out
```

```python
from contextlib import ExitStack

import concourse.bass as bass
from concourse import mybir

ALU = mybir.AluOpType
ACT = mybir.ActivationFunctionType
AX = mybir.AxisListType
F32 = mybir.dt.float32
F32R = mybir.dt.float32r
I32 = mybir.dt.int32
ds = bass.ds

P = 128
B, S, D = 16, 64, 256
T = B * S
NT = T // P
KT = D // P
NH, HD = 16, 16
HT = P // HD
HP = NH // 2
VC = HD + 1
E0, I0 = 8, 1024
C0 = I0 // P
E1, G1, K1, R1 = 64, 8, 8, 8
I1 = 176
IB = I1 - P
TOP1 = 6
NS = 2
KR = K1 * R1
CH = 512
NCH = T // CH
TC = CH // P
EPS = 1e-5
BIG = 3.0e38
MASKED = -10000.0
CLIP = 50.0
QSCALE = 1.0 / float(HD) ** 0.5
RES_MAX = 0.3

WX, WL, WD, WA, WN = 0, 1024, 1408, 1920, 2176
UB = 64
NSC = 3 * P + D
MS = 3 * K1
XC, XR = 4, 2


class Steps:

    def __init__(self, engine, sem, base=0):
        self.engine, self.sem, self.base, self.n = engine, sem, base, 0

    def __call__(self, instruction):
        instruction.then_inc(self.sem, 1)
        self.n += 1

    def wait(self):
        self.engine.wait_ge(self.sem, self.base + self.n)


def apart(engine, turns):
    engine.sem_inc(turns, 1)


def each(ap, n):
    p, a = ap.shape
    return ap.unsqueeze(2).broadcast_to([p, a, n])


def rows(ap, n):
    p, a = ap.shape
    return ap.unsqueeze(1).broadcast_to([p, n, a])


def build(nc, x_in, ctxT_in, ctxTd_in, ctx2_in, mask_in, gx_in, gf_in, wq_in, wk_in, wv_in, wo_in, bqk_in,
          rows_in, rs_in, rw1_in, rw2_in, w1_in, b1_in, w2_in, b2_in, gw_in, inv_in, mu_in, wf_in, sc_in,
          ws_in, out):
    with ExitStack() as ctx:
        psum = [ctx.enter_context(nc.psum_tensor(f"bank{i}", [P, 512], F32)) for i in range(8)]

        def buf(name, shape, dt=F32, where=ctx):
            return where.enter_context(nc.sbuf_tensor(name, shape, dt))

        def sem(name):
            return ctx.enter_context(nc.semaphore(name))

        x = buf("x", [P, NT, D])
        ident = buf("ident", [P, P])
        hmask = buf("hmask", [P, HT])
        tg = buf("tg", [P, 4])
        stats = buf("stats", [P, NT, 6])
        mv = buf("mv", [P, NT, 2])
        rstd = buf("rstd", [P, NT])
        var = buf("var", [P, NT])
        mhalf = buf("mhalf", [P, NT])
        nhi = buf("nhi", [P, KT, T], F32R)
        nlo = buf("nlo", [P, KT, T], F32R)
        raw = buf("raw", [P, 2 * 2048])
        whi = buf("whi", [P, 2, 4096], F32R)
        wlo = buf("wlo", [P, 2, 4096], F32R)
        wts = buf("wts", [P, NT, 2, E0])
        b1 = buf("b1", [P, E0 * C0])
        b2 = buf("b2", [E0, D])

        raw_loaded = sem("raw_loaded")
        turns = sem("turns")

        def load_expert0(sp, e):
            sp.dma_start(raw[:, 0:2048].rearrange("p (k i) -> p k i", k=KT),
                         w1_in[e].rearrange("(k p) i -> p k i", p=P)).then_inc(raw_loaded, 16)
            sp.dma_start(raw[:, 2048:4096].rearrange("p (c d) -> p c d", c=C0),
                         w2_in[e].rearrange("(c p) d -> p c d", p=P)).then_inc(raw_loaded, 16)

        class Norm:

            def __init__(self, tag, hn):
                self.hn = hn
                self.var_ready = sem(f"{tag}_var_ready")
                self.rstd_ready = sem(f"{tag}_rstd_ready")
                self.rows_ready = sem(f"{tag}_rows_ready")
                self.turned = sem(f"{tag}_turned")

            def statistics(self, dve, v, scale2=None, src=None):
                src = x if src is None else src
                for t in range(NT):
                    v(nc.vector.bn_stats(stats[:, t, :], src[:, t, :]))
                v.wait()
                for t in range(NT):
                    v(nc.vector.bn_aggr(mv[:, t, :], stats[:, t, :]))
                v.wait()
                if scale2 is None:
                    nc.vector.tensor_scalar(var[:, :], mv[:, :, 1], EPS, None, ALU.add).then_inc(self.var_ready, 1)
                else:
                    nc.vector.tensor_scalar(var[:, :], mv[:, :, 1], scale2, EPS, ALU.mult,
                                            ALU.add).then_inc(self.var_ready, 1)

            def power(self, pool):
                pool.wait_ge(self.var_ready, 1)
                nc.gpsimd.tensor_tensor(rstd[:, :], var[:, :], mhalf[:, :], ALU.pow).then_inc(self.rstd_ready, 1)

            def normalise(self, dve, src=None):
                src = x if src is None else src
                dve.wait_ge(self.rstd_ready, 1)
                for t in range(NT):
                    nc.vector.tensor_scalar(self.hn[:, t, :], src[:, t, :], mv[:, t, 0:1], rstd[:, t:t + 1],
                                            ALU.subtract, ALU.mult).then_inc(self.rows_ready, 1)

            def transpose(self, pe):
                for t in range(NT):
                    pe.wait_ge(self.rows_ready, t + 1)
                    for k in range(KT):
                        at = k * 2 * P + (t % 2) * P
                        last = nc.tensor.transpose(psum[t // 2][:, at:at + P], self.hn[:, t, k * P:(k + 1) * P],
                                                   ident[:, :])
                    last.then_inc(self.turned, 1)

            def turned_bank(self, engine, j):
                engine.wait_ge(self.turned, 2 * j + 2)
                return psum[j][:, :].rearrange("p (k t) -> p k t", k=KT)

        with ExitStack() as s1:
            def buf1(name, shape, dt=F32):
                return buf(name, shape, dt, s1)

            kT = buf1("kT", [P, KT, T])
            qT = buf1("qT", [P, KT, T])
            oT = buf1("oT", [P, KT, T])
            wo = buf1("wo", [P, KT, D])
            wv = buf1("wv", [P, KT, D])
            lrow = buf1("lrow", [P, 4, D])
            mcol = buf1("mcol", [P, 2, B])
            rs2 = buf1("rs2", [P, 2])
            hn = buf1("hn", [P, NT, D])

            ld = {n: sem(f"ld_{n}") for n in ("x", "ctx", "wqk", "wvo", "small", "row", "mask", "f0")}
            const_ready = sem("const_ready")
            pool_step, dve_step1, act_step = sem("pool_step1"), sem("dve_step1"), sem("act_step1")
            n1 = Norm("n1", hn)
            k_done, q_done, h_ready, qk_out = sem("k_done"), sem("q_done"), sem("h_ready"), sem("qk_out")

            with ExitStack() as s1a:
                ctxT = buf("ctxT", [P, KT, T], F32, s1a)
                hT = buf("hT", [P, KT, T], F32, s1a)
                wq = buf("wq", [P, KT, D], F32, s1a)
                wk = buf("wk", [P, KT, D], F32, s1a)
                bqk = buf("bqk", [P, 2, KT], F32, s1a)
                g4 = buf("g4", [P, 4], F32, s1a)
                mraw = buf("mraw", [P, B], I32, s1a)
                mflt = buf("mflt", [P, B], F32, s1a)
                rsr = buf("rsr", [P, 1], F32, s1a)

                with nc.Block() as block:
                    @block.sync
                    def _(sp):
                        for h in range(2):
                            sp.dma_start(x[:, h * 4:h * 4 + 4, :],
                                         x_in.rearrange("(t p) d -> p t d", p=P)[:, h * 4:h * 4 + 4, :]
                                         ).then_inc(ld["x"], 16)
                        sp.dma_start(wq[:, :, :], wq_in.rearrange("(k p) d -> p k d", p=P)).then_inc(ld["wqk"], 16)
                        sp.dma_start(rsr[:, :], rs_in.partition_broadcast(P)).then_inc(ld["small"], 16)
                        sp.dma_start(g4[:, 0:2], gx_in.partition_broadcast(P)).then_inc(ld["small"], 16)
                        sp.dma_start(g4[:, 2:4], gf_in.partition_broadcast(P)).then_inc(ld["small"], 16)
                        sp.dma_start(wv[:, :, :], wv_in.rearrange("(k p) d -> p k d", p=P)).then_inc(ld["wvo"], 16)
                        sp.dma_start(wo[:, :, :], wo_in.rearrange("(k p) d -> p k d", p=P)).then_inc(ld["wvo"], 16)
                        sp.dma_start(lrow[:, :, :], rows_in.partition_broadcast(P)).then_inc(ld["row"], 16)
                        for h in range(2):
                            sp.dma_start(mraw[h * S:(h + 1) * S, :], mask_in).then_inc(ld["mask"], 16)
                        sp.dma_start(b1[:, :], b1_in).then_inc(ld["f0"], 16)
                        sp.dma_start(b2[:, :], b2_in).then_inc(ld["f0"], 16)
                        load_expert0(sp, 0)
                        sp.wait_ge(ld["wvo"], 32)
                        sp.wait_ge(ld["row"], 16)
                        sp.wait_ge(ld["f0"], 32)

                    @block.gpsimd
                    def _(pool):
                        g = Steps(pool, pool_step)
                        nc.gpsimd.memset(mhalf[:, :], -0.5)
                        g(nc.gpsimd.memset(ident[:, :], 0.0))
                        g(nc.gpsimd.memset(hmask[:, :], 1.0))
                        g.wait()
                        nc.gpsimd.affine_select(out=ident[:, :], in_=ident[:, :], compare_op=ALU.not_equal, fill=1.0,
                                                base=0, pattern=[[-1, P]], channel_multiplier=1
                                                ).then_inc(const_ready, 1)
                        g(nc.gpsimd.affine_select(out=hmask[:, :], in_=hmask[:, :], compare_op=ALU.is_ge, fill=0.0,
                                                  base=0, pattern=[[-HD, HT]], channel_multiplier=1))
                        g.wait()
                        g(nc.gpsimd.affine_select(out=hmask[:, :], in_=hmask[:, :], compare_op=ALU.is_ge, fill=0.0,
                                                  base=HD - 1, pattern=[[HD, HT]], channel_multiplier=-1))
                        n1.power(pool)

                    @block.vector
                    def _(dve):
                        v = Steps(dve, dve_step1)
                        dve.wait_ge(ld["x"], 32)
                        n1.statistics(dve, v)
                        dve.wait_ge(ld["mask"], 32)
                        v(nc.vector.tensor_copy(mflt[:, :], mraw[:, :]))
                        v.wait()
                        v(nc.vector.tensor_scalar(mcol[:, 0, :], mflt[:, :], 0.5, None, ALU.is_gt))
                        dve.wait_ge(ld["small"], 48)
                        v(nc.vector.tensor_scalar(rs2[:, 0:1], rsr[:, :], 0.0, RES_MAX, ALU.max, ALU.min))
                        v.wait()
                        v(nc.vector.tensor_scalar(mcol[:, 1, :], mcol[:, 0, :], -1.0, CLIP, ALU.add, ALU.mult))
                        v(nc.vector.tensor_tensor(rs2[:, 1:2], rs2[:, 0:1], rs2[:, 0:1], ALU.mult))
                        n1.normalise(dve)

                    @block.tensor
                    def _(pe):
                        pe.wait_ge(ld["ctx"], 32)
                        for m in range(KT):
                            for c in range(NCH):
                                for k in range(KT):
                                    last = nc.tensor.matmul(psum[4 + m * NCH + c][:, :], wk[:, k, m * P:(m + 1) * P],
                                                            ctxT[:, k, c * CH:(c + 1) * CH], start=(k == 0),
                                                            stop=(k == KT - 1))
                                last.then_inc(k_done, 1)
                        pe.wait_ge(const_ready, 1)
                        n1.transpose(pe)
                        pe.wait_ge(ld["wqk"], 32)
                        pe.wait_ge(h_ready, 4)
                        for m in range(KT):
                            for c in range(NCH):
                                for k in range(KT):
                                    last = nc.tensor.matmul(psum[m * NCH + c][:, :], wq[:, k, m * P:(m + 1) * P],
                                                            hT[:, k, c * CH:(c + 1) * CH], start=(k == 0),
                                                            stop=(k == KT - 1))
                                last.then_inc(q_done, 1)

                    @block.scalar
                    def _(act):
                        a = Steps(act, act_step)
                        act.dma_start(wk[:, :, :], wk_in.rearrange("(k p) d -> p k d", p=P)).then_inc(ld["ctx"], 16)
                        act.dma_start(ctxT[:, :, :], ctxT_in.rearrange("(k p) t -> p k t", p=P)
                                      ).then_inc(ld["ctx"], 16)
                        act.dma_start(bqk[:, :, :], bqk_in.rearrange("p (j k) -> p j k", j=2)
                                      ).then_inc(ld["wqk"], 16)
                        act.wait_ge(ld["small"], 48)
                        a(nc.scalar.activation(tg[:, :], g4[:, :], ACT.Tanh))
                        act.wait_ge(ld["wqk"], 32)
                        a(nc.scalar.mul(bqk[:, 0, :], bqk[:, 0, :], QSCALE))
                        a.wait()
                        for m in range(KT):
                            for c in range(NCH):
                                act.wait_ge(k_done, m * NCH + c + 1)
                                nc.scalar.activation(kT[:, m, c * CH:(c + 1) * CH], psum[4 + m * NCH + c][:, :],
                                                     ACT.Identity, bias=bqk[:, 1, m:m + 1])
                        for j in range(4):
                            nc.scalar.activation(hT[:, :, 2 * P * j:2 * P * (j + 1)], n1.turned_bank(act, j),
                                                 ACT.Copy).then_inc(h_ready, 1)
                        for m in range(KT):
                            for c in range(NCH):
                                act.wait_ge(q_done, m * NCH + c + 1)
                                nc.scalar.activation(qT[:, m, c * CH:(c + 1) * CH], psum[m * NCH + c][:, :],
                                                     ACT.Identity, bias=bqk[:, 0, m:m + 1], scale=QSCALE)

            with ExitStack() as s2:
                kx = buf("kx", [P, XC, KT, HT, S], F32, s2)
                cv = buf("cv", [P, XC, KT, P], F32, s2)
                vx = buf("vx", [P, XC, HP, 2 * VC], F32, s2)
                sc = buf("sc", [P, XC, CH], F32, s2)
                pt = buf("pt", [P, XC, CH], F32, s2)
                rc = buf("rc", [P, XR, NH], F32, s2)
                o = buf("o", [P, XR, NH, HD], F32, s2)
                vx_zero, kx_ready = sem("vx_zero"), sem("kx_ready")
                cv_in = [sem(f"cv_in{j}") for j in range(XC)]
                v_done, vx_ready, s_done, sc_ready = sem("v_done"), sem("vx_ready"), sem("s_done"), sem("sc_ready")
                p_ready, pv_done, rc_ready, o_ready = sem("p_ready"), sem("pv_done"), sem("rc_ready"), sem("o_ready")
                o_turned, o_copied = sem("o_turned"), sem("o_copied")
                NI = B // XC

                with nc.Block() as block:
                    @block.sync
                    def _(sp):
                        with sp.Fori(0, NI) as it:
                            for j in range(XC):
                                sp.wait_ge(v_done, XC * it + j + 1)
                                sp.dma_start(cv[:, j, :, :],
                                             ctxTd_in[ds(XC * it + j, 1)].rearrange("o (k p) c -> p (o k) c", p=P)
                                             ).then_inc(cv_in[j], 16)

                    @block.gpsimd
                    def _(pool):
                        nc.gpsimd.memset(vx[:, :, :, :], 0.0).then_inc(vx_zero, 1)
                        pool.wait_ge(vx_zero, 1)
                        for h in range(2):
                            nc.gpsimd.memset(vx[h * S:(h + 1) * S, :, :, h * VC + HD:h * VC + HD + 1], 1.0
                                             ).then_inc(vx_zero, 1)
                        pool.wait_ge(vx_zero, 3)
                        with pool.Fori(0, NI) as it:
                            for j in range(XC):
                                pool.wait_ge(s_done, XC * it + j + 1)
                                for k in range(KT):
                                    keys = kT[:, k, ds((XC * it + j) * S, S)]
                                    nc.gpsimd.tensor_tensor(kx[:, j, k, :, :], rows(keys, HT), each(hmask[:, :], S),
                                                            ALU.mult).then_inc(kx_ready, 1)

                    @block.tensor
                    def _(pe):
                        pe.sem_inc(v_done, XC)
                        pe.sem_inc(s_done, XC)
                        with pe.Fori(0, NI) as it:
                            for j in range(XC):
                                pe.wait_ge(cv_in[j], 16 * it + 16)
                                if j % 2 == 0:
                                    pe.wait_ge(o_copied, XR * it + j // 2 + 1)
                                for k in range(KT):
                                    last = nc.tensor.matmul(psum[j // 2][:, (j % 2) * D:(j % 2 + 1) * D],
                                                            cv[:, j, k, :], wv[:, k, :], start=(k == 0),
                                                            stop=(k == KT - 1))
                                last.then_inc(v_done, 1)
                            for j in range(XC):
                                pe.wait_ge(kx_ready, KT * (XC * it + j + 1))
                                pe.wait_ge(sc_ready, XC * it + j + 1)
                                for hp in range(HP):
                                    k, h = hp // (HP // KT), 2 * (hp % (HP // KT))
                                    last = nc.tensor.matmul(psum[2 + j][:, hp * S:(hp + 1) * S],
                                                            kx[:, j, k, h:h + 2, :],
                                                            qT[:, k, ds((XC * it + j) * S, S)],
                                                            start=True, stop=True)
                                last.then_inc(s_done, 1)
                            for j in range(XC):
                                s, h = j // 2, j % 2
                                if h == 0:
                                    pe.wait_ge(o_ready, XR * it + s + 1)
                                pe.wait_ge(vx_ready, 2 * (XC * it + j + 1))
                                pe.wait_ge(p_ready, XC * it + j + 1 + XC)
                                for hp in range(HP):
                                    last = nc.tensor.matmul(psum[6 + s][h * S:(h + 1) * S, hp * 2 * VC:(hp + 1) * 2 * VC],
                                                            pt[:, j, hp * S:(hp + 1) * S], vx[:, j, hp, :],
                                                            start=True, stop=True)
                                last.then_inc(pv_done, 1)
                            for s in range(XR):
                                pe.wait_ge(o_ready, XR * it + s + 1 + XR)
                                for k in range(KT):
                                    last = nc.tensor.transpose(psum[s][:, k * P:(k + 1) * P],
                                                               o[:, s, k * HT:(k + 1) * HT, :].rearrange(
                                                                   "p h d -> p (h d)"), ident[:, :])
                                last.then_inc(o_turned, 1)

                    @block.vector
                    def _(dve):
                        dve.sem_inc(sc_ready, XC)
                        dve.sem_inc(o_ready, XR)
                        dve.wait_ge(vx_zero, 3)
                        with dve.Fori(0, NI) as it:
                            for j in range(XC):
                                if j % 2 == 0:
                                    dve.wait_ge(v_done, XC * it + j + 2 + XC)
                                    dve.wait_ge(pv_done, XC * it + j + 2)
                                bank = psum[j // 2][:, (j % 2) * D:(j % 2 + 1) * D].rearrange(
                                    "p (q h d) -> p q h d", h=2, d=HD)
                                for h in range(2):
                                    r = slice(h * S, (h + 1) * S)
                                    nc.vector.tensor_tensor(
                                        vx[r, j, :, h * VC:h * VC + HD], bank[r, :, h, :],
                                        lrow[r, 0, :].rearrange("p (q h d) -> p q h d", h=2, d=HD)[:, :, h, :],
                                        ALU.add).then_inc(vx_ready, 1)
                            for j in range(XC):
                                dve.wait_ge(s_done, XC * it + j + 1 + XC)
                                dve.wait_ge(p_ready, XC * it + j + 1)
                                nc.vector.tensor_scalar(sc[:, j, :], psum[2 + j][:, :], CLIP, -CLIP, ALU.min,
                                                        ALU.max).then_inc(sc_ready, 1)
                            for s in range(XR):
                                dve.wait_ge(pv_done, XC * it + 2 * s + 2 + XC)
                                heads = psum[6 + s][:, 0:HP * 2 * VC].rearrange("p (h c) -> p h c", c=VC)
                                nc.vector.reciprocal(rc[:, s, :], heads[:, :, HD]).then_inc(rc_ready, 1)
                                dve.wait_ge(rc_ready, XR * it + s + 1)
                                dve.wait_ge(o_turned, XR * it + s + 1)
                                nc.vector.tensor_tensor(o[:, s, :, :], heads[:, :, 0:HD], each(rc[:, s, :], HD),
                                                        ALU.mult).then_inc(o_ready, 1)

                    @block.scalar
                    def _(act):
                        nc.scalar.preload_act_table(ACT.Exp)
                        act.sem_inc(p_ready, XC)
                        act.sem_inc(pv_done, XC)
                        act.sem_inc(o_turned, XR)
                        act.sem_inc(o_copied, XR)
                        with act.Fori(0, NI) as it:
                            for j in range(XC):
                                b = XC * it + j
                                act.wait_ge(sc_ready, b + 1 + XC)
                                act.wait_ge(pv_done, b + 1)
                                apart(act, turns)
                                nc.scalar.activation(pt[:, j, :], sc[:, j, :], ACT.Exp, bias=mcol[:, 1, ds(b, 1)],
                                                     scale=mcol[:, 0, ds(b, 1)]).then_inc(p_ready, 1)
                            for s in range(XR):
                                act.wait_ge(o_turned, XR * it + s + 1 + XR)
                                apart(act, turns)
                                nc.scalar.activation(oT[:, :, ds((XR * it + s) * P, P)],
                                                     psum[s][:, 0:KT * P].rearrange("p (k t) -> p k t", k=KT),
                                                     ACT.Copy).then_inc(o_copied, 1)

            with ExitStack() as s3:
                dl = buf("dl", [P, NT, D], F32, s3)
                hT = buf("hT3", [P, KT, T], F32, s3)
                rw1 = buf("rw1", [P, KT, P], F32, s3)
                rw2 = buf("rw2", [P, E0], F32, s3)
                rg = buf("rg", [P, T], F32, s3)
                lg = buf("lg", [P, NT, E0], F32, s3)
                t8 = buf("t8", [P, 4, NT, E0], F32, s3)
                oh = buf("oh", [P, 2, NT, E0], F32, s3)
                t1 = buf("t1", [P, 8, NT], F32, s3)
                rev = buf("rev", [P, E0], F32, s3)
                ones = buf("ones", [P, P], F32, s3)
                cnt = buf("cnt", [P, 2, E0], F32, s3)
                actv = buf("actv", [P, 2, E0], F32, s3)
                gm = buf("gm", [P, 2, D], F32, s3)
                ld3, const3 = sem("ld_router"), sem("const3")
                dv3, pl3, wo_done = sem("dve_step3"), sem("pool_step3"), sem("wo_done")
                nd, n2 = Norm("nd", dl), Norm("n2", hn)
                hT_ready, r1_done, rg_ready, lg_done = sem("h3_ready"), sem("r1_done"), sem("rg_ready"), sem("lg_done")
                ex_ready, lm_ready, cnt_ready, cnt_done = sem("ex_ready"), sem("lm_ready"), sem("cnt_ready"), sem("cnt_done")

                with nc.Block() as block:
                    @block.sync
                    def _(sp):
                        sp.dma_start(rw1[:, :, :], rw1_in.rearrange("(k p) m -> p k m", p=P)).then_inc(ld3, 16)
                        sp.dma_start(rw2[:, :], rw2_in).then_inc(ld3, 16)

                    @block.gpsimd
                    def _(pool):
                        nc.gpsimd.memset(ones[:, :], 1.0)
                        nc.gpsimd.iota(rev[:, :], pattern=[[-1, E0]], base=E0, channel_multiplier=0,
                                       allow_small_or_imprecise_dtypes=True).then_inc(const3, 1)
                        nd.power(pool)
                        n2.power(pool)

                    @block.tensor
                    def _(pe):
                        for t in range(NT):
                            for k in range(KT):
                                last = nc.tensor.matmul(psum[t // 2][:, (t % 2) * D:(t % 2 + 1) * D],
                                                        oT[:, k, t * P:(t + 1) * P], wo[:, k, :], start=(k == 0),
                                                        stop=(k == KT - 1))
                            last.then_inc(wo_done, 1)
                        n2.transpose(pe)
                        pe.wait_ge(ld3, 32)
                        pe.wait_ge(hT_ready, 4)
                        for c in range(NCH):
                            for k in range(KT):
                                last = nc.tensor.matmul(psum[4 + c][:, :], rw1[:, k, :], hT[:, k, c * CH:(c + 1) * CH],
                                                        start=(k == 0), stop=(k == KT - 1))
                            last.then_inc(r1_done, 1)
                        for t in range(NT):
                            if t % TC == 0:
                                pe.wait_ge(rg_ready, t // TC + 1)
                            last = nc.tensor.matmul(psum[6][:, t * E0:(t + 1) * E0], rg[:, t * P:(t + 1) * P],
                                                    rw2[:, :], start=True, stop=True)
                        last.then_inc(lg_done, 1)
                        pe.wait_ge(const3, 1)
                        pe.wait_ge(cnt_ready, 2)
                        nc.tensor.matmul(psum[7][:, 0:2 * E0], ones[:, :], cnt[:, :, :].rearrange("p k e -> p (k e)"),
                                         start=True, stop=True).then_inc(cnt_done, 1)

                    @block.vector
                    def _(dve):
                        v = Steps(dve, dv3)
                        v(nc.vector.tensor_scalar(gm[:, :, :], lrow[:, 2:4, :], tg[:, 0:1], None, ALU.mult))
                        v.wait()
                        v(nc.vector.tensor_tensor(x[:, :, :], x[:, :, :], rows(gm[:, 1, :], NT), ALU.add))
                        for j in range(NT // 2):
                            dve.wait_ge(wo_done, 2 * j + 2)
                            v(nc.vector.tensor_tensor(dl[:, 2 * j:2 * j + 2, :],
                                                      psum[j][:, :].rearrange("p (t d) -> p t d", t=2),
                                                      rows(lrow[:, 1, :], 2), ALU.add))
                        v.wait()
                        nd.statistics(dve, v, scale2=rs2[:, 1:2], src=dl)
                        dve.wait_ge(nd.rstd_ready, 1)
                        v(nc.vector.tensor_scalar(rstd[:, :], rstd[:, :], rs2[:, 0:1], None, ALU.mult))
                        v.wait()
                        nd.normalise(dve, src=dl)
                        dve.wait_ge(nd.rows_ready, NT)
                        v(nc.vector.tensor_tensor(dl[:, :, :], dl[:, :, :], rows(gm[:, 0, :], NT), ALU.mult))
                        v.wait()
                        v(nc.vector.tensor_tensor(x[:, :, :], x[:, :, :], dl[:, :, :], ALU.add))
                        v.wait()
                        n2.statistics(dve, v)
                        n2.normalise(dve)
                        for j in range(4):
                            cols = slice(2 * P * j, 2 * P * (j + 1))
                            dve.wait_ge(hT_ready, j + 1)
                            v(nc.vector.tensor_copy(nhi[:, :, cols], hT[:, :, cols]))
                            v.wait()
                            v(nc.vector.tensor_tensor(nlo[:, :, cols], hT[:, :, cols], nhi[:, :, cols].bitcast(F32),
                                                      ALU.subtract))
                        dve.wait_ge(lg_done, 1)
                        logits = psum[6][:, 0:NT * E0].rearrange("p (t e) -> p t e", e=E0)
                        v(nc.vector.tensor_reduce(t1[:, 0, :], logits, AX.X, ALU.max))
                        v.wait()
                        nc.vector.tensor_tensor(lg[:, :, :], logits, each(t1[:, 0, :], E0), ALU.subtract
                                                ).then_inc(lm_ready, 1)
                        dve.wait_ge(ex_ready, 1)
                        v(nc.vector.tensor_reduce(t1[:, 1, :], lg[:, :, :], AX.X, ALU.add))
                        v.wait()
                        v(nc.vector.reciprocal(t1[:, 2, :], t1[:, 1, :]))
                        v.wait()
                        v(nc.vector.tensor_tensor(lg[:, :, :], lg[:, :, :], each(t1[:, 2, :], E0), ALU.mult))
                        v.wait()
                        dve.wait_ge(const3, 1)
                        for k in range(2):
                            v(nc.vector.tensor_reduce(t1[:, 3 + k, :], lg[:, :, :], AX.X, ALU.max))
                            v.wait()
                            v(nc.vector.tensor_tensor(t8[:, 0, :, :], lg[:, :, :], each(t1[:, 3 + k, :], E0),
                                                      ALU.is_equal))
                            v.wait()
                            v(nc.vector.tensor_tensor(t8[:, 1, :, :], t8[:, 0, :, :], rows(rev[:, :], NT), ALU.mult))
                            v.wait()
                            v(nc.vector.tensor_reduce(t1[:, 5, :], t8[:, 1, :, :], AX.X, ALU.max))
                            v.wait()
                            v(nc.vector.tensor_tensor(oh[:, k, :, :], t8[:, 1, :, :], each(t1[:, 5, :], E0),
                                                      ALU.is_equal))
                            v.wait()
                            nc.vector.tensor_reduce(cnt[:, k, :], oh[:, k, :, :].rearrange("p t e -> p e t"), AX.X,
                                                    ALU.add).then_inc(cnt_ready, 1)
                            if k == 0:
                                v(nc.vector.scalar_tensor_tensor(lg[:, :, :], oh[:, 0, :, :], -2.0, lg[:, :, :],
                                                                 ALU.mult, ALU.add))
                                v.wait()
                        dve.wait_ge(cnt_done, 1)
                        v(nc.vector.tensor_scalar(actv[:, :, :].rearrange("p k e -> p (k e)"), psum[7][:, 0:2 * E0],
                                                  0.5, None, ALU.is_gt))
                        v(nc.vector.tensor_scalar(t1[:, 6:8, :], t1[:, 3:5, :], tg[:, 2:3], None, ALU.mult))
                        v.wait()
                        for k in range(2):
                            w = each(t1[:, 6 + k, :], E0)
                            v(nc.vector.tensor_tensor(t8[:, 2 * k, :, :], oh[:, k, :, :], w, ALU.mult))
                            v(nc.vector.tensor_tensor(t8[:, 2 * k + 1, :, :], rows(actv[:, k, :], NT), oh[:, k, :, :],
                                                      ALU.subtract))
                            v.wait()
                            v(nc.vector.tensor_tensor(t8[:, 2 * k + 1, :, :], t8[:, 2 * k + 1, :, :], w, ALU.mult))
                            v.wait()
                        v(nc.vector.tensor_tensor(wts[:, :, 0, :], t8[:, 0, :, :], t8[:, 2, :, :], ALU.add))
                        v(nc.vector.tensor_tensor(wts[:, :, 1, :], t8[:, 1, :, :], t8[:, 3, :, :], ALU.add))

                    @block.scalar
                    def _(act):
                        for j in range(4):
                            nc.scalar.activation(hT[:, :, 2 * P * j:2 * P * (j + 1)], n2.turned_bank(act, j),
                                                 ACT.Copy).then_inc(hT_ready, 1)
                        for c in range(NCH):
                            act.wait_ge(r1_done, c + 1)
                            nc.scalar.activation(rg[:, c * CH:(c + 1) * CH], psum[4 + c][:, :], ACT.Gelu
                                                 ).then_inc(rg_ready, 1)
                        act.wait_ge(lm_ready, 1)
                        nc.scalar.activation(lg[:, :, :], lg[:, :, :], ACT.Exp).then_inc(ex_ready, 1)


        ct = buf("ct", [P, KT, E0])
        with ExitStack() as s4:
            hhi = buf("hhi", [P, NCH, C0, CH], F32R, s4)
            hlo = buf("hlo", [P, NCH, C0, CH], F32R, s4)
            ga = buf("ga", [P, 4, CH], F32, s4)
            gb = buf("gb", [P, E0 * C0], F32, s4)
            gbs = buf("gbs", [P, E0 * C0, 4], F32R, s4)
            gb_ready, gbh_ready, gbs_ready = sem("gb_ready"), sem("gbh_ready"), sem("gbs_ready")
            whi_ready, wlo_ready = sem("whi_ready"), sem("wlo_ready")
            hid_done, act_ready, hi_ready, split_ready = (sem("hid_done"), sem("act_ready"), sem("hi_ready"),
                                                          sem("split_ready"))
            y_done, acc_ready, c_done, c_read = sem("y_done"), sem("acc_ready"), sem("c_done"), sem("c_read")
            NPAIR = E0 // 2
            LAST = object()

            def items(it, last):
                seq = [(2 * it + s, s, c) for s in range(2) for c in range(NCH)]
                nxt = seq[1:] + [None if last else (2 * it + 2, 0, 0)]
                return list(zip(seq, nxt))

            def over_pairs(engine, body):
                with engine.Fori(0, NPAIR - 1) as it:
                    body(it, False)
                body(NPAIR - 1, True)

            def unit(item):
                return (item[0] * NCH + item[2]) * C0

            def tile(item):
                return (item[0] * NCH + item[2]) * TC

            with nc.Block() as block:
                @block.sync
                def _(sp):
                    with sp.Fori(1, E0) as e:
                        sp.wait_ge(wlo_ready, e)
                        sp.dma_start(raw[:, 0:2048].rearrange("p (k i) -> p k i", k=KT),
                                     w1_in[ds(e, 1)].rearrange("o (k p) i -> p (o k) i", p=P)).then_inc(raw_loaded, 16)
                        sp.dma_start(raw[:, 2048:4096].rearrange("p (c d) -> p c d", c=C0),
                                     w2_in[ds(e, 1)].rearrange("o (c p) d -> p (o c) d", p=P)).then_inc(raw_loaded, 16)

                @block.gpsimd
                def _(pool):
                    def low(e, s):
                        pool.wait_ge(whi_ready, e + 1)
                        nc.gpsimd.tensor_tensor(wlo[:, s, :], raw[:, :], whi[:, s, :].bitcast(F32), ALU.subtract
                                                ).then_inc(wlo_ready, 1)
                    with pool.Fori(0, NPAIR) as it:
                        for s in range(2):
                            low(2 * it + s, s)

                @block.tensor
                def _(pe):
                    def hidden(item):
                        e, s, c = item
                        if c == 0:
                            pe.wait_ge(wlo_ready, e + 1)
                        for m in range(C0):
                            pe.wait_ge(act_ready, unit(item) + m + 1)
                            n = 0
                            for k in range(KT):
                                for w, a in ((wlo, nhi), (whi, nlo), (whi, nhi)):
                                    at = k * I0 + m * P
                                    last = nc.tensor.matmul(psum[m % 4][:, :], w[:, s, at:at + P],
                                                            a[:, k, c * CH:(c + 1) * CH], start=(n == 0),
                                                            stop=(n == 3 * KT - 1))
                                    n += 1
                            last.then_inc(hid_done, 1)

                    def output(item):
                        e, s, c = item
                        for t in range(TC):
                            pe.wait_ge(acc_ready, tile(item) + t - 2 + 1 + NT)
                            n = 0
                            for m in range(C0):
                                if t == 0:
                                    pe.wait_ge(split_ready, unit(item) + m + 1 + 4)
                                at = 2048 + m * D
                                for h, w in ((hlo, whi), (hhi, wlo), (hhi, whi)):
                                    last = nc.tensor.matmul(psum[4 + t % 2][:, 0:D], h[:, c, m, t * P:(t + 1) * P],
                                                            w[:, s, at:at + D], start=(n == 0),
                                                            stop=(n == 3 * C0 - 1))
                                    n += 1
                            last.then_inc(y_done, 1)

                    def constant(item):
                        e, s, c = item
                        pe.wait_ge(c_read, e + 1)
                        for k in range(KT):
                            n = 0
                            for m in range(C0):
                                at = 2048 + m * D + k * P
                                for w, o_ in ((whi, 0), (wlo, 2)):
                                    last = nc.tensor.matmul(psum[6][:, 2 * k:2 * k + 2], w[:, s, at:at + P],
                                                            gbs[:, ds(e * C0 + m, 1), o_:o_ + 2], start=(n == 0),
                                                            stop=(n == 2 * C0 - 1))
                                    n += 1
                        last.then_inc(c_done, 1)

                    def body(it, last):
                        for item, nxt in items(it, last):
                            if nxt is not None:
                                hidden(nxt)
                            output(item)
                            if item[2] == 0:
                                constant(item)
                    hidden((0, 0, 0))
                    pe.wait_ge(gbs_ready, 2)
                    over_pairs(pe, body)

                @block.scalar
                def _(act):
                    nc.scalar.activation(gb[:, :], b1[:, :], ACT.Gelu).then_inc(gb_ready, 1)
                    act.sem_inc(act_ready, 4)
                    act.sem_inc(y_done, 2 * TC)

                    def gelu(item):
                        e = item[0]
                        for m in range(C0):
                            act.wait_ge(hid_done, unit(item) + m + 1)
                            act.wait_ge(split_ready, unit(item) + m + 1)
                            apart(act, turns)
                            nc.scalar.activation(ga[:, m % 4, :], psum[m % 4][:, :], ACT.Gelu,
                                                 bias=b1[:, ds(e * C0 + m, 1)]).then_inc(act_ready, 1)

                    def body(it, last):
                        for item, nxt in items(it, last):
                            if nxt is not None:
                                gelu(nxt)
                    gelu((0, 0, 0))
                    over_pairs(act, body)

                @block.vector
                def _(dve):
                    dve.sem_inc(split_ready, 4)
                    dve.sem_inc(acc_ready, NT)
                    dve.sem_inc(c_read, 1)

                    def high(e, s):
                        dve.wait_ge(raw_loaded, 32 * e + 32)
                        nc.vector.tensor_copy(whi[:, s, :], raw[:, :]).then_inc(whi_ready, 1)

                    def split(item):
                        c = item[2]
                        dve.wait_ge(y_done, tile(item) + TC)
                        for m in range(C0):
                            dve.wait_ge(act_ready, unit(item) + m + 1 + 4)
                            nc.vector.tensor_copy(hhi[:, c, m, :], ga[:, m % 4, :]).then_inc(hi_ready, 1)
                            dve.wait_ge(hi_ready, unit(item) + m + 1)
                            nc.vector.tensor_tensor(hlo[:, c, m, :], ga[:, m % 4, :],
                                                    hhi[:, c, m, :].bitcast(F32), ALU.subtract
                                                    ).then_inc(split_ready, 1)

                    def accumulate(item):
                        e, s, c = item
                        for t in range(TC):
                            g = c * TC + t
                            dve.wait_ge(y_done, tile(item) + t + 1 + 2 * TC)
                            dve.wait_ge(acc_ready, tile(item) + t + 1)
                            nc.vector.scalar_tensor_tensor(x[:, g, :], psum[4 + t % 2][:, 0:D],
                                                           wts[:, g, 0, ds(e, 1)], x[:, g, :], ALU.mult, ALU.add
                                                           ).then_inc(acc_ready, 1)

                    def body(it, last):
                        for item, nxt in items(it, last):
                            if nxt is not None:
                                split(nxt)
                            accumulate(item)
                            e, s, c = item
                            if c == 0:
                                dve.wait_ge(c_done, e + 1)
                                nc.vector.tensor_reduce(ct[:, :, ds(e, 1)],
                                                        psum[6][:, 0:4].rearrange("p (k j) -> p k j", j=2), AX.X,
                                                        ALU.add).then_inc(c_read, 1)
                            if c == 1 and not last:
                                high(e + 2, s)
                    high(0, 0)
                    dve.wait_ge(gb_ready, 1)
                    nc.vector.tensor_copy(gbs[:, :, 0], gb[:, :]).then_inc(gbh_ready, 1)
                    nc.vector.tensor_copy(gbs[:, :, 2], gb[:, :])
                    nc.vector.memset(gbs[:, :, 3].bitcast(F32), 0.0).then_inc(gbs_ready, 1)
                    dve.wait_ge(gbh_ready, 1)
                    nc.vector.tensor_tensor(gbs[:, :, 1], gb[:, :], gbs[:, :, 0].bitcast(F32), ALU.subtract
                                            ).then_inc(gbs_ready, 1)
                    split((0, 0, 0))
                    high(1, 1)
                    over_pairs(dve, body)

        with ExitStack() as s5:
            hn = buf("hn5", [P, NT, D], F32, s5)
            ctxT = buf("ctxT5", [P, KT, T], F32, s5)
            qT = buf("qT5", [P, KT, T], F32, s5)
            watT = buf("watT", [E0, 2, T], F32, s5)
            cst = buf("cst", [E0, D], F32, s5)
            hi_b = buf("hi_b", [P, S], F32, s5)
            lo_b = buf("lo_b", [P, S], F32, s5)
            n5 = Norm("n5", hn)
            ld5, dv5, pl5, w_turned, w_copied = sem("ld5"), sem("dve_step5"), sem("pool_step5"), sem("w_turned"), sem("w_copied")
            c_turned, cst_ready, add_done = sem("c_turned"), sem("cst_ready"), sem("add_done")

            with nc.Block() as block:
                @block.sync
                def _(sp):
                    sp.dma_start(ctxT[:, :, :], ctxT_in.rearrange("(k p) t -> p k t", p=P)).then_inc(ld5, 16)
                    sp.wait_ge(ld5, 16)

                @block.gpsimd
                def _(pool):
                    g = Steps(pool, pl5)
                    g(nc.gpsimd.memset(hi_b[:, :], BIG))
                    g(nc.gpsimd.memset(lo_b[:, :], -BIG))
                    g.wait()
                    for h in range(2):
                        for bound in (hi_b, lo_b):
                            part = bound[h * S:(h + 1) * S, :]
                            g(nc.gpsimd.affine_select(out=part, in_=part, compare_op=ALU.is_ge, fill=MASKED, base=0,
                                                      pattern=[[-1, S]], channel_multiplier=1))
                            g.wait()
                    n5.power(pool)

                @block.tensor
                def _(pe):
                    for k in range(KT):
                        last = nc.tensor.transpose(psum[4][0:E0, k * P:(k + 1) * P], ct[:, k, :], ident[:, :])
                    last.then_inc(c_turned, 1)
                    for j in range(2):
                        for t in range(NT):
                            last = nc.tensor.transpose(psum[2 * j + t // TC][0:E0, (t % TC) * P:(t % TC + 1) * P],
                                                       wts[:, t, j, :], ident[:, :])
                            if t % TC == TC - 1:
                                last.then_inc(w_turned, 1)
                    pe.wait_ge(cst_ready, 1)
                    for t in range(NT):
                        if t % TC == 0:
                            pe.wait_ge(w_copied, 3 + t // TC)
                        for j, rhs in enumerate((b2, cst)):
                            last = nc.tensor.matmul(psum[4 + t // 2][:, (t % 2) * D:(t % 2 + 1) * D],
                                                    watT[:, j, t * P:(t + 1) * P], rhs[:, :], start=(j == 0),
                                                    stop=(j == 1))
                        last.then_inc(add_done, 1)
                    n5.transpose(pe)

                @block.vector
                def _(dve):
                    v = Steps(dve, dv5)
                    dve.wait_ge(c_turned, 1)
                    nc.vector.tensor_tensor(cst[:, :], psum[4][0:E0, 0:D], b2[:, :], ALU.add).then_inc(cst_ready, 1)
                    for j in range(NT // 2):
                        dve.wait_ge(add_done, 2 * j + 2)
                        v(nc.vector.tensor_tensor(x[:, 2 * j:2 * j + 2, :], x[:, 2 * j:2 * j + 2, :],
                                                  psum[4 + j][:, :].rearrange("p (t d) -> p t d", t=2), ALU.add))
                    v.wait()
                    n5.statistics(dve, v)
                    n5.normalise(dve)

                @block.scalar
                def _(act):
                    for j in range(4):
                        act.wait_ge(w_turned, j + 1)
                        nc.scalar.activation(watT[:, j // 2, (j % 2) * CH:(j % 2 + 1) * CH], psum[j][0:E0, :],
                                             ACT.Copy).then_inc(w_copied, 1)
                    for j in range(4):
                        nc.scalar.activation(qT[:, :, 2 * P * j:2 * P * (j + 1)], n5.turned_bank(act, j), ACT.Copy,
                                             scale=QSCALE)

            with ExitStack() as s6:
                kx = buf("kx6", [P, XC, KT, HT, S], F32, s6)
                qs = buf("qs6", [P, XC, KT, S], F32, s6)
                cv = buf("cv6", [P, XC, D], F32, s6)
                vx = buf("vx6", [P, XC, HP, 2 * VC], F32, s6)
                sm = buf("sm6", [P, XR, KT, HT, S], F32, s6)
                mx = buf("mx6", [P, XR, KT, HT], F32, s6)
                pt = buf("pt6", [P, XR, HP, P], F32, s6)
                rc = buf("rc6", [P, XR, NH], F32, s6)
                o = buf("o6", [P, XR, NH, HD], F32, s6)
                cv_in = [sem(f"cv6_in{j}") for j in range(XC)]
                vx_zero, kx_ready, qs_ready, vx_ready = sem("vx6_zero"), sem("kx6_ready"), sem("qs6_ready"), sem("vx6_ready")
                s_done, s_read, e_ready = sem("s6_done"), sem("s6_read"), sem("e6_ready")
                p_turned, pt_ready, pv_done, o_added = sem("p6_turned"), sem("pt6_ready"), sem("pv6_done"), sem("o6_added")
                step6 = sem("dve_step6")
                NI = B // XC
                STEPS = XR * (KT * 3 + 3)

                with nc.Block() as block:
                    @block.sync
                    def _(sp):
                        with sp.Fori(0, NI) as it:
                            for j in range(XC):
                                sp.wait_ge(vx_ready, 2 * (XC * it + j + 1))
                                src = ctx2_in[ds(XC * it + j, 1)].rearrange("o s d -> (o s) d")
                                for h in range(2):
                                    sp.dma_start(cv[h * S:(h + 1) * S, j, :], src).then_inc(cv_in[j], 16)

                    @block.gpsimd
                    def _(pool):
                        with pool.Fori(0, NI) as it:
                            for j in range(XC):
                                pool.wait_ge(s_done, XC * it + j + 1)
                                for k in range(KT):
                                    keys = ctxT[:, k, ds((XC * it + j) * S, S)]
                                    nc.gpsimd.tensor_tensor(kx[:, j, k, :, :], rows(keys, HT), each(hmask[:, :], S),
                                                            ALU.mult).then_inc(kx_ready, 1)

                    @block.tensor
                    def _(pe):
                        pe.sem_inc(s_done, XC)
                        pe.sem_inc(pv_done, XC)
                        with pe.Fori(0, NI) as it:
                            for j in range(XC):
                                s, h = j // 2, j % 2
                                pe.wait_ge(kx_ready, KT * (XC * it + j + 1))
                                pe.wait_ge(qs_ready, XC * it + j + 1)
                                if h == 0:
                                    pe.wait_ge(s_read, KT * (XR * it + s + 1))
                                for k in range(KT):
                                    last = nc.tensor.matmul(psum[KT * s + k][h * S:(h + 1) * S, :], qs[:, j, k, :],
                                                            kx[:, j, k, :, :].rearrange("p h s -> p (h s)"),
                                                            start=True, stop=True)
                                last.then_inc(s_done, 1)
                            for s in range(XR):
                                for k in range(KT):
                                    pe.wait_ge(e_ready, KT * (XR * it + s) + k + 1 + KT * XR)
                                    pe.wait_ge(pt_ready, KT * (XR * it + s) + k + 1)
                                    for q in range(HP // KT):
                                        last = nc.tensor.transpose(psum[4 + k][:, q * P:(q + 1) * P],
                                                                   sm[:, s, k, 2 * q:2 * q + 2, :].rearrange(
                                                                       "p h s -> p (h s)"), ident[:, :])
                                    last.then_inc(p_turned, 1)
                                pe.wait_ge(pt_ready, KT * (XR * it + s + 1) + KT)
                                pe.wait_ge(o_added, XR * it + s + 1)
                                for h in range(2):
                                    pe.wait_ge(vx_ready, 2 * (XC * it + 2 * s + h + 1) + 2 * XC)
                                    for hp in range(HP):
                                        last = nc.tensor.matmul(
                                            psum[6 + s][h * S:(h + 1) * S, hp * 2 * VC:(hp + 1) * 2 * VC],
                                            pt[:, s, hp, h * S:(h + 1) * S], vx[:, 2 * s + h, hp, :],
                                            start=True, stop=True)
                                    last.then_inc(pv_done, 1)

                    @block.vector
                    def _(dve):
                        dve.sem_inc(s_read, KT * XR)
                        dve.sem_inc(vx_ready, 2 * XC)
                        dve.sem_inc(o_added, XR)
                        v = Steps(dve, vx_zero)
                        v(nc.vector.memset(vx[:, :, :, :], 0.0))
                        v.wait()
                        for h in range(2):
                            v(nc.vector.memset(vx[h * S:(h + 1) * S, :, :, h * VC + HD:h * VC + HD + 1], 1.0))
                        v.wait()
                        with dve.Fori(0, NI) as it:
                            v = Steps(dve, step6, it * STEPS)
                            for j in range(XC):
                                dve.wait_ge(cv_in[j], 32 * it + 32)
                                dve.wait_ge(pv_done, XC * it + j + 1)
                                for h in range(2):
                                    r = slice(h * S, (h + 1) * S)
                                    nc.vector.tensor_copy(
                                        vx[r, j, :, h * VC:h * VC + HD],
                                        cv[r, j, :].rearrange("p (q h d) -> p q h d", h=2, d=HD)[:, :, h, :]
                                    ).then_inc(vx_ready, 1)
                            for s in range(XR):
                                dve.wait_ge(s_done, XC * it + 2 * s + 2 + XC)
                                dve.wait_ge(p_turned, KT * (XR * it + s + 1))
                                for k in range(KT):
                                    bank = psum[KT * s + k][:, :].rearrange("p (h s) -> p h s", s=S)
                                    part = sm[:, s, k, :, :]
                                    nc.vector.tensor_tensor(part, bank, rows(hi_b[:, :], HT), ALU.min
                                                            ).then_inc(s_read, 1)
                                    dve.wait_ge(s_read, KT * (XR * it + s) + k + 1 + KT * XR)
                                    v(nc.vector.tensor_tensor(part, part, rows(lo_b[:, :], HT), ALU.max))
                                    v.wait()
                                    v(nc.vector.tensor_reduce(mx[:, s, k, :], part, AX.X, ALU.max))
                                    v.wait()
                                    v(nc.vector.tensor_tensor(part, part, each(mx[:, s, k, :], S), ALU.subtract))
                            for s in range(XR):
                                dve.wait_ge(pv_done, XC * it + 2 * s + 2 + XC)
                                heads = psum[6 + s][:, 0:HP * 2 * VC].rearrange("p (h c) -> p h c", c=VC)
                                v(nc.vector.reciprocal(rc[:, s, :], heads[:, :, HD]))
                                v.wait()
                                v(nc.vector.tensor_scalar(rc[:, s, :], rc[:, s, :], tg[:, 1:2], None, ALU.mult))
                                v.wait()
                                v(nc.vector.tensor_tensor(o[:, s, :, :], heads[:, :, 0:HD], each(rc[:, s, :], HD),
                                                          ALU.mult))
                                v.wait()
                                rows_x = x[:, ds(XR * it + s, 1), :].rearrange("p o d -> p (o d)")
                                nc.vector.tensor_tensor(rows_x, rows_x, o[:, s, :, :].rearrange("p h d -> p (h d)"),
                                                        ALU.add).then_inc(o_added, 1)
                            assert v.n == STEPS

                    @block.scalar
                    def _(act):
                        nc.scalar.preload_act_table(ACT.Exp)
                        act.sem_inc(e_ready, KT * XR)
                        act.sem_inc(pt_ready, KT)
                        act.sem_inc(p_turned, KT * XR)
                        with act.Fori(0, NI) as it:
                            for j in range(XC):
                                act.wait_ge(s_done, XC * it + j + 1)
                                apart(act, turns)
                                nc.scalar.activation(qs[:, j, :, :], qT[:, :, ds((XC * it + j) * S, S)], ACT.Copy
                                                     ).then_inc(qs_ready, 1)
                            for s in range(XR):
                                for k in range(KT):
                                    act.wait_ge(step6, it * STEPS + 3 * (KT * s + k) + 3)
                                    part = sm[:, s, k, :, :]
                                    nc.scalar.activation(part, part, ACT.Exp).then_inc(e_ready, 1)
                            for s in range(XR):
                                for k in range(KT):
                                    act.wait_ge(p_turned, KT * (XR * it + s) + k + 1 + KT * XR)
                                    if k == 0:
                                        act.wait_ge(pv_done, XC * it + 2 * s + 2)
                                    nc.scalar.activation(pt[:, s, k * 4:k * 4 + 4, :].rearrange("p q t -> p (q t)"),
                                                         psum[4 + k][:, :], ACT.Copy).then_inc(pt_ready, 1)

        with ExitStack() as s7:
            hT = buf("hT7", [P, KT, T], F32, s7)
            wT = buf("wT", [4 * K1, G1, T], F32R, s7)
            scal = buf("scal", [P, NT, G1 + 1], F32, s7)
            selw = buf("selw", [4 * K1, P], F32R, s7)
            s1c = buf("s1c", [4 * K1, 2], F32, s7)
            w_loaded, mu_loaded = sem("w7_loaded"), sem("mu7_loaded")
            scb = buf("scb", [P, NSC], F32, s7)
            mur = buf("mur", [MS, D], F32, s7)

            def load_group(sp, g):
                sp.dma_start(raw[:, 0:WN], wf_in[ds(g, 1)].rearrange("o p c -> (o p) c")).then_inc(w_loaded, 16)
                for h in range(2):
                    sp.dma_start(scb[h * S:(h + 1) * S, :], sc_in[ds(g, 1), h, :].broadcast_to([S, NSC])
                                 ).then_inc(w_loaded, 16)
                sp.dma_start(mur[:, :], mu_in[ds(g, 1)].rearrange("o r d -> (o r) d")
                             ).then_inc(w_loaded, 16)

            with ExitStack() as s7a:
                hn = buf("hn7", [P, NT, D], F32, s7a)
                gw = buf("gw", [P, KT, E1], F32, s7a)
                invb = buf("invb", [E1, E1], I32, s7a)
                invf = buf("invf", [E1, 2, E1], F32, s7a)
                eidx = buf("eidx", [E1, 1], F32, s7a)
                sel = buf("sel", [E1, E1], F32, s7a)
                pr = buf("pr", [P, NT, E1], F32, s7a)
                big = buf("big", [P, 6, NT, E1], F32, s7a)
                top = buf("top", [P, NT, 8], F32, s7a)
                t1 = buf("t17", [P, 4, NT], F32, s7a)
                tg8 = buf("tg8", [P, 3, NT, G1], F32, s7a)
                wdT = buf("wdT", [E1, T], F32, s7a)
                wst = buf("wst", [P, NT, G1, 32], F32R, s7a)
                jk = buf("jk", [4 * K1, P], F32, s7a)
                pi = buf("pi", [4 * K1, 4], I32, s7a)
                pf = buf("pf", [4 * K1, 3], F32, s7a)
                n7 = Norm("n7", hn)
                ld7, iota_ready, pl7, dv7 = sem("ld7"), sem("iota_ready"), sem("pool_step7"), sem("dve_step7")
                hT_ready, g_done, lm_ready, ex_ready = sem("h7_ready"), sem("g7_done"), sem("lm7_ready"), sem("ex7_ready")
                wd_ready, wd_turned, wdT_ready, f_done = sem("wd_ready"), sem("wd_turned"), sem("wdT_ready"), sem("f_done")
                z_ready, ez_ready, st_ready = sem("z_ready"), sem("ez_ready"), sem("st_ready")
                st_turned, wT_ready = sem("st_turned"), sem("wT_ready")

                with nc.Block() as block:
                    @block.sync
                    def _(sp):
                        sp.dma_start(gw[:, :, :], gw_in.rearrange("(k p) e -> p k e", p=P)).then_inc(ld7, 16)
                        sp.dma_start(invb[:, :], inv_in.partition_broadcast(E1)).then_inc(ld7, 16)
                        load_group(sp, 0)

                    @block.gpsimd
                    def _(pool):
                        g = Steps(pool, pl7)
                        exact = dict(allow_small_or_imprecise_dtypes=True)
                        g(nc.gpsimd.iota(eidx[:, :], pattern=[[0, 1]], base=0, channel_multiplier=1, **exact))
                        g(nc.gpsimd.iota(pi[:, 0:1], pattern=[[0, 1]], base=0, channel_multiplier=1))
                        g(nc.gpsimd.iota(jk[:, :], pattern=[[0, 2], [1, K1], [0, R1]], base=0, channel_multiplier=0,
                                         **exact))
                        g.wait()
                        nc.gpsimd.memset(big[:, 5, :, :], 0.0).then_inc(iota_ready, 1)
                        n7.power(pool)

                    @block.tensor
                    def _(pe):
                        n7.transpose(pe)
                        pe.wait_ge(ld7, 32)
                        for t in range(NT):
                            if t % 2 == 0:
                                pe.wait_ge(hT_ready, t // 2 + 1)
                            for k in range(KT):
                                last = nc.tensor.matmul(psum[4][:, t * E1:(t + 1) * E1], hT[:, k, t * P:(t + 1) * P],
                                                        gw[:, k, :], start=(k == 0), stop=(k == KT - 1))
                        last.then_inc(g_done, 1)
                        pe.wait_ge(wd_ready, 1)
                        for t in range(NT):
                            last = nc.tensor.transpose(psum[5 + t // TC][0:E1, (t % TC) * P:(t % TC + 1) * P],
                                                       pr[:, t, :], ident[:, :])
                            if t % TC == TC - 1:
                                last.then_inc(wd_turned, 1)
                        for t in range(NT):
                            pe.wait_ge(wdT_ready, t // TC + 1)
                            last = nc.tensor.matmul(psum[7][:, t * E1:(t + 1) * E1], wdT[:, t * P:(t + 1) * P],
                                                    sel[:, :], start=True, stop=True)
                        last.then_inc(f_done, 1)
                        pe.wait_ge(st_ready, 2)
                        for q in range(G1):
                            for c in range(NCH):
                                n = q * NCH + c
                                if n >= 4:
                                    pe.wait_ge(wT_ready, n - 3)
                                for t in range(TC):
                                    last = nc.tensor.transpose(psum[n % 4][0:4 * K1, t * P:(t + 1) * P],
                                                               wst[:, c * TC + t, q, :].bitcast(F32), ident[:, :])
                                last.then_inc(st_turned, 1)

                    @block.vector
                    def _(dve):
                        v = Steps(dve, dv7)
                        n7.statistics(dve, v)
                        n7.normalise(dve)
                        dve.wait_ge(iota_ready, 1)
                        v(nc.vector.tensor_scalar(pi[:, 1:2], pi[:, 0:1], 7, None, ALU.bitwise_and))
                        v(nc.vector.tensor_scalar(pi[:, 2:3], pi[:, 0:1], 24, None, ALU.bitwise_and))
                        v.wait()
                        v(nc.vector.tensor_copy(pf[:, 0:2], pi[:, 1:3]))
                        v.wait()
                        v(nc.vector.tensor_scalar(s1c[:, 1:2], pf[:, 1:2], 8.0, None, ALU.is_equal))
                        v.wait()
                        v(nc.vector.tensor_scalar(s1c[:, 0:1], s1c[:, 1:2], -1.0, 1.0, ALU.mult, ALU.add))
                        v.wait()
                        v(nc.vector.tensor_scalar(selw[:, :], jk[:, :], pf[:, 0:1], s1c[:, 0:1], ALU.is_equal,
                                                  ALU.mult))
                        dve.wait_ge(ld7, 32)
                        v(nc.vector.tensor_copy(invf[:, 0, :], invb[:, :]))
                        v.wait()
                        v(nc.vector.tensor_scalar(invf[:, 1, :], invf[:, 0, :], 0.0, float(E1), ALU.is_lt, ALU.mult))
                        v.wait()
                        v(nc.vector.tensor_tensor(invf[:, 0, :], invf[:, 0, :], invf[:, 1, :], ALU.add))
                        v.wait()
                        v(nc.vector.tensor_scalar(sel[:, :], invf[:, 0, :], eidx[:, 0:1], None, ALU.is_equal))
                        for j in range(4):
                            cols = slice(2 * P * j, 2 * P * (j + 1))
                            dve.wait_ge(hT_ready, j + 1)
                            v(nc.vector.tensor_copy(nhi[:, :, cols], hT[:, :, cols]))
                            v.wait()
                            v(nc.vector.tensor_tensor(nlo[:, :, cols], hT[:, :, cols], nhi[:, :, cols].bitcast(F32),
                                                      ALU.subtract))
                        dve.wait_ge(g_done, 1)
                        logits = psum[4][:, :].rearrange("p (t e) -> p t e", e=E1)
                        v(nc.vector.tensor_reduce(t1[:, 0, :], logits, AX.X, ALU.max))
                        v.wait()
                        nc.vector.tensor_tensor(pr[:, :, :], logits, each(t1[:, 0, :], E1), ALU.subtract
                                                ).then_inc(lm_ready, 1)
                        dve.wait_ge(ex_ready, 1)
                        v(nc.vector.tensor_reduce(t1[:, 1, :], pr[:, :, :], AX.X, ALU.add))
                        v.wait()
                        v(nc.vector.reciprocal(t1[:, 2, :], t1[:, 1, :]))
                        v.wait()
                        v(nc.vector.tensor_tensor(pr[:, :, :], pr[:, :, :], each(t1[:, 2, :], E1), ALU.mult))
                        v.wait()
                        for t in range(NT):
                            v(nc.vector.max(top[:, t, :], pr[:, t, :]))
                        v.wait()
                        least = each(top[:, :, TOP1 - 1], E1)
                        v(nc.vector.tensor_tensor(big[:, 0, :, :], pr[:, :, :], least, ALU.is_gt))
                        v(nc.vector.tensor_tensor(big[:, 1, :, :], pr[:, :, :], least, ALU.is_equal))
                        v.wait()
                        v(nc.vector.tensor_reduce(t1[:, 3, :], big[:, 0, :, :], AX.X, ALU.add))
                        src, dst, step = 1, 2, 1
                        while step < E1:
                            v(nc.vector.tensor_tensor(big[:, dst, :, step:], big[:, src, :, step:],
                                                      big[:, src, :, :E1 - step], ALU.add))
                            v(nc.vector.tensor_copy(big[:, dst, :, :step], big[:, src, :, :step]))
                            v.wait()
                            src, dst, step = dst, (3 if dst == 2 else 2), 2 * step
                        v(nc.vector.tensor_tensor(big[:, 4, :, :], big[:, src, :, :], each(t1[:, 3, :], E1), ALU.add))
                        v.wait()
                        v(nc.vector.tensor_scalar(big[:, 4, :, :], big[:, 4, :, :], TOP1 + 0.5, None, ALU.is_lt))
                        v.wait()
                        v(nc.vector.tensor_tensor(big[:, 4, :, :], big[:, 4, :, :], big[:, 1, :, :], ALU.mult))
                        v.wait()
                        v(nc.vector.tensor_tensor(big[:, 4, :, :], big[:, 4, :, :], big[:, 0, :, :], ALU.add))
                        v.wait()
                        nc.vector.tensor_tensor(pr[:, :, :], pr[:, :, :], big[:, 4, :, :], ALU.mult
                                                ).then_inc(wd_ready, 1)
                        dve.wait_ge(f_done, 1)
                        flat, z = big[:, 0, :, :], big[:, 1, :, :]
                        f3 = flat.rearrange("p t (g k) -> p t g k", k=K1)
                        z3 = z.rearrange("p t (g k) -> p t g k", k=K1)
                        v(nc.vector.tensor_copy(flat, psum[7][:, :].rearrange("p (t e) -> p t e", e=E1)))
                        v.wait()
                        v(nc.vector.tensor_reduce(tg8[:, 0, :, :], f3, AX.X, ALU.add))
                        v(nc.vector.tensor_scalar(z, flat, 0.0, -1.0e9, ALU.is_equal, ALU.mult))
                        v.wait()
                        v(nc.vector.tensor_scalar(scal[:, :, 0:G1], tg8[:, 0, :, :], tg[:, 3:4], None, ALU.mult))
                        v(nc.vector.tensor_scalar(scal[:, :, G1], t1[:, 0, :], 0.0, tg[:, 3:4], ALU.mult, ALU.add))
                        v(nc.vector.tensor_tensor(z, z, flat, ALU.add))
                        v.wait()
                        v(nc.vector.tensor_reduce(tg8[:, 1, :, :], z3, AX.X, ALU.max))
                        v.wait()
                        zg = z.rearrange("p t (g k) -> p (t g) k", k=K1)
                        nc.vector.tensor_tensor(zg, zg, each(tg8[:, 1, :, :].rearrange("p t g -> p (t g)"), K1),
                                                ALU.subtract).then_inc(z_ready, 1)
                        dve.wait_ge(ez_ready, 1)
                        v(nc.vector.tensor_reduce(tg8[:, 2, :, :], z3, AX.X, ALU.add))
                        v.wait()
                        v(nc.vector.reciprocal(tg8[:, 0, :, :], tg8[:, 2, :, :]))
                        v.wait()
                        v(nc.vector.tensor_tensor(zg, zg, each(tg8[:, 0, :, :].rearrange("p t g -> p (t g)"), K1),
                                                  ALU.mult))
                        v.wait()
                        v(nc.vector.tensor_copy(wst[:, :, :, 0:K1], z3))
                        v(nc.vector.tensor_copy(wst[:, :, :, K1:2 * K1], z3))
                        v(nc.vector.tensor_copy(wst[:, :, :, 3 * K1:4 * K1],
                                                big[:, 5, :, :].rearrange("p t (g k) -> p t g k", k=K1)))
                        v.wait()
                        nc.vector.tensor_tensor(wst[:, :, :, 2 * K1:3 * K1], z3,
                                                wst[:, :, :, 0:K1].bitcast(F32), ALU.subtract).then_inc(st_ready, 2)
                        for n in range(1, G1 * NCH, 2):
                            dve.wait_ge(st_turned, n + 1)
                            dve.wait_ge(wT_ready, n)
                            nc.vector.tensor_copy(wT[:, n // NCH, (n % NCH) * CH:(n % NCH + 1) * CH],
                                                  psum[n % 4][0:4 * K1, :]).then_inc(wT_ready, 1)

                    @block.scalar
                    def _(act):
                        for j in range(4):
                            nc.scalar.activation(hT[:, :, 2 * P * j:2 * P * (j + 1)], n7.turned_bank(act, j),
                                                 ACT.Copy).then_inc(hT_ready, 1)
                        act.wait_ge(lm_ready, 1)
                        nc.scalar.activation(pr[:, :, :], pr[:, :, :], ACT.Exp).then_inc(ex_ready, 1)
                        for c in range(NCH):
                            act.wait_ge(wd_turned, c + 1)
                            nc.scalar.activation(wdT[:, c * CH:(c + 1) * CH], psum[5 + c][0:E1, :], ACT.Copy
                                                 ).then_inc(wdT_ready, 1)
                        act.wait_ge(z_ready, 1)
                        nc.scalar.activation(big[:, 1, :, :], big[:, 1, :, :], ACT.Exp).then_inc(ez_ready, 1)
                        for n in range(0, G1 * NCH, 2):
                            act.wait_ge(st_turned, n + 1)
                            if n:
                                act.wait_ge(wT_ready, n)
                            nc.scalar.activation(wT[:, n // NCH, (n % NCH) * CH:(n % NCH + 1) * CH],
                                                 psum[n % 4][0:4 * K1, :], ACT.Copy).then_inc(wT_ready, 1)

            with ExitStack() as s8:
                xef = buf("xef", [P, KT, CH], F32, s8)
                xhi = buf("xhi", [P, KT, CH], F32R, s8)
                xlo = buf("xlo", [P, KT, CH], F32R, s8)
                we = buf("we", [P, NCH, CH], F32, s8)
                waf = buf("waf", [P, CH], F32, s8)
                wahi = buf("wahi", [P, CH], F32R, s8)
                walo = buf("walo", [P, CH], F32R, s8)
                sg0 = buf("sg0", [P, CH], F32, s8)
                sg1 = buf("sg1", [IB, CH], F32, s8)
                h0f = buf("h0f", [P, CH], F32, s8)
                h1f = buf("h1f", [P, CH], F32, s8)
                h0hi = buf("h0hi", [P, NCH, CH], F32R, s8)
                h0lo = buf("h0lo", [P, NCH, CH], F32R, s8)
                h1hi = buf("h1hi", [P, NCH, CH], F32R, s8)
                h1lo = buf("h1lo", [P, NCH, CH], F32R, s8)
                mus = buf("mus", [MS, 2, D], F32R, s8)
                muh = buf("muh", [MS, D], F32R, s8)
                mul_ = buf("mul", [MS, 2, D], F32, s8)
                names = ("mu_done qa_done we_done dq_done t_done dn_done we_ready wahi_ready xhi_ready sg_ready "
                         "hhi_ready wadhi_ready xef_ready xlo_ready waf_ready walo_ready wadf_ready wadlo_ready "
                         "hf_ready hlo_ready acc_ready prep_ready zero_ready prep_step "
                         "turns_pool turns_pe")
                q8 = {n: sem("m_" + n) for n in names.split()}
                PREP = 8
                NG = G1 + NS

                def wait(engine, name, value):
                    if not isinstance(value, int) or value > 0:
                        engine.wait_ge(q8[name], value)

                def item_of(g, s, c):
                    return dict(g=g, s=s, c=c, n=g * NCH + c, routed=True)

                def pair(it, routed=True, before=None, after=None):
                    seq = [dict(item_of(2 * it + s, s, c), routed=routed) for s in range(2) for c in range(NCH)]
                    before = seq[0] if before == "same" else before
                    prev = [dict(item_of(2 * it - 1, 1, NCH - 1), routed=routed) if before is seq[0] else before]
                    nxt = [dict(item_of(2 * it + 2, 0, 0), routed=routed) if after == "same" else after]
                    return list(zip(prev + seq[:-1], seq, seq[1:] + nxt))

                def over_items(engine, body):
                    last_routed = item_of(G1 - 1, 1, NCH - 1)
                    first_shared = dict(item_of(G1, 0, 0), routed=False)
                    for p, i, n in pair(0, after="same"):
                        body(p, i, n)
                    with engine.Fori(1, G1 // 2 - 1) as it:
                        for p, i, n in pair(it, before="same", after="same"):
                            body(p, i, n)
                    for p, i, n in pair(G1 // 2 - 1, before="same", after=first_shared):
                        body(p, i, n)
                    for p, i, n in pair(G1 // 2, routed=False, before=last_routed):
                        body(p, i, n)
                    body(dict(item_of(NG - 1, 1, NCH - 1), routed=False), None, None)

                def cols(i):
                    return slice(i["c"] * CH, (i["c"] + 1) * CH)

                with nc.Block() as block:
                    @block.sync
                    def _(sp):
                        with sp.Fori(1, G1) as g:
                            wait(sp, "prep_ready", g)
                            load_group(sp, g)
                        for h in range(NS):
                            wait(sp, "prep_ready", G1 + h)
                            sp.dma_start(raw[:, 0:WN], ws_in[h]).then_inc(w_loaded, 16)

                    @block.gpsimd
                    def _(pool):
                        def slot_free(g):
                            wait(pool, "dn_done", (g * NCH - NCH) * TC)

                        def prepare(g, s):
                            g_ = Steps(pool, q8["prep_step"], g * PREP)
                            pool.wait_ge(w_loaded, 64 * g + 64)
                            slot_free(g)
                            g_(nc.gpsimd.tensor_tensor(raw[:, WL:WD], raw[:, WL:WD], scb[:, 0:3 * P], ALU.mult))
                            dn = raw[S:P, WD + D:WD + 2 * D]
                            g_.wait()
                            g_(nc.gpsimd.tensor_tensor(dn, dn, scb[S:P, 3 * P:NSC], ALU.mult))
                            g_.wait()
                            apart(pool, q8["turns_pool"])
                            g_(nc.gpsimd.tensor_copy(muh[:, :], mur[:, :]))
                            g_.wait()
                            g_(nc.gpsimd.tensor_tensor(mul_[:, 0, :], mur[:, :], muh[:, :].bitcast(F32),
                                                       ALU.subtract))
                            g_.wait()
                            apart(pool, q8["turns_pool"])
                            g_(nc.gpsimd.tensor_copy(whi[:, s, 0:WN], raw[:, 0:WN]))
                            g_.wait()
                            apart(pool, q8["turns_pool"])
                            g_(nc.gpsimd.tensor_scalar(mul_[:, 0, :], mul_[:, 0, :], s1c[0:MS, 1:2], None, ALU.mult))
                            g_(nc.gpsimd.tensor_scalar(mul_[:, 1, :], muh[:, :].bitcast(F32), s1c[0:MS, 0:1], None,
                                                       ALU.mult))
                            g_.wait()
                            g_(nc.gpsimd.tensor_tensor(mus[:, s, :], mul_[:, 0, :], mul_[:, 1, :], ALU.add))
                            g_.wait()
                            nc.gpsimd.tensor_tensor(wlo[:, s, 0:WN], raw[:, 0:WN], whi[:, s, 0:WN].bitcast(F32),
                                                    ALU.subtract).then_inc(q8["prep_ready"], 1)
                            wait(pool, "prep_ready", g + 1)
                            assert g_.n == PREP, g_.n

                        for s in range(2):
                            prepare(s, s)
                        with pool.Fori(1, G1 // 2) as it:
                            for s in range(2):
                                prepare(2 * it + s, s)
                        for h in range(NS):
                            pool.wait_ge(w_loaded, 64 * G1 + 16 * h + 16)
                            slot_free(G1 + h)
                            nc.gpsimd.tensor_copy(whi[:, h, 0:WN], raw[:, 0:WN]).then_inc(q8["prep_step"], 1)
                            pool.wait_ge(q8["prep_step"], G1 * PREP + h + 1)
                            nc.gpsimd.tensor_tensor(wlo[:, h, 0:WN], raw[:, 0:WN], whi[:, h, 0:WN].bitcast(F32),
                                                    ALU.subtract).then_inc(q8["prep_ready"], 1)

                    @block.tensor
                    def _(pe):
                        def split_product(bank, terms, first, last):
                            n = 0
                            for w, a in terms:
                                for i, j in ((1, 0), (0, 1), (0, 0)):
                                    done = nc.tensor.matmul(bank, w[i], a[j], start=first and n == 0,
                                                            stop=last and n == 3 * len(terms) - 1)
                                    n += 1
                            return done

                        def weights(s, a, b, r=slice(0, P)):
                            return whi[r, s, a:b], wlo[r, s, a:b]

                        def mixed(i):
                            wait(pe, "prep_ready", i["g"] + 1)
                            wait(pe, "xef_ready", KT * i["n"])
                            apart(pe, q8["turns_pe"])
                            for k in range(KT):
                                nc.tensor.matmul(psum[k][:, :], mus[:, i["s"], k * P:(k + 1) * P],
                                                 wT[0:MS, ds(i["g"], 1), cols(i)].rearrange("r o t -> r (o t)"),
                                                 start=True, stop=True).then_inc(q8["mu_done"], 1)

                        def body(prev, i, nxt):
                            if i is not None:
                                s, c, n = i["s"], i["c"], i["n"]
                                src = (xhi, xlo) if i["routed"] else (nhi[:, :, cols(i)], nlo[:, :, cols(i)])
                                wait(pe, "prep_ready", i["g"] + 1)
                            if i is not None and i["routed"]:
                                wait(pe, "xlo_ready", KT * (n + 1))
                                wait(pe, "waf_ready", n)
                                terms = [(weights(s, k * 512 + 384, k * 512 + 512), (src[0][:, k, :], src[1][:, k, :]))
                                         for k in range(KT)]
                                split_product(psum[2][:, :], terms, True, True).then_inc(q8["qa_done"], 1)
                                wait(pe, "acc_ready", TC * (n - 1))
                                apart(pe, q8["turns_pe"])
                                nc.tensor.matmul(psum[3][:, :], selw[0:MS, :],
                                                 wT[0:MS, ds(i["g"], 1), cols(i)].rearrange("r o t -> r (o t)"),
                                                 start=True, stop=True).then_inc(q8["we_done"], 1)
                            if prev is not None and prev["routed"]:
                                wait(pe, "hlo_ready", 2 * prev["n"] + 2)
                                if i is None or not i["routed"]:
                                    wait(pe, "acc_ready", TC * prev["n"])
                                sp_, cp = prev["s"], prev["c"]
                                terms = [(weights(sp_, WA, WA + P), (h0hi[:, cp, :], h0lo[:, cp, :])),
                                         (weights(sp_, WA + P, WA + 2 * P, slice(0, IB)),
                                          (h1hi[0:IB, cp, :], h1lo[0:IB, cp, :]))]
                                split_product(psum[7][:, :], terms, True, True).then_inc(q8["dq_done"], 1)
                            if i is not None:
                                wait(pe, "sg_ready", 2 * n)
                                wait(pe, "hf_ready", 2 * n)
                                for j in range(3):
                                    terms = [(weights(s, k * 512 + j * P, k * 512 + (j + 1) * P),
                                              (src[0][:, k, :], src[1][:, k, :])) for k in range(KT)]
                                    last = split_product(psum[4 + j][:, :], terms, True, not i["routed"])
                                    if not i["routed"]:
                                        last.then_inc(q8["t_done"], 1)
                            if nxt is not None and nxt["routed"]:
                                mixed(nxt)
                            if i is not None and i["routed"]:
                                wait(pe, "walo_ready", n + 1)
                                for j in range(3):
                                    at = WL + j * P
                                    split_product(psum[4 + j][:, :], [(weights(s, at, at + P),
                                                                       (wahi[:, :], walo[:, :]))],
                                                  False, True).then_inc(q8["t_done"], 1)
                            if prev is not None:
                                sp_, cp, m = prev["s"], prev["c"], prev["n"]
                                wait(pe, "hlo_ready", 2 * m + 2)
                                if prev["routed"]:
                                    wait(pe, "wadlo_ready", m + 1)
                                if i is not None and i["routed"]:
                                    wait(pe, "we_ready", n + 1)
                                r = P if prev["routed"] else IB
                                for t in range(TC):
                                    wait(pe, "acc_ready", TC * m + t - 1)
                                    tok = slice(t * P, (t + 1) * P)
                                    terms = [((h0hi[:, cp, tok], h0lo[:, cp, tok]), weights(sp_, WD, WD + D)),
                                             ((h1hi[0:r, cp, tok], h1lo[0:r, cp, tok]),
                                              weights(sp_, WD + D, WD + 2 * D, slice(0, r)))]
                                    split_product(psum[3 if t % 2 else 7][:, 0:D], terms, True, True
                                                  ).then_inc(q8["dn_done"], 1)

                        mixed(item_of(0, 0, 0))
                        over_items(pe, body)

                    @block.vector
                    def _(dve):
                        def mix(i):
                            n = i["n"]
                            for k in range(KT):
                                wait(dve, "mu_done", KT * n + k + 1)
                                wait(dve, "xhi_ready", KT * (n - 1) + k + 1)
                                nc.vector.tensor_tensor(xef[:, k, :], psum[k][:, :], hT[:, k, cols(i)], ALU.add
                                                        ).then_inc(q8["xef_ready"], 1)
                            for k in range(KT):
                                wait(dve, "xhi_ready", KT * n + k + 1)
                                nc.vector.tensor_tensor(xlo[:, k, :], xef[:, k, :], xhi[:, k, :].bitcast(F32),
                                                        ALU.subtract).then_inc(q8["xlo_ready"], 1)

                        def accumulate(prev, ts):
                            m = prev["n"]
                            col = prev["g"] if prev["routed"] else G1
                            for t in ts:
                                g = prev["c"] * TC + t
                                wait(dve, "dn_done", TC * m + t + 1)
                                wait(dve, "acc_ready", TC * (m - NCH) + t + 1)
                                nc.vector.scalar_tensor_tensor(x[:, g, :], psum[3 if t % 2 else 7][:, 0:D],
                                                               scal[:, g, ds(col, 1)], x[:, g, :], ALU.mult, ALU.add
                                                               ).then_inc(q8["acc_ready"], 1)

                        def body(prev, i, nxt):
                            if i is not None and i["routed"]:
                                n, c = i["n"], i["c"]
                                wait(dve, "qa_done", n + 1)
                                wait(dve, "we_ready", n + 1)
                                nc.vector.tensor_tensor(waf[:, :], psum[2][:, :], we[:, c, :], ALU.mult
                                                        ).then_inc(q8["waf_ready"], 1)
                                wait(dve, "wahi_ready", n + 1)
                                nc.vector.tensor_tensor(walo[:, :], waf[:, :], wahi[:, :].bitcast(F32), ALU.subtract
                                                        ).then_inc(q8["walo_ready"], 1)
                            if prev is not None and prev["routed"]:
                                m, cp = prev["n"], prev["c"]
                                wait(dve, "dq_done", m + 1)
                                nc.vector.tensor_tensor(h1f[UB:P, :], psum[7][UB:P, :], we[UB:P, cp, :], ALU.mult
                                                        ).then_inc(q8["wadf_ready"], 1)
                                wait(dve, "wadhi_ready", m + 1)
                                nc.vector.tensor_tensor(h1lo[UB:P, cp, :], h1f[UB:P, :],
                                                        h1hi[UB:P, cp, :].bitcast(F32), ALU.subtract
                                                        ).then_inc(q8["wadlo_ready"], 1)
                            if nxt is not None and nxt["routed"]:
                                mix(nxt)
                            if i is not None:
                                n, c = i["n"], i["c"]
                                wait(dve, "dn_done", TC * (n - 1))
                                wait(dve, "t_done", 3 * n + 3)
                                wait(dve, "sg_ready", 2 * n + 2)
                                wait(dve, "hlo_ready", 2 * n)
                                nc.vector.tensor_tensor(h0f[:, :], sg0[:, :], psum[5][:, :], ALU.mult
                                                        ).then_inc(q8["hf_ready"], 1)
                                nc.vector.tensor_tensor(h1f[0:IB, :], sg1[:, :], psum[6][UB:UB + IB, :], ALU.mult
                                                        ).then_inc(q8["hf_ready"], 1)
                            if prev is not None:
                                accumulate(prev, range(0, TC // 2))
                            if i is not None:
                                wait(dve, "hhi_ready", 2 * n + 1)
                                nc.vector.tensor_tensor(h0lo[:, c, :], h0f[:, :], h0hi[:, c, :].bitcast(F32),
                                                        ALU.subtract).then_inc(q8["hlo_ready"], 1)
                                wait(dve, "hhi_ready", 2 * n + 2)
                                nc.vector.tensor_tensor(h1lo[0:IB, c, :], h1f[0:IB, :],
                                                        h1hi[0:IB, c, :].bitcast(F32), ALU.subtract
                                                        ).then_inc(q8["hlo_ready"], 1)
                            if prev is not None:
                                accumulate(prev, range(TC // 2, TC))

                        for h in (h1hi, h1lo):
                            nc.vector.memset(h[32:UB, :, :].bitcast(F32), 0.0).then_inc(q8["zero_ready"], 1)
                        wait(dve, "zero_ready", 2)
                        mix(item_of(0, 0, 0))
                        over_items(dve, body)

                    @block.scalar
                    def _(act):
                        def mix(i):
                            for k in range(KT):
                                wait(act, "xef_ready", KT * i["n"] + k + 1)
                                nc.scalar.activation(xhi[:, k, :], xef[:, k, :], ACT.Copy).then_inc(q8["xhi_ready"], 1)

                        def body(prev, i, nxt):
                            if i is not None and i["routed"]:
                                n, c = i["n"], i["c"]
                                wait(act, "we_done", n + 1)
                                wait(act, "wadf_ready", n - 1)
                                nc.scalar.activation(we[:, c, :], psum[3][:, :], ACT.Copy).then_inc(q8["we_ready"], 1)
                                wait(act, "waf_ready", n + 1)
                                nc.scalar.activation(wahi[:, :], waf[:, :], ACT.Copy).then_inc(q8["wahi_ready"], 1)
                            if prev is not None and prev["routed"]:
                                m, cp = prev["n"], prev["c"]
                                wait(act, "wadf_ready", m + 1)
                                nc.scalar.activation(h1hi[UB:P, cp, :], h1f[UB:P, :], ACT.Copy
                                                     ).then_inc(q8["wadhi_ready"], 1)
                            if nxt is not None and nxt["routed"]:
                                mix(nxt)
                            if i is not None:
                                n, c = i["n"], i["c"]
                                wait(act, "t_done", 3 * n + 1)
                                wait(act, "hf_ready", 2 * n)
                                nc.scalar.activation(sg0[:, :], psum[4][:, :], ACT.Silu).then_inc(q8["sg_ready"], 1)
                                wait(act, "t_done", 3 * n + 3)
                                nc.scalar.activation(sg1[:, :], psum[6][0:IB, :], ACT.Silu).then_inc(q8["sg_ready"], 1)
                                wait(act, "hf_ready", 2 * n + 1)
                                nc.scalar.activation(h0hi[:, c, :], h0f[:, :], ACT.Copy).then_inc(q8["hhi_ready"], 1)
                                wait(act, "hf_ready", 2 * n + 2)
                                nc.scalar.activation(h1hi[0:IB, c, :], h1f[0:IB, :], ACT.Copy
                                                     ).then_inc(q8["hhi_ready"], 1)

                        act.wait_ge(q8["zero_ready"], 2)
                        nc.scalar.preload_act_table(ACT.Silu)
                        mix(item_of(0, 0, 0))
                        over_items(act, body)

        out_written = sem("out_written")
        with nc.Block() as block:
            @block.sync
            def _(sp):
                sp.dma_start(out.rearrange("(t p) d -> p t d", p=P), x[:, :, :]).then_inc(out_written, 16)
                sp.wait_ge(out_written, 16)


def layouts(i):
    import numpy as np

    def T_(a):
        return np.ascontiguousarray(np.swapaxes(a, -1, -2))

    ctx = i["ctx_2048"]
    r = {}
    r["x_in"] = i["x"].reshape(T, D)
    r["ctxT_in"] = T_(ctx.reshape(T, D))
    r["ctxTd_in"] = np.concatenate([T_(ctx), T_(ctx)], axis=2)
    r["ctx2_in"] = ctx
    r["mask_in"] = T_(i["mask_BxS2_ik0"])
    r["gx_in"] = i["g_xattn"]
    r["gf_in"] = i["g_ffn"]
    for n in "qkvo":
        r[f"w{n}_in"] = T_(i[f"L0_xattn_W{n}"])
    r["bqk_in"] = T_(np.stack([i["L0_xattn_bq"], i["L0_xattn_bk"]]).reshape(2 * KT, P))
    r["rows_in"] = np.stack([i[f"L0_xattn_{n}"] for n in ("bv", "bo", "ln_gamma", "ln_beta")])
    r["rs_in"] = np.reshape(i["L0_xattn_residual_scale"], (1,))
    r["rw1_in"] = i["L0_ffn_rw1"]
    r["rw2_in"] = i["L0_ffn_rw2"]
    r["w1_in"] = i["L0_ffn_w1"]
    r["b1_in"] = T_(i["L0_ffn_b1"].reshape(E0 * C0, P))
    r["w2_in"] = i["L0_ffn_w2"]
    r["b2_in"] = i["L0_ffn_b2"]
    r["gw_in"] = T_(i["L1_ffn_gate_weight"])
    r["inv_in"] = i["L1_ffn_inv_mapping"].reshape(E1)
    mu = T_(i["L1_ffn_mask_up_W"])
    r["mu_in"] = np.concatenate([mu, mu, mu], axis=1)

    def three(gate, up):
        gap = np.zeros(gate.shape[:-1] + (UB - IB,), gate.dtype)
        return np.concatenate([gate[..., :P], up[..., :P], gate[..., P:], gap, up[..., P:], gap], axis=-1)

    def by_slice(a):
        n, _, c = a.shape
        return a.reshape(n, KT, P, c).transpose(0, 2, 1, 3).reshape(n, P, KT * c)

    def down(a, tail):
        n = a.shape[0]
        gap = np.zeros((n, UB - IB, a.shape[2]), a.dtype)
        rest = np.concatenate([a[:, P:], gap, tail], axis=1)
        return np.concatenate([a[:, :P], rest], axis=2)

    g = {k: i["L1_ffn_" + k] for k in ("gate_W", "gate_qa", "gate_qb", "gate_scale", "up_W", "up_qa", "up_qb",
                                       "up_scale", "down_W", "down_qa", "down_qb", "down_scale")}
    inner = [T_(g[k].reshape(G1, KR, -1)) for k in ("gate_qa", "up_qa")]
    wx = by_slice(np.concatenate([three(T_(g["gate_W"]), T_(g["up_W"]))] + inner, axis=2))
    outer = [g[k].transpose(0, 1, 3, 2).reshape(G1, KR, -1) for k in ("gate_qb", "up_qb", "down_qb")]
    z = np.zeros_like(outer[0])
    wl = np.concatenate([three(outer[0], z), three(z, outer[1])], axis=1)
    wd = down(T_(g["down_W"]), outer[2])
    qa = T_(g["down_qa"].reshape(G1, KR, I1))
    qa = np.concatenate([np.zeros_like(qa), qa], axis=2)
    wa = down(qa, np.zeros((G1, KR, P), qa.dtype))
    r["wf_in"] = np.concatenate([wx, wl, wd, wa], axis=2)
    zs = np.zeros_like(g["gate_scale"])
    r["sc_in"] = np.stack([np.concatenate([three(g["gate_scale"], zs), np.zeros_like(g["down_scale"])], axis=1),
                           np.concatenate([three(zs, g["up_scale"]), g["down_scale"]], axis=1)], axis=1)
    sg, su = (i[f"L1_ffn_sh_{n}_W"].reshape(NS, I1, D) for n in ("gate", "up"))
    sd = T_(i["L1_ffn_sh_down_W"]).reshape(NS, I1, D)
    tail = np.zeros((NS, KR, D), sd.dtype)
    none = np.zeros((NS, D, P), sd.dtype)
    r["ws_in"] = np.concatenate([by_slice(np.concatenate([three(T_(sg), T_(su)), none], axis=2)),
                                 np.zeros((NS, P, 3 * P), sd.dtype), down(sd, tail),
                                 np.zeros((NS, P, 2 * P), sd.dtype)], axis=2)
    return {k: np.ascontiguousarray(v) for k, v in r.items()}


ORDER = ["x_in", "ctxT_in", "ctxTd_in", "ctx2_in", "mask_in", "gx_in", "gf_in", "wq_in", "wk_in", "wv_in", "wo_in",
         "bqk_in", "rows_in", "rs_in", "rw1_in", "rw2_in", "w1_in", "b1_in", "w2_in", "b2_in", "gw_in", "inv_in",
         "mu_in", "wf_in", "sc_in", "ws_in"]


def kernel(**inputs):
    import numpy as np
    from concourse import bacc
    from concourse.bass_utils import run_bass_kernel_spmd

    nc = bacc.Bacc("TRN2", target_bir_lowering=False, num_devices=1)
    arrays = layouts({k: np.asarray(v) for k, v in inputs.items()})
    args = [nc.dram_tensor(n, arrays[n].shape, mybir.dt.from_np(arrays[n].dtype), kind="ExternalInput").ap()
            for n in ORDER]
    out = nc.dram_tensor("out", (T, D), F32, kind="ExternalOutput").ap()
    build(nc, *args, out)
    r = run_bass_kernel_spmd(nc, [arrays], core_ids=[0])
    return r.results[0]["out"].reshape(B, S, D)
```

```python
from contextlib import ExitStack

import concourse.bass as bass
from concourse import mybir

ALU = mybir.AluOpType
ACT = mybir.ActivationFunctionType
AX = mybir.AxisListType
F32 = mybir.dt.float32
F32R = mybir.dt.float32r
I32 = mybir.dt.int32
ds = bass.ds

P = 128
B, S, D = 16, 64, 256
T = B * S
NT = T // P
KT = D // P
NH, HD = 16, 16
HT = P // HD
HP = NH // 2
VC = HD + 1
E0, I0 = 8, 1024
C0 = I0 // P
E1, G1, K1, R1 = 64, 8, 8, 8
I1 = 176
IB = I1 - P
TOP1 = 6
GB = C0 * 4 * E0
NS = 2
KR = K1 * R1
CH = 512
NCH = T // CH
TC = CH // P
EPS = 1e-5
BIG = 3.0e38
FAR = 1.0e30
MASKED = -10000.0
CLIP = 50.0
QSCALE = 1.0 / float(HD) ** 0.5
RES_MAX = 0.3

WX, WL, WD, WA, WN = 0, 1024, 1408, 1920, 2176
UB = 64
NSC = 3 * P + D
MS = 3 * K1
XC, XR = 4, 2


class Steps:

    def __init__(self, engine, sem, base=0):
        self.engine, self.sem, self.base, self.n = engine, sem, base, 0

    def __call__(self, instruction):
        instruction.then_inc(self.sem, 1)
        self.n += 1

    def wait(self):
        self.engine.wait_ge(self.sem, self.base + self.n)


def apart(engine, turns):
    engine.sem_inc(turns, 1)


def each(ap, n):
    p, a = ap.shape
    return ap.unsqueeze(2).broadcast_to([p, a, n])


def rows(ap, n):
    p, a = ap.shape
    return ap.unsqueeze(1).broadcast_to([p, n, a])


def build(nc, x_in, ctxT_in, ctxTt_in, ctx2_in, mask_in, gx_in, gf_in, wq_in, wk_in, wv_in, wo_in, bqk_in,
          rows_in, rs_in, rw1_in, rw2_in, w1_in, b1_in, w2_in, b2_in, gw_in, inv_in, mu_in, wf_in, sc_in,
          ws_in, out):
    with ExitStack() as ctx:
        psum = [ctx.enter_context(nc.psum_tensor(f"bank{i}", [P, 512], F32)) for i in range(8)]

        def buf(name, shape, dt=F32, where=ctx):
            return where.enter_context(nc.sbuf_tensor(name, shape, dt))

        def sem(name):
            return ctx.enter_context(nc.semaphore(name))

        x = buf("x", [P, NT, D])
        ident = buf("ident", [P, P])
        hmask = buf("hmask", [P, HT])
        tg = buf("tg", [P, 4])
        stats = buf("stats", [P, NT, 6])
        mv = buf("mv", [P, NT, 2])
        rstd = buf("rstd", [P, NT])
        var = buf("var", [P, NT])
        mhalf = buf("mhalf", [P, NT])
        nhi = buf("nhi", [P, KT, T], F32R)
        nlo = buf("nlo", [P, KT, T], F32R)
        raw = buf("raw", [P, 2 * 2048])
        whi = buf("whi", [P, 2, 4096], F32R)
        wlo = buf("wlo", [P, 2, 4096], F32R)
        wts = buf("wts", [P, NT, 3, E0])
        b1 = buf("b1", [P, E0 * C0])
        cst = buf("cst", [3 * E0, D])

        raw_loaded = sem("raw_loaded")
        whi_ready, wlo_ready = sem("whi_ready"), sem("wlo_ready")
        turns = sem("turns")

        def load_expert0(sp, e):
            sp.dma_start(raw[:, 0:2048].rearrange("p (k i) -> p k i", k=KT),
                         w1_in[e].rearrange("(k p) i -> p k i", p=P)).then_inc(raw_loaded, 16)
            sp.dma_start(raw[:, 2048:4096].rearrange("p (c d) -> p c d", c=C0),
                         w2_in[e].rearrange("(c p) d -> p c d", p=P)).then_inc(raw_loaded, 16)

        def expert_high(act, e):
            act.wait_ge(raw_loaded, 32 * e + 32)
            nc.scalar.activation(whi[:, e, :], raw[:, :], ACT.Copy).then_inc(whi_ready, 1)

        def expert_low(pool, e):
            pool.wait_ge(whi_ready, e + 1)
            nc.gpsimd.tensor_tensor(wlo[:, e, :], raw[:, :], whi[:, e, :].bitcast(F32), ALU.subtract
                                    ).then_inc(wlo_ready, 1)

        def over_tiles(engine, step):
            def body(it, last):
                for s in range(XR):
                    after = [(XR * it + s + d, (s + d) % XR) for d in range(3)]
                    step(*(None if last and s + d >= XR else after[d] for d in range(3)))
            with engine.Fori(0, NT // XR - 1) as it:
                body(it, False)
            body(NT // XR - 1, True)

        class Norm:

            def __init__(self, tag, hn):
                self.hn = hn
                self.var_ready = sem(f"{tag}_var_ready")
                self.rstd_ready = sem(f"{tag}_rstd_ready")
                self.rows_ready = sem(f"{tag}_rows_ready")
                self.turned = sem(f"{tag}_turned")

            def tile_statistics(self, v, tiles, src):
                for t in tiles:
                    v(nc.vector.bn_stats(stats[:, t, :], src[:, t, :]))

            def statistics(self, dve, v, scale2=None, src=None, tiles=range(NT)):
                self.tile_statistics(v, tiles, x if src is None else src)
                v.wait()
                for t in range(NT):
                    v(nc.vector.bn_aggr(mv[:, t, :], stats[:, t, :]))
                v.wait()
                if scale2 is None:
                    nc.vector.tensor_scalar(var[:, :], mv[:, :, 1], EPS, None, ALU.add).then_inc(self.var_ready, 1)
                else:
                    nc.vector.tensor_scalar(var[:, :], mv[:, :, 1], scale2, EPS, ALU.mult,
                                            ALU.add).then_inc(self.var_ready, 1)

            def power(self, pool):
                pool.wait_ge(self.var_ready, 1)
                nc.gpsimd.tensor_tensor(rstd[:, :], var[:, :], mhalf[:, :], ALU.pow).then_inc(self.rstd_ready, 1)

            def normalise(self, dve, src=None):
                src = x if src is None else src
                dve.wait_ge(self.rstd_ready, 1)
                for t in range(NT):
                    nc.vector.tensor_scalar(self.hn[:, t, :], src[:, t, :], mv[:, t, 0:1], rstd[:, t:t + 1],
                                            ALU.subtract, ALU.mult).then_inc(self.rows_ready, 1)

            def transpose(self, pe):
                for t in range(NT):
                    pe.wait_ge(self.rows_ready, t + 1)
                    for k in range(KT):
                        at = k * 2 * P + (t % 2) * P
                        last = nc.tensor.transpose(psum[t // 2][:, at:at + P], self.hn[:, t, k * P:(k + 1) * P],
                                                   ident[:, :])
                    last.then_inc(self.turned, 1)

            def turned_bank(self, engine, j):
                engine.wait_ge(self.turned, 2 * j + 2)
                return psum[j][:, :].rearrange("p (k t) -> p k t", k=KT)

        with ExitStack() as s1:
            def buf1(name, shape, dt=F32):
                return buf(name, shape, dt, s1)

            kT = buf1("kT", [P, KT, T])
            qT = buf1("qT", [P, KT, T])
            oT = buf1("oT", [P, KT, T])
            wo = buf1("wo", [P, KT, D])
            wv = buf1("wv", [P, KT, D])
            lrow = buf1("lrow", [P, 4, D])
            mcol = buf1("mcol", [P, 2, B])
            rs2 = buf1("rs2", [P, 2])
            hn = buf1("hn", [P, NT, D])

            vx = buf1("vx", [P, XC, HP, 2 * VC])
            vx_zero = sem("vx_zero")

            ld = {n: sem(f"ld_{n}") for n in ("x", "ctx", "wqk", "wvo", "small", "row", "mask", "f0")}
            const_ready, cst_zero = sem("const_ready"), sem("cst_zero")
            pool_step, dve_step1, act_step = sem("pool_step1"), sem("dve_step1"), sem("act_step1")
            n1 = Norm("n1", hn)
            k_done, q_done, h_ready, qk_out = sem("k_done"), sem("q_done"), sem("h_ready"), sem("qk_out")

            with ExitStack() as s1a:
                ctxT = buf("ctxT", [P, KT, T], F32, s1a)
                hT = buf("hT", [P, KT, T], F32, s1a)
                wq = buf("wq", [P, KT, D], F32, s1a)
                wk = buf("wk", [P, KT, D], F32, s1a)
                bqk = buf("bqk", [P, 2, KT], F32, s1a)
                g4 = buf("g4", [P, 4], F32, s1a)
                mraw = buf("mraw", [P, B], I32, s1a)
                mflt = buf("mflt", [P, B], F32, s1a)
                rsr = buf("rsr", [P, 1], F32, s1a)

                with nc.Block() as block:
                    @block.sync
                    def _(sp):
                        for h in range(2):
                            sp.dma_start(x[:, h * 4:h * 4 + 4, :],
                                         x_in.rearrange("(t p) d -> p t d", p=P)[:, h * 4:h * 4 + 4, :]
                                         ).then_inc(ld["x"], 16)
                        sp.dma_start(wq[:, :, :], wq_in.rearrange("(k p) d -> p k d", p=P)).then_inc(ld["wqk"], 16)
                        sp.dma_start(rsr[:, :], rs_in.partition_broadcast(P)).then_inc(ld["small"], 16)
                        sp.dma_start(g4[:, 0:2], gx_in.partition_broadcast(P)).then_inc(ld["small"], 16)
                        sp.dma_start(g4[:, 2:4], gf_in.partition_broadcast(P)).then_inc(ld["small"], 16)
                        sp.dma_start(wv[:, :, :], wv_in.rearrange("(k p) d -> p k d", p=P)).then_inc(ld["wvo"], 16)
                        sp.dma_start(wo[:, :, :], wo_in.rearrange("(k p) d -> p k d", p=P)).then_inc(ld["wvo"], 16)
                        sp.dma_start(lrow[:, :, :], rows_in.partition_broadcast(P)).then_inc(ld["row"], 16)
                        for h in range(2):
                            sp.dma_start(mraw[h * S:(h + 1) * S, :], mask_in).then_inc(ld["mask"], 16)
                        sp.dma_start(b1[:, :], b1_in).then_inc(ld["f0"], 16)
                        sp.wait_ge(cst_zero, 1)
                        for j in (0, 2):
                            sp.dma_start(cst[j * E0:(j + 1) * E0, :], b2_in).then_inc(ld["f0"], 16)
                        load_expert0(sp, 0)
                        sp.wait_ge(ld["wvo"], 32)
                        sp.wait_ge(ld["row"], 16)
                        sp.wait_ge(ld["f0"], 48)

                    @block.gpsimd
                    def _(pool):
                        g = Steps(pool, pool_step)
                        nc.gpsimd.memset(cst[:, :], 0.0).then_inc(cst_zero, 1)
                        pool.wait_ge(cst_zero, 1)
                        nc.gpsimd.memset(mhalf[:, :], -0.5)
                        g(nc.gpsimd.memset(ident[:, :], 0.0))
                        g(nc.gpsimd.memset(hmask[:, :], 1.0))
                        g.wait()
                        nc.gpsimd.affine_select(out=ident[:, :], in_=ident[:, :], compare_op=ALU.not_equal, fill=1.0,
                                                base=0, pattern=[[-1, P]], channel_multiplier=1
                                                ).then_inc(const_ready, 1)
                        g(nc.gpsimd.affine_select(out=hmask[:, :], in_=hmask[:, :], compare_op=ALU.is_ge, fill=0.0,
                                                  base=0, pattern=[[-HD, HT]], channel_multiplier=1))
                        g.wait()
                        g(nc.gpsimd.affine_select(out=hmask[:, :], in_=hmask[:, :], compare_op=ALU.is_ge, fill=0.0,
                                                  base=HD - 1, pattern=[[HD, HT]], channel_multiplier=-1))
                        n1.power(pool)
                        nc.gpsimd.memset(vx[:, :, :, :], 0.0).then_inc(vx_zero, 1)
                        for h in range(2):
                            pool.wait_ge(vx_zero, h + 1)
                            nc.gpsimd.memset(vx[h * S:(h + 1) * S, :, :, h * VC + HD:h * VC + HD + 1], 1.0
                                             ).then_inc(vx_zero, 1)
                        pool.wait_ge(vx_zero, 3)

                    @block.vector
                    def _(dve):
                        v = Steps(dve, dve_step1)
                        dve.wait_ge(ld["x"], 32)
                        n1.statistics(dve, v)
                        dve.wait_ge(ld["mask"], 32)
                        v(nc.vector.tensor_copy(mflt[:, :], mraw[:, :]))
                        v.wait()
                        v(nc.vector.tensor_scalar(mcol[:, 0, :], mflt[:, :], 0.5, None, ALU.is_gt))
                        dve.wait_ge(ld["small"], 48)
                        v(nc.vector.tensor_scalar(rs2[:, 0:1], rsr[:, :], 0.0, RES_MAX, ALU.max, ALU.min))
                        v.wait()
                        v(nc.vector.tensor_scalar(mcol[:, 1, :], mcol[:, 0, :], -1.0, CLIP, ALU.add, ALU.mult))
                        v(nc.vector.tensor_tensor(rs2[:, 1:2], rs2[:, 0:1], rs2[:, 0:1], ALU.mult))
                        n1.normalise(dve)

                    @block.tensor
                    def _(pe):
                        pe.wait_ge(ld["ctx"], 32)
                        for m in range(KT):
                            for c in range(NCH):
                                for k in range(KT):
                                    last = nc.tensor.matmul(psum[4 + m * NCH + c][:, :], wk[:, k, m * P:(m + 1) * P],
                                                            ctxT[:, k, c * CH:(c + 1) * CH], start=(k == 0),
                                                            stop=(k == KT - 1))
                                last.then_inc(k_done, 1)
                        pe.wait_ge(const_ready, 1)
                        n1.transpose(pe)
                        pe.wait_ge(ld["wqk"], 32)
                        pe.wait_ge(h_ready, 4)
                        for m in range(KT):
                            for c in range(NCH):
                                for k in range(KT):
                                    last = nc.tensor.matmul(psum[m * NCH + c][:, :], wq[:, k, m * P:(m + 1) * P],
                                                            hT[:, k, c * CH:(c + 1) * CH], start=(k == 0),
                                                            stop=(k == KT - 1))
                                last.then_inc(q_done, 1)

                    @block.scalar
                    def _(act):
                        a = Steps(act, act_step)
                        act.dma_start(wk[:, :, :], wk_in.rearrange("(k p) d -> p k d", p=P)).then_inc(ld["ctx"], 16)
                        act.dma_start(ctxT[:, :, :], ctxT_in.rearrange("(k p) t -> p k t", p=P)
                                      ).then_inc(ld["ctx"], 16)
                        act.dma_start(bqk[:, :, :], bqk_in.rearrange("p (j k) -> p j k", j=2)
                                      ).then_inc(ld["wqk"], 16)
                        act.wait_ge(ld["small"], 48)
                        a(nc.scalar.activation(tg[:, :], g4[:, :], ACT.Tanh))
                        act.wait_ge(ld["wqk"], 32)
                        a(nc.scalar.mul(bqk[:, 0, :], bqk[:, 0, :], QSCALE))
                        a.wait()
                        for m in range(KT):
                            for c in range(NCH):
                                act.wait_ge(k_done, m * NCH + c + 1)
                                nc.scalar.activation(kT[:, m, c * CH:(c + 1) * CH], psum[4 + m * NCH + c][:, :],
                                                     ACT.Identity, bias=bqk[:, 1, m:m + 1])
                        for j in range(4):
                            nc.scalar.activation(hT[:, :, 2 * P * j:2 * P * (j + 1)], n1.turned_bank(act, j),
                                                 ACT.Copy).then_inc(h_ready, 1)
                        for m in range(KT):
                            for c in range(NCH):
                                act.wait_ge(q_done, m * NCH + c + 1)
                                nc.scalar.activation(qT[:, m, c * CH:(c + 1) * CH], psum[m * NCH + c][:, :],
                                                     ACT.Identity, bias=bqk[:, 0, m:m + 1], scale=QSCALE)

            with ExitStack() as s2:
                kx = buf("kx", [P, XC, KT, HT, S], F32, s2)
                cv = buf("cv", [P, XR, KT, P], F32, s2)
                sc = buf("sc", [P, XC, CH], F32, s2)
                pt = buf("pt", [P, XC, CH], F32, s2)
                rc = buf("rc", [P, XR, NH], F32, s2)
                o = buf("o", [P, XR, NH, HD], F32, s2)
                kx_ready = sem("kx_ready")
                cv_in = [sem(f"cv_in{j}") for j in range(XR)]
                v_done, vx_ready, s_done, sc_ready = sem("v_done"), sem("vx_ready"), sem("s_done"), sem("sc_ready")
                p_ready, pv_done, rc_ready, o_ready = sem("p_ready"), sem("pv_done"), sem("rc_ready"), sem("o_ready")
                o_turned, o_copied = sem("o_turned"), sem("o_copied")
                NI = B // XC

                with nc.Block() as block:
                    @block.sync
                    def _(sp):
                        with sp.Fori(0, NI) as it:
                            for j in range(XR):
                                sp.wait_ge(v_done, XR * it + j + 1)
                                sp.dma_start(cv[:, j, :, :],
                                             ctxTt_in[ds(XR * it + j, 1)].rearrange("o (k p) c -> p (o k) c", p=P)
                                             ).then_inc(cv_in[j], 16)

                    @block.gpsimd
                    def _(pool):
                        with pool.Fori(0, NI) as it:
                            for j in range(XC):
                                pool.wait_ge(s_done, XC * it + j + 1)
                                for k in range(KT):
                                    keys = kT[:, k, ds((XC * it + j) * S, S)]
                                    nc.gpsimd.tensor_tensor(kx[:, j, k, :, :], rows(keys, HT), each(hmask[:, :], S),
                                                            ALU.mult).then_inc(kx_ready, 1)

                    @block.tensor
                    def _(pe):
                        pe.sem_inc(v_done, XR)
                        pe.sem_inc(s_done, XC)

                        def values(tile):
                            n, s = tile
                            pe.wait_ge(o_copied, n + 1)
                            pe.wait_ge(cv_in[s], 16 * ((n - s) // XR) + 16 if isinstance(n, int)
                                       else (n - s) * (16 // XR) + 16)
                            for k in range(KT):
                                last = nc.tensor.matmul(psum[s][:, 0:D], cv[:, s, k, :], wv[:, k, :],
                                                        start=(k == 0), stop=(k == KT - 1))
                            last.then_inc(v_done, 1)

                        def scores(tile):
                            n, s = tile
                            for h in range(2):
                                j = 2 * s + h
                                pe.wait_ge(kx_ready, KT * (2 * n + h + 1))
                                pe.wait_ge(sc_ready, 2 * n + h + 1)
                                for hp in range(HP):
                                    k, q = hp // (HP // KT), 2 * (hp % (HP // KT))
                                    last = nc.tensor.matmul(psum[2 + j][:, hp * S:(hp + 1) * S],
                                                            kx[:, j, k, q:q + 2, :],
                                                            qT[:, k, ds((2 * n + h) * S, S)],
                                                            start=True, stop=True)
                                last.then_inc(s_done, 1)

                        def product(tile):
                            n, s = tile
                            pe.wait_ge(o_ready, n + 1)
                            pe.wait_ge(vx_ready, 2 * (2 * n + 2))
                            pe.wait_ge(p_ready, 2 * n + 2 + XC)
                            for hp in range(HP):
                                for h in range(2):
                                    j = 2 * s + h
                                    last = nc.tensor.matmul(psum[6 + s][h * S:(h + 1) * S, hp * 2 * VC:(hp + 1) * 2 * VC],
                                                            pt[:, j, hp * S:(hp + 1) * S], vx[:, j, hp, :],
                                                            start=True, stop=True)
                                    if hp == HP - 1:
                                        last.then_inc(pv_done, 1)

                        def turn(tile):
                            n, s = tile
                            pe.wait_ge(o_ready, n + 1 + XR)
                            for k in range(KT):
                                last = nc.tensor.transpose(psum[s][:, k * P:(k + 1) * P],
                                                           o[:, s, k * HT:(k + 1) * HT, :].rearrange(
                                                               "p h d -> p (h d)"), ident[:, :])
                            last.then_inc(o_turned, 1)

                        def step(tile, nxt, _):
                            if nxt is not None:
                                scores(nxt)
                            product(tile)
                            if nxt is not None:
                                values(nxt)
                            pe.wait_ge(vx_ready, 4 * (tile[0] + 1))
                            turn(tile)

                        scores((0, 0))
                        values((0, 0))
                        over_tiles(pe, step)

                    @block.vector
                    def _(dve):
                        dve.sem_inc(sc_ready, XC)
                        dve.sem_inc(o_ready, XR)

                        def values(tile):
                            n, s = tile
                            dve.wait_ge(v_done, n + 1 + XR)
                            dve.wait_ge(pv_done, 2 * n + 2)
                            for g in range(2):
                                bank = psum[s][:, 0:D].rearrange("p (q h d) -> p q h d", h=2, d=HD)
                                own = slice(g * S, (g + 1) * S)
                                for h in range(2):
                                    nc.vector.tensor_tensor(
                                        vx[h * S:(h + 1) * S, 2 * s + g, :, h * VC:h * VC + HD], bank[own, :, h, :],
                                        lrow[own, 0, :].rearrange("p (q h d) -> p q h d", h=2, d=HD)[:, :, h, :],
                                        ALU.add).then_inc(vx_ready, 1)

                        def clip(tile):
                            n, s = tile
                            for h in range(2):
                                dve.wait_ge(s_done, 2 * n + h + 1 + XC)
                                dve.wait_ge(p_ready, 2 * n + h + 1)
                                nc.vector.tensor_scalar(sc[:, 2 * s + h, :], psum[2 + 2 * s + h][:, :], CLIP, -CLIP,
                                                        ALU.min, ALU.max).then_inc(sc_ready, 1)

                        def divide(tile):
                            n, s = tile
                            dve.wait_ge(pv_done, 2 * n + 2 + XC)
                            dve.wait_ge(o_ready, n + 1)
                            heads = psum[6 + s][:, 0:HP * 2 * VC].rearrange("p (h c) -> p h c", c=VC)
                            nc.vector.reciprocal(rc[:, s, :], heads[:, :, HD]).then_inc(rc_ready, 1)
                            dve.wait_ge(rc_ready, n + 1)
                            dve.wait_ge(o_turned, n + 1)
                            nc.vector.tensor_tensor(o[:, s, :, :], heads[:, :, 0:HD], each(rc[:, s, :], HD),
                                                    ALU.mult).then_inc(o_ready, 1)

                        def step(tile, nxt, _):
                            if nxt is not None:
                                clip(nxt)
                            divide(tile)
                            if nxt is not None:
                                values(nxt)

                        clip((0, 0))
                        values((0, 0))
                        over_tiles(dve, step)

                    @block.scalar
                    def _(act):
                        nc.scalar.preload_act_table(ACT.Exp)
                        act.sem_inc(p_ready, XC)
                        act.sem_inc(pv_done, XC)
                        act.sem_inc(o_turned, XR)
                        act.sem_inc(o_copied, XR)

                        def exponentials(tile):
                            n, s = tile
                            for h in range(2):
                                b, j = 2 * n + h, 2 * s + h
                                act.wait_ge(sc_ready, b + 1 + XC)
                                act.wait_ge(pv_done, b + 1)
                                apart(act, turns)
                                nc.scalar.activation(pt[:, j, :], sc[:, j, :], ACT.Exp, bias=mcol[:, 1, ds(b, 1)],
                                                     scale=mcol[:, 0, ds(b, 1)]).then_inc(p_ready, 1)

                        def step(tile, nxt, _):
                            if nxt is not None:
                                exponentials(nxt)
                            n, s = tile
                            act.wait_ge(o_turned, n + 1 + XR)
                            apart(act, turns)
                            nc.scalar.activation(oT[:, :, ds(n * P, P)],
                                                 psum[s][:, 0:KT * P].rearrange("p (k t) -> p k t", k=KT),
                                                 ACT.Copy).then_inc(o_copied, 1)

                        exponentials((0, 0))
                        over_tiles(act, step)

            with ExitStack() as s3:
                dl = buf("dl", [P, NT, D], F32, s3)
                hT = buf("hT3", [P, KT, T], F32, s3)
                rw1 = buf("rw1", [P, KT, P], F32, s3)
                rw2 = buf("rw2", [P, E0], F32, s3)
                rg = buf("rg", [P, T], F32, s3)
                lg = buf("lg", [P, NT, E0], F32, s3)
                t8 = buf("t8", [P, 4, NT, E0], F32, s3)
                oh = buf("oh", [P, 2, NT, E0], F32, s3)
                t1 = buf("t1", [P, 8, NT], F32, s3)
                rev = buf("rev", [P, E0], F32, s3)
                ones = buf("ones", [P, P], F32, s3)
                cnt = buf("cnt", [P, 2, E0], F32, s3)
                actv = buf("actv", [P, 2, E0], F32, s3)
                gm = buf("gm", [P, 2, D], F32, s3)
                ld3, const3 = sem("ld_router"), sem("const3")
                dv3, nhi_ready, wo_done = sem("dve_step3"), sem("nhi3_ready"), sem("wo_done")
                nd, n2 = Norm("nd", dl), Norm("n2", hn)
                hT_ready, r1_done, rg_ready, lg_done = sem("h3_ready"), sem("r1_done"), sem("rg_ready"), sem("lg_done")
                ex_ready, lm_ready, cnt_ready, cnt_done = sem("ex_ready"), sem("lm_ready"), sem("cnt_ready"), sem("cnt_done")

                with nc.Block() as block:
                    @block.sync
                    def _(sp):
                        sp.dma_start(rw1[:, :, :], rw1_in.rearrange("(k p) m -> p k m", p=P)).then_inc(ld3, 16)
                        sp.dma_start(rw2[:, :], rw2_in).then_inc(ld3, 16)
                        sp.wait_ge(wlo_ready, 1)
                        load_expert0(sp, 1)

                    @block.gpsimd
                    def _(pool):
                        nc.gpsimd.memset(ones[:, :], 1.0)
                        nc.gpsimd.iota(rev[:, :], pattern=[[-1, E0]], base=E0, channel_multiplier=0,
                                       allow_small_or_imprecise_dtypes=True).then_inc(const3, 1)
                        expert_low(pool, 0)
                        nd.power(pool)
                        n2.power(pool)

                    @block.tensor
                    def _(pe):
                        for t in range(NT):
                            for k in range(KT):
                                last = nc.tensor.matmul(psum[t // 2][:, (t % 2) * D:(t % 2 + 1) * D],
                                                        oT[:, k, t * P:(t + 1) * P], wo[:, k, :], start=(k == 0),
                                                        stop=(k == KT - 1))
                            last.then_inc(wo_done, 1)
                        n2.transpose(pe)
                        pe.wait_ge(ld3, 32)
                        pe.wait_ge(hT_ready, 4)
                        for c in range(NCH):
                            for k in range(KT):
                                last = nc.tensor.matmul(psum[4 + c][:, :], rw1[:, k, :], hT[:, k, c * CH:(c + 1) * CH],
                                                        start=(k == 0), stop=(k == KT - 1))
                            last.then_inc(r1_done, 1)
                        for t in range(NT):
                            if t % TC == 0:
                                pe.wait_ge(rg_ready, t // TC + 1)
                            last = nc.tensor.matmul(psum[6][:, t * E0:(t + 1) * E0], rg[:, t * P:(t + 1) * P],
                                                    rw2[:, :], start=True, stop=True)
                        last.then_inc(lg_done, 1)
                        pe.wait_ge(const3, 1)
                        pe.wait_ge(cnt_ready, 2)
                        nc.tensor.matmul(psum[7][:, 0:2 * E0], ones[:, :], cnt[:, :, :].rearrange("p k e -> p (k e)"),
                                         start=True, stop=True).then_inc(cnt_done, 1)

                    @block.vector
                    def _(dve):
                        v = Steps(dve, dv3)
                        v(nc.vector.tensor_scalar(gm[:, :, :], lrow[:, 2:4, :], tg[:, 0:1], None, ALU.mult))
                        v.wait()
                        v(nc.vector.tensor_tensor(x[:, :, :], x[:, :, :], rows(gm[:, 1, :], NT), ALU.add))
                        for j in range(NT // 2):
                            dve.wait_ge(wo_done, 2 * j + 2)
                            v(nc.vector.tensor_tensor(dl[:, 2 * j:2 * j + 2, :],
                                                      psum[j][:, :].rearrange("p (t d) -> p t d", t=2),
                                                      rows(lrow[:, 1, :], 2), ALU.add))
                            v.wait()
                            nd.tile_statistics(v, range(2 * j, 2 * j + 2), dl)
                        nd.statistics(dve, v, scale2=rs2[:, 1:2], src=None, tiles=())
                        for t in range(NT):
                            v(nc.vector.scalar_tensor_tensor(dl[:, t, :], dl[:, t, :], mv[:, t, 0:1], gm[:, 0, :],
                                                             ALU.subtract, ALU.mult))
                        dve.wait_ge(nd.rstd_ready, 1)
                        v(nc.vector.tensor_scalar(rstd[:, :], rstd[:, :], rs2[:, 0:1], None, ALU.mult))
                        v.wait()
                        for t in range(NT):
                            v(nc.vector.scalar_tensor_tensor(x[:, t, :], dl[:, t, :], rstd[:, t:t + 1], x[:, t, :],
                                                             ALU.mult, ALU.add))
                        v.wait()
                        n2.statistics(dve, v)
                        n2.normalise(dve)
                        for j in range(4):
                            cols = slice(2 * P * j, 2 * P * (j + 1))
                            dve.wait_ge(nhi_ready, j + 1)
                            v(nc.vector.tensor_tensor(nlo[:, :, cols], hT[:, :, cols], nhi[:, :, cols].bitcast(F32),
                                                      ALU.subtract))
                        dve.wait_ge(lg_done, 1)
                        logits = psum[6][:, 0:NT * E0].rearrange("p (t e) -> p t e", e=E0)
                        v(nc.vector.tensor_reduce(t1[:, 0, :], logits, AX.X, ALU.max))
                        v.wait()
                        nc.vector.tensor_tensor(lg[:, :, :], logits, each(t1[:, 0, :], E0), ALU.subtract
                                                ).then_inc(lm_ready, 1)
                        dve.wait_ge(ex_ready, 1)
                        v(nc.vector.tensor_reduce(t1[:, 1, :], lg[:, :, :], AX.X, ALU.add))
                        v.wait()
                        v(nc.vector.reciprocal(t1[:, 2, :], t1[:, 1, :]))
                        v.wait()
                        v(nc.vector.tensor_tensor(lg[:, :, :], lg[:, :, :], each(t1[:, 2, :], E0), ALU.mult))
                        v.wait()
                        dve.wait_ge(const3, 1)
                        for k in range(2):
                            v(nc.vector.tensor_reduce(t1[:, 3 + k, :], lg[:, :, :], AX.X, ALU.max))
                            v.wait()
                            v(nc.vector.tensor_tensor(t8[:, 0, :, :], lg[:, :, :], each(t1[:, 3 + k, :], E0),
                                                      ALU.is_equal))
                            v.wait()
                            v(nc.vector.tensor_tensor(t8[:, 1, :, :], t8[:, 0, :, :], rows(rev[:, :], NT), ALU.mult))
                            v.wait()
                            v(nc.vector.tensor_reduce(t1[:, 5, :], t8[:, 1, :, :], AX.X, ALU.max))
                            v.wait()
                            v(nc.vector.tensor_tensor(oh[:, k, :, :], t8[:, 1, :, :], each(t1[:, 5, :], E0),
                                                      ALU.is_equal))
                            v.wait()
                            nc.vector.tensor_reduce(cnt[:, k, :], oh[:, k, :, :].rearrange("p t e -> p e t"), AX.X,
                                                    ALU.add).then_inc(cnt_ready, 1)
                            if k == 0:
                                v(nc.vector.scalar_tensor_tensor(lg[:, :, :], oh[:, 0, :, :], -2.0, lg[:, :, :],
                                                                 ALU.mult, ALU.add))
                                v.wait()
                        dve.wait_ge(cnt_done, 1)
                        v(nc.vector.tensor_scalar(actv[:, :, :].rearrange("p k e -> p (k e)"), psum[7][:, 0:2 * E0],
                                                  0.5, None, ALU.is_gt))
                        v(nc.vector.tensor_scalar(t1[:, 6:8, :], t1[:, 3:5, :], tg[:, 2:3], None, ALU.mult))
                        v.wait()
                        for k in range(2):
                            w = each(t1[:, 6 + k, :], E0)
                            v(nc.vector.tensor_tensor(t8[:, 2 * k, :, :], oh[:, k, :, :], w, ALU.mult))
                            v(nc.vector.tensor_tensor(t8[:, 2 * k + 1, :, :], rows(actv[:, k, :], NT), oh[:, k, :, :],
                                                      ALU.subtract))
                            v.wait()
                            v(nc.vector.tensor_tensor(t8[:, 2 * k + 1, :, :], t8[:, 2 * k + 1, :, :], w, ALU.mult))
                            v.wait()
                        v(nc.vector.tensor_tensor(wts[:, :, 2, :], t8[:, 0, :, :], t8[:, 2, :, :], ALU.add))
                        for j in range(2):
                            v(nc.vector.tensor_tensor(wts[:, :, j, :], t8[:, 1, :, :], t8[:, 3, :, :], ALU.add))

                    @block.scalar
                    def _(act):
                        expert_high(act, 0)
                        for j in range(4):
                            cols = slice(2 * P * j, 2 * P * (j + 1))
                            nc.scalar.activation(hT[:, :, cols], n2.turned_bank(act, j), ACT.Copy
                                                 ).then_inc(hT_ready, 1)
                        for j in range(4):
                            cols = slice(2 * P * j, 2 * P * (j + 1))
                            act.wait_ge(hT_ready, j + 1)
                            nc.scalar.activation(nhi[:, :, cols], hT[:, :, cols], ACT.Copy).then_inc(nhi_ready, 1)
                        for c in range(NCH):
                            act.wait_ge(r1_done, c + 1)
                            nc.scalar.activation(rg[:, c * CH:(c + 1) * CH], psum[4 + c][:, :], ACT.Gelu
                                                 ).then_inc(rg_ready, 1)
                        act.wait_ge(lm_ready, 1)
                        nc.scalar.activation(lg[:, :, :], lg[:, :, :], ACT.Exp).then_inc(ex_ready, 1)

        with ExitStack() as s4:
            hhi = buf("hhi", [P, NCH, C0, CH], F32R, s4)
            hlo = buf("hlo", [P, NCH, C0, CH], F32R, s4)
            ga = buf("ga", [P, 4, CH], F32, s4)
            gb = buf("gb", [P, E0 * C0], F32, s4)
            gbp = buf("gbp", [P, E0 * (GB + 1)], F32R, s4)
            gbe = buf("gbe", [P, 2, GB], F32R, s4)
            gbd = gbp[:, :].rearrange("p (e q) -> p e q", q=GB + 1)[:, :, 0:GB].rearrange(
                "p e (m j) -> p e m j", j=4 * E0)
            gb_ready, gbz_ready, gbh_ready, gbs_ready = sem("gb_ready"), sem("gbz_ready"), sem("gbh_ready"), sem("gbs_ready")
            gbe_ready = sem("gbe_ready")
            hid_done, act_ready, hi_ready, split_ready = (sem("hid_done"), sem("act_ready"), sem("hi_ready"),
                                                          sem("split_ready"))
            y_done, acc_ready, c_done, c_read = sem("y_done"), sem("acc_ready"), sem("c_done"), sem("c_read")
            NPAIR = E0 // 2
            LAST = object()

            def items(it, last):
                seq = [(2 * it + s, s, c) for s in range(2) for c in range(NCH)]
                nxt = seq[1:] + [None if last else (2 * it + 2, 0, 0)]
                return list(zip(seq, nxt))

            def over_pairs(engine, body):
                with engine.Fori(0, NPAIR - 1) as it:
                    body(it, False)
                body(NPAIR - 1, True)

            def unit(item):
                return (item[0] * NCH + item[2]) * C0

            def tile(item):
                return (item[0] * NCH + item[2]) * TC

            with nc.Block() as block:
                @block.sync
                def _(sp):
                    with sp.Fori(2, E0) as e:
                        sp.wait_ge(wlo_ready, e)
                        sp.dma_start(raw[:, 0:2048].rearrange("p (k i) -> p k i", k=KT),
                                     w1_in[ds(e, 1)].rearrange("o (k p) i -> p (o k) i", p=P)).then_inc(raw_loaded, 16)
                        sp.dma_start(raw[:, 2048:4096].rearrange("p (c d) -> p c d", c=C0),
                                     w2_in[ds(e, 1)].rearrange("o (c p) d -> p (o c) d", p=P)).then_inc(raw_loaded, 16)

                @block.gpsimd
                def _(pool):
                    def low(e, s):
                        pool.wait_ge(whi_ready, e + 1)
                        nc.gpsimd.tensor_tensor(wlo[:, s, :], raw[:, :], whi[:, s, :].bitcast(F32), ALU.subtract
                                                ).then_inc(wlo_ready, 1)
                    nc.gpsimd.memset(gbp[:, :].bitcast(F32), 0.0).then_inc(gbz_ready, 1)
                    expert_low(pool, 1)
                    with pool.Fori(1, NPAIR) as it:
                        for s in range(2):
                            low(2 * it + s, s)

                @block.tensor
                def _(pe):
                    def hidden(item):
                        e, s, c = item
                        if c == 0:
                            pe.wait_ge(wlo_ready, e + 1)
                        for m in range(C0):
                            pe.wait_ge(act_ready, unit(item) + m + 1)
                            n = 0
                            for k in range(KT):
                                for w, a in ((wlo, nhi), (whi, nlo), (whi, nhi)):
                                    at = k * I0 + m * P
                                    last = nc.tensor.matmul(psum[m % 4][:, :], w[:, s, at:at + P],
                                                            a[:, k, c * CH:(c + 1) * CH], start=(n == 0),
                                                            stop=(n == 3 * KT - 1))
                                    n += 1
                            last.then_inc(hid_done, 1)

                    def output(item):
                        e, s, c = item
                        for t in range(TC):
                            pe.wait_ge(acc_ready, tile(item) + t - 2 + 1 + NT)
                            n = 0
                            for m in range(C0):
                                if t == 0:
                                    pe.wait_ge(split_ready, unit(item) + m + 1 + 4)
                                at = 2048 + m * D
                                for h, w in ((hlo, whi), (hhi, wlo), (hhi, whi)):
                                    last = nc.tensor.matmul(psum[4 + t % 2][:, 0:D], h[:, c, m, t * P:(t + 1) * P],
                                                            w[:, s, at:at + D], start=(n == 0),
                                                            stop=(n == 3 * C0 - 1))
                                    n += 1
                            last.then_inc(y_done, 1)

                    def constant(item):
                        e, s, c = item
                        pe.wait_ge(c_read, e + 1)
                        pe.wait_ge(gbe_ready, e + 1)
                        n = 0
                        for m in range(C0):
                            at = 2048 + m * D
                            for w, o_ in ((whi, 0), (wlo, 2 * E0)):
                                o_ += m * 4 * E0
                                last = nc.tensor.matmul(psum[6][0:2 * E0, 0:D], gbe[:, s, o_:o_ + 2 * E0],
                                                        w[:, s, at:at + D], start=(n == 0), stop=(n == 2 * C0 - 1))
                                n += 1
                        last.then_inc(c_done, 1)

                    def body(it, last):
                        for item, nxt in items(it, last):
                            if nxt is not None:
                                hidden(nxt)
                            output(item)
                            if item[2] == 0:
                                constant(item)
                    hidden((0, 0, 0))
                    over_pairs(pe, body)

                @block.scalar
                def _(act):
                    nc.scalar.activation(gb[:, :], b1[:, :], ACT.Gelu).then_inc(gb_ready, 1)
                    expert_high(act, 1)
                    act.sem_inc(act_ready, 4)
                    act.sem_inc(y_done, 2 * TC)

                    def gelu(item):
                        e, s, c = item
                        act.wait_ge(y_done, tile(item) + TC)
                        for m in range(C0):
                            act.wait_ge(hid_done, unit(item) + m + 1)
                            act.wait_ge(split_ready, unit(item) + m + 1)
                            apart(act, turns)
                            nc.scalar.activation(ga[:, m % 4, :], psum[m % 4][:, :], ACT.Gelu,
                                                 bias=b1[:, ds(e * C0 + m, 1)]).then_inc(act_ready, 1)
                            act.wait_ge(act_ready, unit(item) + m + 1 + 4)
                            nc.scalar.activation(hhi[:, c, m, :], ga[:, m % 4, :], ACT.Copy).then_inc(hi_ready, 1)

                    def body(it, last):
                        for item, nxt in items(it, last):
                            e, s, c = item
                            if c == 0:
                                nc.scalar.activation(gbe[:, s, :], gbp[:, ds(e * GB, GB)].bitcast(F32), ACT.Copy
                                                     ).then_inc(gbe_ready, 1)
                            if nxt is not None:
                                gelu(nxt)
                    gelu((0, 0, 0))
                    act.wait_ge(gbs_ready, 3)
                    over_pairs(act, body)

                @block.vector
                def _(dve):
                    dve.sem_inc(split_ready, 4)
                    dve.sem_inc(acc_ready, NT)
                    dve.sem_inc(c_read, 1)

                    def high(e, s):
                        dve.wait_ge(raw_loaded, 32 * e + 32)
                        nc.vector.tensor_copy(whi[:, s, :], raw[:, :]).then_inc(whi_ready, 1)

                    def split(item):
                        c = item[2]
                        dve.wait_ge(y_done, tile(item) + TC)
                        for m in range(C0):
                            dve.wait_ge(hi_ready, unit(item) + m + 1)
                            nc.vector.tensor_tensor(hlo[:, c, m, :], ga[:, m % 4, :],
                                                    hhi[:, c, m, :].bitcast(F32), ALU.subtract
                                                    ).then_inc(split_ready, 1)

                    def accumulate(item):
                        e, s, c = item
                        for t in range(TC):
                            g = c * TC + t
                            dve.wait_ge(y_done, tile(item) + t + 1 + 2 * TC)
                            dve.wait_ge(acc_ready, tile(item) + t + 1)
                            nc.vector.scalar_tensor_tensor(x[:, g, :], psum[4 + t % 2][:, 0:D],
                                                           wts[:, g, 2, ds(e, 1)], x[:, g, :], ALU.mult, ALU.add
                                                           ).then_inc(acc_ready, 1)

                    def body(it, last):
                        for item, nxt in items(it, last):
                            if nxt is not None:
                                split(nxt)
                            accumulate(item)
                            e, s, c = item
                            if c == 0:
                                dve.wait_ge(c_done, e + 1)
                                dve.wait_ge(c_read, e + 1)
                                nc.vector.tensor_tensor(cst[0:2 * E0, :], cst[0:2 * E0, :], psum[6][0:2 * E0, 0:D],
                                                        ALU.add).then_inc(c_read, 1)
                            if c == 1 and not last:
                                high(e + 2, s)
                    dve.wait_ge(gb_ready, 1)
                    dve.wait_ge(gbz_ready, 1)
                    g3 = gb[:, :].rearrange("p (e m) -> p e m", m=C0)
                    nc.vector.tensor_copy(gbd[:, :, :, 0], g3).then_inc(gbh_ready, 1)
                    nc.vector.tensor_copy(gbd[:, :, :, 2 * E0], g3).then_inc(gbs_ready, 1)
                    dve.wait_ge(gbh_ready, 1)
                    nc.vector.tensor_tensor(gbd[:, :, :, E0], g3, gbd[:, :, :, 0].bitcast(F32), ALU.subtract
                                            ).then_inc(gbs_ready, 2)
                    split((0, 0, 0))
                    over_pairs(dve, body)

        with ExitStack() as s5:
            hn = buf("hn5", [P, NT, D], F32, s5)
            ctxT = buf("ctxT5", [P, KT, T], F32, s5)
            qT = buf("qT5", [P, KT, T], F32, s5)
            watT = buf("watT", [3 * E0, T], F32, s5)
            far = buf("far", [P, S], F32, s5)
            lo_b = buf("lo_b", [P, S], F32, s5)
            far_r = buf("far_r", [P, S], F32R, s5)
            ident_r = buf("ident_r", [P, P], F32R, s5)
            BOUND_STEPS = 6
            n5 = Norm("n5", hn)
            ld5, dv5, pl5, w_turned, w_copied = sem("ld5"), sem("dve_step5"), sem("pool_step5"), sem("w_turned"), sem("w_copied")
            add_done = sem("add_done")

            with nc.Block() as block:
                @block.sync
                def _(sp):
                    sp.dma_start(ctxT[:, :, :], ctxT_in.rearrange("(k p) t -> p k t", p=P)).then_inc(ld5, 16)
                    sp.wait_ge(ld5, 16)

                @block.gpsimd
                def _(pool):
                    g = Steps(pool, pl5)
                    g(nc.gpsimd.memset(far[:, :], 0.0))
                    g(nc.gpsimd.memset(lo_b[:, :], -BIG))
                    g.wait()
                    for h in range(2):
                        for bound, fill in ((far, -FAR), (lo_b, MASKED)):
                            part = bound[h * S:(h + 1) * S, :]
                            g(nc.gpsimd.affine_select(out=part, in_=part, compare_op=ALU.is_ge, fill=fill, base=0,
                                                      pattern=[[-1, S]], channel_multiplier=1))
                            g.wait()
                    assert g.n == BOUND_STEPS
                    n5.power(pool)

                @block.tensor
                def _(pe):
                    for t in range(NT):
                        last = nc.tensor.transpose(psum[t // TC][0:3 * E0, (t % TC) * P:(t % TC + 1) * P],
                                                   wts[:, t, :, :].rearrange("p j e -> p (j e)"), ident[:, :])
                        if t % TC == TC - 1:
                            last.then_inc(w_turned, 1)
                    for t in range(NT):
                        if t % TC == 0:
                            pe.wait_ge(w_copied, 1 + t // TC)
                        last = nc.tensor.matmul(psum[4 + t // 2][:, (t % 2) * D:(t % 2 + 1) * D],
                                                watT[:, t * P:(t + 1) * P], cst[:, :], start=True, stop=True)
                        last.then_inc(add_done, 1)
                    n5.transpose(pe)

                @block.vector
                def _(dve):
                    v = Steps(dve, dv5)
                    for j in range(NT // 2):
                        dve.wait_ge(add_done, 2 * j + 2)
                        v(nc.vector.tensor_tensor(x[:, 2 * j:2 * j + 2, :], x[:, 2 * j:2 * j + 2, :],
                                                  psum[4 + j][:, :].rearrange("p (t d) -> p t d", t=2), ALU.add))
                    v.wait()
                    n5.statistics(dve, v)
                    n5.normalise(dve)

                @block.scalar
                def _(act):
                    nc.scalar.activation(ident_r[:, :], ident[:, :], ACT.Copy)
                    for c in range(NCH):
                        act.wait_ge(w_turned, c + 1)
                        nc.scalar.activation(watT[:, c * CH:(c + 1) * CH], psum[c][0:3 * E0, :], ACT.Copy
                                             ).then_inc(w_copied, 1)
                    act.wait_ge(pl5, BOUND_STEPS)
                    nc.scalar.activation(far_r[:, :], far[:, :], ACT.Copy)
                    for j in range(4):
                        nc.scalar.activation(qT[:, :, 2 * P * j:2 * P * (j + 1)], n5.turned_bank(act, j), ACT.Copy,
                                             scale=QSCALE)

            with ExitStack() as s6:
                kx = buf("kx6", [P, XC, KT, HT, S], F32, s6)
                qs = buf("qs6", [P, XC, KT, S], F32, s6)
                cv = buf("cv6", [P, XC, D], F32, s6)
                vx = buf("vx6", [P, XC, HP, 2 * VC], F32, s6)
                sm = buf("sm6", [P, XR, KT, HT, S], F32, s6)
                mx = buf("mx6", [P, XR, KT, HT], F32, s6)
                pt = buf("pt6", [P, XR, HP, P], F32, s6)
                rc = buf("rc6", [P, XR, NH], F32, s6)
                o = buf("o6", [P, XR, NH, HD], F32, s6)
                cv_in = [sem(f"cv6_in{j}") for j in range(XC)]
                vx_zero, kx_ready, qs_ready, vx_ready = sem("vx6_zero"), sem("kx6_ready"), sem("qs6_ready"), sem("vx6_ready")
                s_done, s_read, e_ready = sem("s6_done"), sem("s6_read"), sem("e6_ready")
                p_turned, pt_ready, pv_done, o_added = sem("p6_turned"), sem("pt6_ready"), sem("pv6_done"), sem("o6_added")
                mask_step, out_step = sem("mask_step"), sem("out_step")
                NI = B // XC

                with nc.Block() as block:
                    @block.sync
                    def _(sp):
                        with sp.Fori(0, NI) as it:
                            for j in range(XC):
                                sp.wait_ge(vx_ready, 2 * (XC * it + j + 1))
                                src = ctx2_in[ds(XC * it + j, 1)].rearrange("o s d -> (o s) d")
                                for h in range(2):
                                    sp.dma_start(cv[h * S:(h + 1) * S, j, :], src).then_inc(cv_in[j], 16)

                    @block.gpsimd
                    def _(pool):
                        with pool.Fori(0, NI) as it:
                            for j in range(XC):
                                pool.wait_ge(s_done, XC * it + j + 1)
                                for k in range(KT):
                                    keys = ctxT[:, k, ds((XC * it + j) * S, S)]
                                    nc.gpsimd.tensor_tensor(kx[:, j, k, :, :], rows(keys, HT), each(hmask[:, :], S),
                                                            ALU.mult).then_inc(kx_ready, 1)

                    @block.tensor
                    def _(pe):
                        pe.sem_inc(s_done, XC)
                        pe.sem_inc(pv_done, XC)

                        def scores(tile):
                            n, s = tile
                            pe.wait_ge(s_read, KT * (n + 1))
                            for k in range(KT):
                                nc.tensor.matmul(psum[KT * s + k][:, :], ident_r[:, :], rows(far_r[:, :], HT),
                                                 start=True, stop=False)
                            pe.wait_ge(kx_ready, KT * (2 * n + 2))
                            pe.wait_ge(qs_ready, 2 * n + 2)
                            for k in range(KT):
                                for h in range(2):
                                    last = nc.tensor.matmul(psum[KT * s + k][h * S:(h + 1) * S, :],
                                                            qs[:, 2 * s + h, k, :],
                                                            kx[:, 2 * s + h, k, :, :].rearrange("p h s -> p (h s)"),
                                                            start=False, stop=True)
                                    if k == KT - 1:
                                        last.then_inc(s_done, 1)

                        def step(tile, nxt, _):
                            if nxt is not None:
                                scores(nxt)
                            n, s = tile
                            for k in range(KT):
                                pe.wait_ge(e_ready, KT * n + k + 1 + KT * XR)
                                pe.wait_ge(pt_ready, KT * n + k + 1)
                                for q in range(HP // KT):
                                    last = nc.tensor.transpose(psum[4 + k][:, q * P:(q + 1) * P],
                                                               sm[:, s, k, 2 * q:2 * q + 2, :].rearrange(
                                                                   "p h s -> p (h s)"), ident[:, :])
                                last.then_inc(p_turned, 1)
                            pe.wait_ge(pt_ready, KT * (n + 1) + KT)
                            pe.wait_ge(o_added, n + 1)
                            pe.wait_ge(vx_ready, 2 * (2 * n + 2) + 2 * XC)
                            for hp in range(HP):
                                for h in range(2):
                                    last = nc.tensor.matmul(
                                        psum[6 + s][h * S:(h + 1) * S, hp * 2 * VC:(hp + 1) * 2 * VC],
                                        pt[:, s, hp, h * S:(h + 1) * S], vx[:, 2 * s + h, hp, :],
                                        start=True, stop=True)
                                    if hp == HP - 1:
                                        last.then_inc(pv_done, 1)

                        scores((0, 0))
                        over_tiles(pe, step)

                    @block.vector
                    def _(dve):
                        dve.sem_inc(s_read, KT * XR)
                        dve.sem_inc(o_added, XR)
                        v = Steps(dve, vx_zero)
                        v(nc.vector.memset(vx[:, :, :, :], 0.0))
                        v.wait()
                        for h in range(2):
                            v(nc.vector.memset(vx[h * S:(h + 1) * S, :, :, h * VC + HD:h * VC + HD + 1], 1.0))

                        def masked(tile):
                            n, s = tile
                            v = Steps(dve, mask_step, n * 2 * KT)
                            dve.wait_ge(s_done, 2 * n + 2 + XC)
                            dve.wait_ge(p_turned, KT * (n + 1))
                            for k in range(KT):
                                bank = psum[KT * s + k][:, :].rearrange("p (h s) -> p h s", s=S)
                                part = sm[:, s, k, :, :]
                                nc.vector.tensor_tensor(part, bank, rows(lo_b[:, :], HT), ALU.max
                                                        ).then_inc(s_read, 1)
                                dve.wait_ge(s_read, KT * n + k + 1 + KT * XR)
                                v(nc.vector.tensor_reduce(mx[:, s, k, :], part, AX.X, ALU.max))
                                v.wait()
                                v(nc.vector.tensor_tensor(part, part, each(mx[:, s, k, :], S), ALU.subtract))

                        def step(tile, nxt, _):
                            if nxt is not None:
                                masked(nxt)
                            n, s = tile
                            v = Steps(dve, out_step, n * 2)
                            dve.wait_ge(pv_done, 2 * n + 2 + XC)
                            dve.wait_ge(o_added, n + XR)
                            heads = psum[6 + s][:, 0:HP * 2 * VC].rearrange("p (h c) -> p h c", c=VC)
                            v(nc.vector.reciprocal(rc[:, s, :], heads[:, :, HD]))
                            v.wait()
                            v(nc.vector.tensor_tensor(o[:, s, :, :], heads[:, :, 0:HD], each(rc[:, s, :], HD),
                                                      ALU.mult))
                            v.wait()
                            rows_x = x[:, ds(n, 1), :].rearrange("p o d -> p (o d)")
                            nc.vector.tensor_tensor(rows_x, rows_x, o[:, s, :, :].rearrange("p h d -> p (h d)"),
                                                    ALU.add).then_inc(o_added, 1)

                        masked((0, 0))
                        over_tiles(dve, step)

                    @block.scalar
                    def _(act):
                        nc.scalar.preload_act_table(ACT.Exp)
                        act.sem_inc(e_ready, KT * XR)
                        act.sem_inc(pt_ready, KT)
                        act.sem_inc(p_turned, KT * XR)
                        act.sem_inc(vx_ready, 2 * XC)

                        def operands(tile):
                            n, s = tile
                            for h in range(2):
                                j = 2 * s + h
                                act.wait_ge(s_done, 2 * n + h + 1)
                                apart(act, turns)
                                nc.scalar.activation(qs[:, j, :, :], qT[:, :, ds((2 * n + h) * S, S)], ACT.Copy
                                                     ).then_inc(qs_ready, 1)
                            for g in range(2):
                                j = 2 * s + g
                                act.wait_ge(cv_in[j], 32 * ((n - s) // XR) + 32 if isinstance(n, int)
                                            else (n - s) * (32 // XR) + 32)
                                act.wait_ge(pv_done, 2 * n + g + 1)
                                for h in range(2):
                                    r = slice(h * S, (h + 1) * S)
                                    nc.scalar.activation(
                                        vx[r, j, :, h * VC:h * VC + HD],
                                        cv[r, j, :].rearrange("p (q h d) -> p q h d", h=2, d=HD)[:, :, h, :],
                                        ACT.Identity, scale=tg[r, 1:2]).then_inc(vx_ready, 1)

                        def exponentials(tile):
                            n, s = tile
                            for k in range(KT):
                                act.wait_ge(mask_step, 2 * (KT * n + k) + 2)
                                part = sm[:, s, k, :, :]
                                nc.scalar.activation(part, part, ACT.Exp).then_inc(e_ready, 1)

                        def step(tile, nxt, after):
                            n, s = tile
                            for k in range(KT):
                                act.wait_ge(p_turned, KT * n + k + 1 + KT * XR)
                                if k == 0:
                                    act.wait_ge(pv_done, 2 * n + 2)
                                nc.scalar.activation(pt[:, s, k * 4:k * 4 + 4, :].rearrange("p q t -> p (q t)"),
                                                     psum[4 + k][:, :], ACT.Copy).then_inc(pt_ready, 1)
                            if after is not None:
                                operands(after)
                            if nxt is not None:
                                exponentials(nxt)

                        act.wait_ge(vx_zero, 3)
                        operands((0, 0))
                        operands((1, 1))
                        exponentials((0, 0))
                        over_tiles(act, step)

        with ExitStack() as s7:
            hT = buf("hT7", [P, KT, T], F32, s7)
            wT = buf("wT", [4 * K1, G1, T], F32R, s7)
            scal = buf("scal", [P, NT, G1 + 1], F32, s7)
            selw = buf("selw", [4 * K1, P], F32R, s7)
            s1c = buf("s1c", [4 * K1, 2], F32, s7)
            scb = buf("scb", [P, NSC], F32, s7)
            mur = buf("mur", [MS, D], F32, s7)
            mus = buf("mus", [MS, 2, D], F32R, s7)
            muh = buf("muh", [MS, D], F32R, s7)
            mul_ = buf("mul", [MS, 2, D], F32, s7)
            w_loaded, scaled_ready, wh_ready = sem("w7_loaded"), sem("scaled_ready"), sem("wh_ready")
            mus_ready, prep_ready, prep_step = sem("mus_ready"), sem("prep_ready"), sem("prep_step")
            s1c_ready, turns_pool = sem("s1c_ready"), sem("turns_pool")
            WPARTS = ((0, WD), (WD, WN))
            PREP = 6

            def load_group(sp, g):
                sp.dma_start(raw[:, 0:WN], wf_in[ds(g, 1)].rearrange("o p c -> (o p) c")).then_inc(w_loaded, 16)
                for h in range(2):
                    sp.dma_start(scb[h * S:(h + 1) * S, :], sc_in[ds(g, 1), h, :].broadcast_to([S, NSC])
                                 ).then_inc(w_loaded, 16)
                sp.dma_start(mur[:, :], mu_in[ds(g, 1)].rearrange("o r d -> (o r) d")
                             ).then_inc(w_loaded, 16)

            def scale(pool, g):
                g_ = Steps(pool, prep_step, g * PREP)
                pool.wait_ge(w_loaded, 64 * g + 64)
                g_(nc.gpsimd.tensor_tensor(raw[:, WL:WD], raw[:, WL:WD], scb[:, 0:3 * P], ALU.mult))
                g_.wait()
                dn = raw[S:P, WD + D:WD + 2 * D]
                nc.gpsimd.tensor_tensor(dn, dn, scb[S:P, 3 * P:NSC], ALU.mult).then_inc(scaled_ready, 1)
                pool.wait_ge(scaled_ready, g + 1)

            def stack_mixing(pool, g, s):
                g_ = Steps(pool, prep_step, g * PREP + 1)
                apart(pool, turns_pool)
                g_(nc.gpsimd.tensor_copy(muh[:, :], mur[:, :]))
                g_.wait()
                g_(nc.gpsimd.tensor_tensor(mul_[:, 0, :], mur[:, :], muh[:, :].bitcast(F32), ALU.subtract))
                g_.wait()
                apart(pool, turns_pool)
                g_(nc.gpsimd.tensor_scalar(mul_[:, 0, :], mul_[:, 0, :], s1c[0:MS, 1:2], None, ALU.mult))
                g_(nc.gpsimd.tensor_scalar(mul_[:, 1, :], muh[:, :].bitcast(F32), s1c[0:MS, 0:1], None, ALU.mult))
                g_.wait()
                nc.gpsimd.tensor_tensor(mus[:, s, :], mul_[:, 0, :], mul_[:, 1, :], ALU.add
                                        ).then_inc(mus_ready, 1)
                pool.wait_ge(mus_ready, g + 1)

            def low_part(pool, g, s, part):
                a, b = WPARTS[part]
                pool.wait_ge(wh_ready, 2 * g + part + 1)
                to = prep_ready if part == 1 else prep_step
                nc.gpsimd.tensor_tensor(wlo[:, s, a:b], raw[:, a:b], whi[:, s, a:b].bitcast(F32), ALU.subtract
                                        ).then_inc(to, 1)

            def high_part(s, part):
                a, b = WPARTS[part]
                nc.scalar.activation(whi[:, s, a:b], raw[:, a:b], ACT.Copy).then_inc(wh_ready, 1)

            with ExitStack() as s7a:
                hn = buf("hn7", [P, NT, D], F32, s7a)
                gw = buf("gw", [P, KT, E1], F32, s7a)
                invb = buf("invb", [E1, E1], I32, s7a)
                invf = buf("invf", [E1, 2, E1], F32, s7a)
                eidx = buf("eidx", [E1, 1], F32, s7a)
                sel = buf("sel", [E1, E1], F32, s7a)
                pre = buf("pre", [P, NT, E1 + 8 - TOP1], F32, s7a)
                rep = buf("rep", [P, NT, E1 + 8 - TOP1], F32, s7a)
                pr = pre[:, :, 0:E1]
                big = buf("big", [P, 2, NT, E1], F32, s7a)
                top = buf("top", [P, NT, 8], F32, s7a)
                t1 = buf("t17", [P, 4, NT], F32, s7a)
                tg8 = buf("tg8", [P, 3, NT, G1], F32, s7a)
                wdT = buf("wdT", [E1, T], F32, s7a)
                wst = buf("wst", [P, NT, G1, 32], F32R, s7a)
                jk = buf("jk", [4 * K1, P], F32, s7a)
                pi = buf("pi", [4 * K1, 4], I32, s7a)
                pf = buf("pf", [4 * K1, 3], F32, s7a)
                n7 = Norm("n7", hn)
                ld7, iota_ready, pl7, dv7 = sem("ld7"), sem("iota_ready"), sem("pool_step7"), sem("dve_step7")
                hT_ready, g_done, lm_ready, ex_ready = sem("h7_ready"), sem("g7_done"), sem("lm7_ready"), sem("ex7_ready")
                wd_ready, wd_turned, wdT_ready, f_done = sem("wd_ready"), sem("wd_turned"), sem("wdT_ready"), sem("f_done")
                z_ready, ez_ready, st_ready = sem("z_ready"), sem("ez_ready"), sem("st_ready")
                st_turned, hi_ready, nhi_ready = sem("st_turned"), sem("hi7_ready"), sem("nhi7_ready")

                with nc.Block() as block:
                    @block.sync
                    def _(sp):
                        sp.dma_start(gw[:, :, :], gw_in.rearrange("(k p) e -> p k e", p=P)).then_inc(ld7, 16)
                        sp.dma_start(invb[:, :], inv_in.partition_broadcast(E1)).then_inc(ld7, 16)
                        load_group(sp, 0)
                        sp.wait_ge(prep_ready, 1)
                        load_group(sp, 1)

                    @block.gpsimd
                    def _(pool):
                        g = Steps(pool, pl7)
                        exact = dict(allow_small_or_imprecise_dtypes=True)
                        g(nc.gpsimd.iota(eidx[:, :], pattern=[[0, 1]], base=0, channel_multiplier=1, **exact))
                        g(nc.gpsimd.iota(pi[:, 0:1], pattern=[[0, 1]], base=0, channel_multiplier=1))
                        g(nc.gpsimd.iota(jk[:, :], pattern=[[0, 2], [1, K1], [0, R1]], base=0, channel_multiplier=0,
                                         **exact))
                        g.wait()
                        g(nc.gpsimd.memset(pre[:, :, E1:], 2.0))
                        g(nc.gpsimd.memset(wst[:, :, :, 3 * K1:4 * K1].bitcast(F32), 0.0))
                        g.wait()
                        pool.sem_inc(iota_ready, 1)
                        n7.power(pool)
                        pool.wait_ge(s1c_ready, 1)
                        for j in range(2):
                            scale(pool, j)
                            stack_mixing(pool, j, j)
                            for part in range(2):
                                low_part(pool, j, j, part)

                    @block.tensor
                    def _(pe):
                        n7.transpose(pe)
                        pe.wait_ge(ld7, 32)
                        for t in range(NT):
                            if t % 2 == 0:
                                pe.wait_ge(hT_ready, t // 2 + 1)
                            for k in range(KT):
                                last = nc.tensor.matmul(psum[4][:, t * E1:(t + 1) * E1], hT[:, k, t * P:(t + 1) * P],
                                                        gw[:, k, :], start=(k == 0), stop=(k == KT - 1))
                        last.then_inc(g_done, 1)
                        pe.wait_ge(wd_ready, 1)
                        for t in range(NT):
                            last = nc.tensor.transpose(psum[5 + t // TC][0:E1, (t % TC) * P:(t % TC + 1) * P],
                                                       pr[:, t, :], ident[:, :])
                            if t % TC == TC - 1:
                                last.then_inc(wd_turned, 1)
                        for t in range(NT):
                            pe.wait_ge(wdT_ready, t // TC + 1)
                            last = nc.tensor.matmul(psum[7][:, t * E1:(t + 1) * E1], wdT[:, t * P:(t + 1) * P],
                                                    sel[:, :], start=True, stop=True)
                        last.then_inc(f_done, 1)
                        pe.wait_ge(st_ready, 2)
                        for q in range(2):
                            for c in range(NCH):
                                for t in range(TC):
                                    last = nc.tensor.transpose(psum[q * NCH + c][:, t * P:(t + 1) * P],
                                                               wst[:, c * TC + t, 4 * q:4 * q + 4, :].bitcast(F32
                                                                   ).rearrange("p g k -> p (g k)"), ident[:, :])
                                last.then_inc(st_turned, 1)

                    @block.vector
                    def _(dve):
                        v = Steps(dve, dv7)
                        n7.statistics(dve, v)
                        n7.normalise(dve)
                        dve.wait_ge(iota_ready, 1)
                        v(nc.vector.tensor_scalar(pi[:, 1:2], pi[:, 0:1], 7, None, ALU.bitwise_and))
                        v(nc.vector.tensor_scalar(pi[:, 2:3], pi[:, 0:1], 24, None, ALU.bitwise_and))
                        v.wait()
                        v(nc.vector.tensor_copy(pf[:, 0:2], pi[:, 1:3]))
                        v.wait()
                        v(nc.vector.tensor_scalar(s1c[:, 1:2], pf[:, 1:2], 8.0, None, ALU.is_equal))
                        v.wait()
                        nc.vector.tensor_scalar(s1c[:, 0:1], s1c[:, 1:2], -1.0, 1.0, ALU.mult, ALU.add
                                                ).then_inc(s1c_ready, 1)
                        dve.wait_ge(s1c_ready, 1)
                        v(nc.vector.tensor_scalar(selw[:, :], jk[:, :], pf[:, 0:1], s1c[:, 0:1], ALU.is_equal,
                                                  ALU.mult))
                        dve.wait_ge(ld7, 32)
                        v(nc.vector.tensor_copy(invf[:, 0, :], invb[:, :]))
                        v.wait()
                        v(nc.vector.tensor_scalar(invf[:, 1, :], invf[:, 0, :], 0.0, float(E1), ALU.is_lt, ALU.mult))
                        v.wait()
                        v(nc.vector.tensor_tensor(invf[:, 0, :], invf[:, 0, :], invf[:, 1, :], ALU.add))
                        v.wait()
                        v(nc.vector.tensor_scalar(sel[:, :], invf[:, 0, :], eidx[:, 0:1], None, ALU.is_equal))
                        dve.wait_ge(g_done, 1)
                        logits = psum[4][:, :].rearrange("p (t e) -> p t e", e=E1)
                        v(nc.vector.tensor_reduce(t1[:, 0, :], logits, AX.X, ALU.max))
                        v.wait()
                        nc.vector.tensor_tensor(pr, logits, each(t1[:, 0, :], E1), ALU.subtract
                                                ).then_inc(lm_ready, 1)
                        dve.wait_ge(ex_ready, 1)
                        v(nc.vector.tensor_reduce(t1[:, 1, :], pr, AX.X, ALU.add))
                        v.wait()
                        v(nc.vector.reciprocal(t1[:, 2, :], t1[:, 1, :]))
                        v.wait()
                        v(nc.vector.tensor_tensor(pr, pr, each(t1[:, 2, :], E1), ALU.mult))
                        v.wait()
                        for t in range(NT):
                            v(nc.vector.max(top[:, t, :], pre[:, t, :]))
                        v.wait()
                        for t in range(NT):
                            v(nc.vector.match_replace(rep[:, t, :], top[:, t, :], pre[:, t, :], -1.0))
                        v.wait()
                        nc.vector.scalar_tensor_tensor(pr, rep[:, :, 0:E1], 0.0, pr, ALU.is_lt, ALU.mult
                                                       ).then_inc(wd_ready, 1)
                        dve.wait_ge(f_done, 1)
                        flat, z = big[:, 0, :, :], big[:, 1, :, :]
                        f3 = flat.rearrange("p t (g k) -> p t g k", k=K1)
                        z3 = z.rearrange("p t (g k) -> p t g k", k=K1)
                        v(nc.vector.tensor_copy(flat, psum[7][:, :].rearrange("p (t e) -> p t e", e=E1)))
                        v.wait()
                        v(nc.vector.tensor_reduce(tg8[:, 0, :, :], f3, AX.X, ALU.add))
                        v(nc.vector.tensor_scalar(z, flat, 0.0, -1.0e9, ALU.is_equal, ALU.mult))
                        v.wait()
                        v(nc.vector.tensor_scalar(scal[:, :, 0:G1], tg8[:, 0, :, :], tg[:, 3:4], None, ALU.mult))
                        v(nc.vector.tensor_scalar(scal[:, :, G1], t1[:, 0, :], 0.0, tg[:, 3:4], ALU.mult, ALU.add))
                        v(nc.vector.tensor_tensor(z, z, flat, ALU.add))
                        v.wait()
                        v(nc.vector.tensor_reduce(tg8[:, 1, :, :], z3, AX.X, ALU.max))
                        v.wait()
                        zg = z.rearrange("p t (g k) -> p (t g) k", k=K1)
                        nc.vector.tensor_tensor(zg, zg, each(tg8[:, 1, :, :].rearrange("p t g -> p (t g)"), K1),
                                                ALU.subtract).then_inc(z_ready, 1)
                        dve.wait_ge(ez_ready, 1)
                        v(nc.vector.tensor_reduce(tg8[:, 2, :, :], z3, AX.X, ALU.add))
                        v.wait()
                        v(nc.vector.reciprocal(tg8[:, 0, :, :], tg8[:, 2, :, :]))
                        v.wait()
                        v(nc.vector.tensor_tensor(zg, zg, each(tg8[:, 0, :, :].rearrange("p t g -> p (t g)"), K1),
                                                  ALU.mult))
                        v.wait()
                        nc.vector.tensor_copy(wst[:, :, :, 0:K1], z3).then_inc(hi_ready, 1)
                        dve.wait_ge(hi_ready, 1)
                        nc.vector.tensor_tensor(wst[:, :, :, 2 * K1:3 * K1], z3,
                                                wst[:, :, :, 0:K1].bitcast(F32), ALU.subtract).then_inc(st_ready, 1)
                        for n in range(1, 2 * NCH, 2):
                            dve.wait_ge(st_turned, n + 1)
                            for g in range(4):
                                nc.vector.tensor_copy(wT[:, n // NCH * 4 + g, (n % NCH) * CH:(n % NCH + 1) * CH],
                                                      psum[n][g * 4 * K1:(g + 1) * 4 * K1, :])

                    @block.scalar
                    def _(act):
                        for j in range(4):
                            nc.scalar.activation(hT[:, :, 2 * P * j:2 * P * (j + 1)], n7.turned_bank(act, j),
                                                 ACT.Copy).then_inc(hT_ready, 1)
                        act.wait_ge(scaled_ready, 1)
                        high_part(0, 0)
                        high_part(0, 1)
                        act.wait_ge(lm_ready, 1)
                        nc.scalar.activation(pr, pr, ACT.Exp).then_inc(ex_ready, 1)
                        for c in range(NCH):
                            act.wait_ge(wd_turned, c + 1)
                            nc.scalar.activation(wdT[:, c * CH:(c + 1) * CH], psum[5 + c][0:E1, :], ACT.Copy
                                                 ).then_inc(wdT_ready, 1)
                        act.wait_ge(hT_ready, 4)
                        for k in range(KT):
                            nc.scalar.activation(nhi[:, k, :], hT[:, k, :], ACT.Copy).then_inc(nhi_ready, 1)
                        act.wait_ge(scaled_ready, 2)
                        high_part(1, 0)
                        high_part(1, 1)
                        act.wait_ge(z_ready, 1)
                        nc.scalar.activation(big[:, 1, :, :], big[:, 1, :, :], ACT.Exp).then_inc(ez_ready, 1)
                        act.wait_ge(hi_ready, 1)
                        nc.scalar.activation(wst[:, :, :, K1:2 * K1], wst[:, :, :, 0:K1].bitcast(F32), ACT.Copy
                                             ).then_inc(st_ready, 1)
                        for n in range(0, 2 * NCH, 2):
                            act.wait_ge(st_turned, n + 1)
                            for g in range(4):
                                nc.scalar.activation(wT[:, n // NCH * 4 + g, (n % NCH) * CH:(n % NCH + 1) * CH],
                                                     psum[n][g * 4 * K1:(g + 1) * 4 * K1, :], ACT.Copy)

            with ExitStack() as s8:
                xef = buf("xef", [P, KT, CH], F32, s8)
                xhi = buf("xhi", [P, NCH, KT, CH], F32R, s8)
                xlo = buf("xlo", [P, NCH, KT, CH], F32R, s8)
                we = buf("we", [P, NCH, CH], F32, s8)
                spare = raw[:, WN:WN + 3 * CH].rearrange("p (j c) -> p j c", j=3)
                waf = spare[:, 0, :]
                wahi = buf("wahi", [P, CH], F32R, s8)
                walo = buf("walo", [P, CH], F32R, s8)
                sg0 = spare[:, 1, :]
                sg1 = buf("sg1", [IB, CH], F32, s8)
                h0f = spare[:, 2, :]
                h1f = buf("h1f", [P, CH], F32, s8)
                h0hi = buf("h0hi", [P, NCH, CH], F32R, s8)
                h0lo = buf("h0lo", [P, NCH, CH], F32R, s8)
                h1hi = buf("h1hi", [P, NCH, CH], F32R, s8)
                h1lo = buf("h1lo", [P, NCH, CH], F32R, s8)
                names = ("mu_done qa_done we_done dq_done t_done dn_done we_ready wahi_ready xhi_ready sg_ready "
                         "hhi_ready wadhi_ready xef_ready xlo_ready waf_ready walo_ready wadf_ready wadlo_ready "
                         "hf_ready hlo_ready acc_ready zero_ready nlo_ready turns_pe")
                q8 = {n: sem("m_" + n) for n in names.split()}
                NG = G1 + NS
                DOWN_BANKS = (7, 3, 0, 1)

                def wait(engine, name, value):
                    if not isinstance(value, int) or value > 0:
                        engine.wait_ge(q8[name], value)

                def item_of(g, s, c):
                    return dict(g=g, s=s, c=c, n=g * NCH + c, routed=True)

                def pair(it, routed=True, before=None, after=None):
                    seq = [dict(item_of(2 * it + s, s, c), routed=routed) for s in range(2) for c in range(NCH)]
                    before = seq[0] if before == "same" else before
                    prev = [dict(item_of(2 * it - 1, 1, NCH - 1), routed=routed) if before is seq[0] else before]
                    nxt = [dict(item_of(2 * it + 2, 0, 0), routed=routed) if after == "same" else after]
                    return list(zip(prev + seq[:-1], seq, seq[1:] + nxt))

                def over_items(engine, body):
                    last_routed = item_of(G1 - 1, 1, NCH - 1)
                    first_shared = dict(item_of(G1, 0, 0), routed=False)
                    for p, i, n in pair(0, after="same"):
                        body(p, i, n)
                    with engine.Fori(1, G1 // 2 - 1) as it:
                        for p, i, n in pair(it, before="same", after="same"):
                            body(p, i, n)
                    for p, i, n in pair(G1 // 2 - 1, before="same", after=first_shared):
                        body(p, i, n)
                    for p, i, n in pair(G1 // 2, routed=False, before=last_routed):
                        body(p, i, n)
                    body(dict(item_of(NG - 1, 1, NCH - 1), routed=False), None, None)

                def cols(i):
                    return slice(i["c"] * CH, (i["c"] + 1) * CH)

                with nc.Block() as block:
                    @block.sync
                    def _(sp):
                        with sp.Fori(2, G1) as g:
                            sp.wait_ge(prep_ready, g)
                            load_group(sp, g)
                        for h in range(NS):
                            sp.wait_ge(prep_ready, G1 + h)
                            sp.dma_start(raw[:, 0:WN], ws_in[h]).then_inc(w_loaded, 16)

                    @block.gpsimd
                    def _(pool):
                        for k in range(KT):
                            nc.gpsimd.tensor_tensor(nlo[:, k, :], hT[:, k, :], nhi[:, k, :].bitcast(F32),
                                                    ALU.subtract).then_inc(q8["nlo_ready"], 1)
                        with pool.Fori(1, G1 // 2) as it:
                            for s in range(2):
                                g = 2 * it + s
                                scale(pool, g)
                                wait(pool, "mu_done", (g - 1) * NCH * KT)
                                stack_mixing(pool, g, s)
                                for part in range(2):
                                    low_part(pool, g, s, part)
                        for h in range(NS):
                            for part in range(2):
                                low_part(pool, G1 + h, h, part)

                    @block.tensor
                    def _(pe):
                        def split_product(bank, terms, first, last):
                            n = 0
                            for w, a in terms:
                                for i, j in ((1, 0), (0, 1), (0, 0)):
                                    done = nc.tensor.matmul(bank, w[i], a[j], start=first and n == 0,
                                                            stop=last and n == 3 * len(terms) - 1)
                                    n += 1
                            return done

                        def weights(s, a, b, r=slice(0, P)):
                            return whi[r, s, a:b], wlo[r, s, a:b]

                        def mixed(i):
                            pe.wait_ge(mus_ready, i["g"] + 1)
                            wait(pe, "xef_ready", KT * i["n"])
                            apart(pe, q8["turns_pe"])
                            for k in range(KT):
                                nc.tensor.matmul(psum[k][:, :], mus[:, i["s"], k * P:(k + 1) * P],
                                                 wT[0:MS, ds(i["g"], 1), cols(i)].rearrange("r o t -> r (o t)"),
                                                 start=True, stop=True).then_inc(q8["mu_done"], 1)

                        def stream(i, j, src):
                            terms = [(weights(i["s"], k * 512 + j * P, k * 512 + (j + 1) * P),
                                      (src[0][:, k, :], src[1][:, k, :])) for k in range(KT)]
                            last = split_product(psum[4 + j][:, :], terms, True, not i["routed"])
                            if not i["routed"]:
                                last.then_inc(q8["t_done"], 1)

                        def body(prev, i, nxt):
                            if i is not None:
                                s, c, n = i["s"], i["c"], i["n"]
                                src = (xhi[:, c], xlo[:, c]) if i["routed"] else (nhi[:, :, cols(i)], nlo[:, :, cols(i)])
                                pe.wait_ge(prep_ready, i["g"] + 1)
                                if not i["routed"]:
                                    wait(pe, "nlo_ready", KT)
                            if i is not None and i["routed"]:
                                wait(pe, "xlo_ready", KT * (n + 1))
                                wait(pe, "waf_ready", n)
                                terms = [(weights(s, k * 512 + 384, k * 512 + 512), (src[0][:, k, :], src[1][:, k, :]))
                                         for k in range(KT)]
                                split_product(psum[2][:, :], terms, True, True).then_inc(q8["qa_done"], 1)
                                wait(pe, "acc_ready", TC * (n - 1))
                                apart(pe, q8["turns_pe"])
                                nc.tensor.matmul(psum[3][:, :], selw[0:MS, :],
                                                 wT[0:MS, ds(i["g"], 1), cols(i)].rearrange("r o t -> r (o t)"),
                                                 start=True, stop=True).then_inc(q8["we_done"], 1)
                            if nxt is not None and nxt["routed"]:
                                mixed(nxt)
                            if i is not None:
                                wait(pe, "sg_ready", 2 * n)
                                wait(pe, "hf_ready", 2 * n)
                                stream(i, 0, src)
                                stream(i, 1, src)
                            if prev is not None and prev["routed"]:
                                wait(pe, "hlo_ready", 2 * prev["n"] + 2)
                                if i is None or not i["routed"]:
                                    wait(pe, "acc_ready", TC * prev["n"])
                                sp_, cp = prev["s"], prev["c"]
                                terms = [(weights(sp_, WA, WA + P), (h0hi[:, cp, :], h0lo[:, cp, :])),
                                         (weights(sp_, WA + P, WA + 2 * P, slice(0, IB)),
                                          (h1hi[0:IB, cp, :], h1lo[0:IB, cp, :]))]
                                split_product(psum[7][:, :], terms, True, True).then_inc(q8["dq_done"], 1)
                            if i is not None:
                                stream(i, 2, src)
                            if i is not None and i["routed"]:
                                wait(pe, "walo_ready", n + 1)
                                for f, (w, a) in enumerate(((wlo, wahi), (whi, walo), (whi, wahi))):
                                    for j in range(2):
                                        r, at = slice(j * KR, (j + 1) * KR), WL + j * P
                                        last = nc.tensor.matmul(psum[4 + j][:, :], w[r, s, at:at + P], a[r, :],
                                                                start=False, stop=(f == 2))
                                        if f == 2:
                                            last.then_inc(q8["t_done"], 1)
                                split_product(psum[6][:, :], [(weights(s, WL + 2 * P, WD), (wahi[:, :], walo[:, :]))],
                                              False, True).then_inc(q8["t_done"], 1)
                            if prev is not None:
                                sp_, cp, m = prev["s"], prev["c"], prev["n"]
                                wait(pe, "hlo_ready", 2 * m + 2)
                                if prev["routed"]:
                                    wait(pe, "wadlo_ready", m + 1)
                                if i is not None and i["routed"]:
                                    wait(pe, "we_ready", n + 1)
                                r = P if prev["routed"] else IB
                                for t in range(TC):
                                    wait(pe, "acc_ready", TC * (m - 1) + t + 1)
                                    if t == 2 and nxt is not None and nxt["routed"]:
                                        wait(pe, "xef_ready", KT * nxt["n"] + KT)
                                    tok = slice(t * P, (t + 1) * P)
                                    terms = [((h0hi[:, cp, tok], h0lo[:, cp, tok]), weights(sp_, WD, WD + D)),
                                             ((h1hi[0:r, cp, tok], h1lo[0:r, cp, tok]),
                                              weights(sp_, WD + D, WD + 2 * D, slice(0, r)))]
                                    split_product(psum[DOWN_BANKS[t]][:, 0:D], terms, True, True
                                                  ).then_inc(q8["dn_done"], 1)

                        mixed(item_of(0, 0, 0))
                        over_items(pe, body)

                    @block.vector
                    def _(dve):
                        def mix(i):
                            n = i["n"]
                            for k in range(KT):
                                wait(dve, "mu_done", KT * n + k + 1)
                                wait(dve, "xhi_ready", KT * (n - 1) + k + 1)
                                wait(dve, "xlo_ready", KT * (n - 1) + k + 1)
                                nc.vector.tensor_tensor(xef[:, k, :], psum[k][:, :], hT[:, k, cols(i)], ALU.add
                                                        ).then_inc(q8["xef_ready"], 1)
                            for k in range(KT):
                                wait(dve, "xhi_ready", KT * n + k + 1)
                                nc.vector.tensor_tensor(xlo[:, i["c"], k, :], xef[:, k, :], xhi[:, i["c"], k, :].bitcast(F32),
                                                        ALU.subtract).then_inc(q8["xlo_ready"], 1)

                        def accumulate(prev, ts):
                            m = prev["n"]
                            col = prev["g"] if prev["routed"] else G1
                            for t in ts:
                                g = prev["c"] * TC + t
                                wait(dve, "dn_done", TC * m + t + 1)
                                wait(dve, "acc_ready", TC * (m - NCH) + t + 1)
                                nc.vector.scalar_tensor_tensor(x[:, g, :], psum[DOWN_BANKS[t]][:, 0:D],
                                                               scal[:, g, ds(col, 1)], x[:, g, :], ALU.mult, ALU.add
                                                               ).then_inc(q8["acc_ready"], 1)

                        def body(prev, i, nxt):
                            if i is not None and i["routed"]:
                                n, c = i["n"], i["c"]
                                wait(dve, "qa_done", n + 1)
                                wait(dve, "we_ready", n + 1)
                                nc.vector.tensor_tensor(waf, psum[2][:, :], we[:, c, :], ALU.mult
                                                        ).then_inc(q8["waf_ready"], 1)
                                wait(dve, "wahi_ready", n + 1)
                                nc.vector.tensor_tensor(walo[:, :], waf, wahi[:, :].bitcast(F32), ALU.subtract
                                                        ).then_inc(q8["walo_ready"], 1)
                            if nxt is not None and nxt["routed"]:
                                mix(nxt)
                            if prev is not None and prev["routed"]:
                                m, cp = prev["n"], prev["c"]
                                wait(dve, "dq_done", m + 1)
                                nc.vector.tensor_tensor(h1f[UB:P, :], psum[7][UB:P, :], we[UB:P, cp, :], ALU.mult
                                                        ).then_inc(q8["wadf_ready"], 1)
                                wait(dve, "wadhi_ready", m + 1)
                                nc.vector.tensor_tensor(h1lo[UB:P, cp, :], h1f[UB:P, :],
                                                        h1hi[UB:P, cp, :].bitcast(F32), ALU.subtract
                                                        ).then_inc(q8["wadlo_ready"], 1)
                            if i is not None:
                                n, c = i["n"], i["c"]
                                wait(dve, "dn_done", TC * (n - 1))
                                wait(dve, "t_done", 3 * n + 2)
                                wait(dve, "sg_ready", 2 * n + 1)
                                wait(dve, "hlo_ready", 2 * n)
                                nc.vector.tensor_tensor(h0f, sg0, psum[5][:, :], ALU.mult
                                                        ).then_inc(q8["hf_ready"], 1)
                            if prev is not None:
                                accumulate(prev, [0])
                            if i is not None:
                                wait(dve, "t_done", 3 * n + 3)
                                wait(dve, "sg_ready", 2 * n + 2)
                                nc.vector.tensor_tensor(h1f[0:IB, :], sg1[:, :], psum[6][UB:UB + IB, :], ALU.mult
                                                        ).then_inc(q8["hf_ready"], 1)
                            if prev is not None:
                                accumulate(prev, range(1, TC))
                            if i is not None:
                                wait(dve, "hhi_ready", 2 * n + 1)
                                nc.vector.tensor_tensor(h0lo[:, c, :], h0f, h0hi[:, c, :].bitcast(F32),
                                                        ALU.subtract).then_inc(q8["hlo_ready"], 1)
                                wait(dve, "hhi_ready", 2 * n + 2)
                                nc.vector.tensor_tensor(h1lo[0:IB, c, :], h1f[0:IB, :],
                                                        h1hi[0:IB, c, :].bitcast(F32), ALU.subtract
                                                        ).then_inc(q8["hlo_ready"], 1)

                        mix(item_of(0, 0, 0))
                        for h in (h1hi, h1lo):
                            nc.vector.memset(h[32:UB, :, :].bitcast(F32), 0.0).then_inc(q8["zero_ready"], 1)
                        wait(dve, "zero_ready", 2)
                        over_items(dve, body)

                    @block.scalar
                    def _(act):
                        def mix(i):
                            for k in range(KT):
                                wait(act, "xef_ready", KT * i["n"] + k + 1)
                                nc.scalar.activation(xhi[:, i["c"], k, :], xef[:, k, :], ACT.Copy
                                                     ).then_inc(q8["xhi_ready"], 1)

                        def high(i, part):
                            g = i["g"]
                            if isinstance(g, int) and g in (0, NG - 1):
                                return
                            if isinstance(g, int) and g + 1 >= G1:
                                act.wait_ge(w_loaded, 64 * G1 + 16 * (g + 1 - G1) + 16)
                            else:
                                act.wait_ge(scaled_ready, g + 2)
                            if part == 0:
                                wait(act, "t_done", 3 * NCH * g)
                            else:
                                wait(act, "dn_done", TC * NCH * g)
                            high_part(1 - i["s"], part)

                        def body(prev, i, nxt):
                            if i is not None and i["routed"]:
                                n, c = i["n"], i["c"]
                                wait(act, "we_done", n + 1)
                                wait(act, "wadf_ready", n - 1)
                                nc.scalar.activation(we[:, c, :], psum[3][:, :], ACT.Copy).then_inc(q8["we_ready"], 1)
                                wait(act, "waf_ready", n + 1)
                                nc.scalar.activation(wahi[:, :], waf, ACT.Copy).then_inc(q8["wahi_ready"], 1)
                            if i is not None and i["c"] == 1:
                                high(i, 1)
                            if nxt is not None and nxt["routed"]:
                                mix(nxt)
                            if prev is not None and prev["routed"]:
                                m, cp = prev["n"], prev["c"]
                                wait(act, "wadf_ready", m + 1)
                                nc.scalar.activation(h1hi[UB:P, cp, :], h1f[UB:P, :], ACT.Copy
                                                     ).then_inc(q8["wadhi_ready"], 1)
                            if i is not None:
                                n, c = i["n"], i["c"]
                                wait(act, "t_done", 3 * n + 1)
                                wait(act, "hf_ready", 2 * n)
                                nc.scalar.activation(sg0, psum[4][:, :], ACT.Silu).then_inc(q8["sg_ready"], 1)
                                wait(act, "t_done", 3 * n + 3)
                                nc.scalar.activation(sg1[:, :], psum[6][0:IB, :], ACT.Silu).then_inc(q8["sg_ready"], 1)
                                wait(act, "hf_ready", 2 * n + 1)
                                nc.scalar.activation(h0hi[:, c, :], h0f, ACT.Copy).then_inc(q8["hhi_ready"], 1)
                                wait(act, "hf_ready", 2 * n + 2)
                                nc.scalar.activation(h1hi[0:IB, c, :], h1f[0:IB, :], ACT.Copy
                                                     ).then_inc(q8["hhi_ready"], 1)
                                if c == 0:
                                    high(i, 0)

                        nc.scalar.preload_act_table(ACT.Silu)
                        mix(item_of(0, 0, 0))
                        act.wait_ge(q8["zero_ready"], 2)
                        over_items(act, body)

        out_written = sem("out_written")
        with nc.Block() as block:
            @block.sync
            def _(sp):
                sp.dma_start(out.rearrange("(t p) d -> p t d", p=P), x[:, :, :]).then_inc(out_written, 16)
                sp.wait_ge(out_written, 16)


def layouts(i):
    import numpy as np

    def T_(a):
        return np.ascontiguousarray(np.swapaxes(a, -1, -2))

    ctx = i["ctx_2048"]
    r = {}
    r["x_in"] = i["x"].reshape(T, D)
    r["ctxT_in"] = T_(ctx.reshape(T, D))
    r["ctxTt_in"] = T_(ctx.reshape(NT, P, D))
    r["ctx2_in"] = ctx
    r["mask_in"] = T_(i["mask_BxS2_ik0"])
    r["gx_in"] = i["g_xattn"]
    r["gf_in"] = i["g_ffn"]
    for n in "qkvo":
        r[f"w{n}_in"] = T_(i[f"L0_xattn_W{n}"])
    r["bqk_in"] = T_(np.stack([i["L0_xattn_bq"], i["L0_xattn_bk"]]).reshape(2 * KT, P))
    r["rows_in"] = np.stack([i[f"L0_xattn_{n}"] for n in ("bv", "bo", "ln_gamma", "ln_beta")])
    r["rs_in"] = np.reshape(i["L0_xattn_residual_scale"], (1,))
    r["rw1_in"] = i["L0_ffn_rw1"]
    r["rw2_in"] = i["L0_ffn_rw2"]
    r["w1_in"] = i["L0_ffn_w1"]
    r["b1_in"] = T_(i["L0_ffn_b1"].reshape(E0 * C0, P))
    r["w2_in"] = i["L0_ffn_w2"]
    r["b2_in"] = i["L0_ffn_b2"]
    r["gw_in"] = T_(i["L1_ffn_gate_weight"])
    r["inv_in"] = i["L1_ffn_inv_mapping"].reshape(E1)
    mu = T_(i["L1_ffn_mask_up_W"])
    r["mu_in"] = np.concatenate([mu, mu, mu], axis=1)

    def three(gate, up):
        gap = np.zeros(gate.shape[:-1] + (UB - IB,), gate.dtype)
        return np.concatenate([gate[..., :P], up[..., :P], gate[..., P:], gap, up[..., P:], gap], axis=-1)

    def by_slice(a):
        n, _, c = a.shape
        return a.reshape(n, KT, P, c).transpose(0, 2, 1, 3).reshape(n, P, KT * c)

    def down(a, tail):
        n = a.shape[0]
        gap = np.zeros((n, UB - IB, a.shape[2]), a.dtype)
        rest = np.concatenate([a[:, P:], gap, tail], axis=1)
        return np.concatenate([a[:, :P], rest], axis=2)

    g = {k: i["L1_ffn_" + k] for k in ("gate_W", "gate_qa", "gate_qb", "gate_scale", "up_W", "up_qa", "up_qb",
                                       "up_scale", "down_W", "down_qa", "down_qb", "down_scale")}
    inner = [T_(g[k].reshape(G1, KR, -1)) for k in ("gate_qa", "up_qa")]
    wx = by_slice(np.concatenate([three(T_(g["gate_W"]), T_(g["up_W"]))] + inner, axis=2))
    outer = [g[k].transpose(0, 1, 3, 2).reshape(G1, KR, -1) for k in ("gate_qb", "up_qb", "down_qb")]
    z = np.zeros_like(outer[0])
    wl = np.concatenate([three(outer[0], z), three(z, outer[1])], axis=1)
    wd = down(T_(g["down_W"]), outer[2])
    qa = T_(g["down_qa"].reshape(G1, KR, I1))
    qa = np.concatenate([np.zeros_like(qa), qa], axis=2)
    wa = down(qa, np.zeros((G1, KR, P), qa.dtype))
    r["wf_in"] = np.concatenate([wx, wl, wd, wa], axis=2)
    zs = np.zeros_like(g["gate_scale"])
    r["sc_in"] = np.stack([np.concatenate([three(g["gate_scale"], zs), np.zeros_like(g["down_scale"])], axis=1),
                           np.concatenate([three(zs, g["up_scale"]), g["down_scale"]], axis=1)], axis=1)
    sg, su = (i[f"L1_ffn_sh_{n}_W"].reshape(NS, I1, D) for n in ("gate", "up"))
    sd = T_(i["L1_ffn_sh_down_W"]).reshape(NS, I1, D)
    tail = np.zeros((NS, KR, D), sd.dtype)
    none = np.zeros((NS, D, P), sd.dtype)
    r["ws_in"] = np.concatenate([by_slice(np.concatenate([three(T_(sg), T_(su)), none], axis=2)),
                                 np.zeros((NS, P, 3 * P), sd.dtype), down(sd, tail),
                                 np.zeros((NS, P, 2 * P), sd.dtype)], axis=2)
    return {k: np.ascontiguousarray(v) for k, v in r.items()}


ORDER = ["x_in", "ctxT_in", "ctxTt_in", "ctx2_in", "mask_in", "gx_in", "gf_in", "wq_in", "wk_in", "wv_in", "wo_in",
         "bqk_in", "rows_in", "rs_in", "rw1_in", "rw2_in", "w1_in", "b1_in", "w2_in", "b2_in", "gw_in", "inv_in",
         "mu_in", "wf_in", "sc_in", "ws_in"]


def kernel(**inputs):
    import numpy as np
    from concourse import bacc
    from concourse.bass_utils import run_bass_kernel_spmd

    nc = bacc.Bacc("TRN2", target_bir_lowering=False, num_devices=1)
    arrays = layouts({k: np.asarray(v) for k, v in inputs.items()})
    args = [nc.dram_tensor(n, arrays[n].shape, mybir.dt.from_np(arrays[n].dtype), kind="ExternalInput").ap()
            for n in ORDER]
    out = nc.dram_tensor("out", (T, D), F32, kind="ExternalOutput").ap()
    build(nc, *args, out)
    r = run_bass_kernel_spmd(nc, [arrays], core_ids=[0])
    return r.results[0]["out"].reshape(B, S, D)
```

```python
from contextlib import ExitStack

import concourse.bass as bass
from concourse import mybir

ALU = mybir.AluOpType
ACT = mybir.ActivationFunctionType
AX = mybir.AxisListType
F32 = mybir.dt.float32
F32R = mybir.dt.float32r
I32 = mybir.dt.int32
ds = bass.ds

P = 128
B, S, D = 16, 64, 256
T = B * S
NT = T // P
KT = D // P
NH, HD = 16, 16
HT = P // HD
HP = NH // 2
VC = HD + 1
E0, I0 = 8, 1024
C0 = I0 // P
E1, G1, K1, R1 = 64, 8, 8, 8
I1 = 176
IB = I1 - P
TOP1 = 6
GB = C0 * 4 * E0
NS = 2
KR = K1 * R1
CH = 512
NCH = T // CH
TC = CH // P
EPS = 1e-5
BIG = 3.0e38
FAR = 1.0e30
MASKED = -10000.0
CLIP = 50.0
QSCALE = 1.0 / float(HD) ** 0.5
RES_MAX = 0.3

WX, WL, WD, WA, WN = 0, 1024, 1408, 1920, 2176
SD, SN = 3 * P * KT, 3 * P * KT + 2 * D
UB = 64
NSC = 3 * P + D
MS = 3 * K1
XC, XR = 4, 2


class Steps:

    def __init__(self, engine, sem, base=0):
        self.engine, self.sem, self.base, self.n = engine, sem, base, 0

    def __call__(self, instruction):
        instruction.then_inc(self.sem, 1)
        self.n += 1

    def wait(self):
        self.engine.wait_ge(self.sem, self.base + self.n)


def apart(engine, turns):
    engine.sem_inc(turns, 1)


def each(ap, n):
    p, a = ap.shape
    return ap.unsqueeze(2).broadcast_to([p, a, n])


def rows(ap, n):
    p, a = ap.shape
    return ap.unsqueeze(1).broadcast_to([p, n, a])


def build(nc, x_in, ctxT_in, ctxTt_in, ctx2_in, mask_in, gx_in, gf_in, wq_in, wk_in, wv_in, wo_in, bqk_in,
          rows_in, rs_in, rw1_in, rw2_in, w1_in, b1_in, w2_in, b2_in, gw_in, inv_in, mu_in, wf_in, sc_in,
          ws_in, out):
    with ExitStack() as ctx:
        psum = [ctx.enter_context(nc.psum_tensor(f"bank{i}", [P, 512], F32)) for i in range(8)]

        def buf(name, shape, dt=F32, where=ctx):
            return where.enter_context(nc.sbuf_tensor(name, shape, dt))

        def sem(name):
            return ctx.enter_context(nc.semaphore(name))

        x = buf("x", [P, NT, D])
        ident = buf("ident", [P, P])
        hmask = buf("hmask", [P, HT])
        tg = buf("tg", [P, 4])
        stats = buf("stats", [P, NT, 6])
        mv = buf("mv", [P, NT, 2])
        rstd = buf("rstd", [P, NT])
        var = buf("var", [P, NT])
        mhalf = buf("mhalf", [P, NT])
        nhi = buf("nhi", [P, KT, T], F32R)
        nlo = buf("nlo", [P, KT, T], F32R)
        raw = buf("raw", [P, 2 * 2048])
        whi = buf("whi", [P, 2, 4096], F32R)
        wlo = buf("wlo", [P, 2, 4096], F32R)
        wts = buf("wts", [P, NT, 3, E0])
        b1 = buf("b1", [P, E0 * C0])
        cst = buf("cst", [3 * E0, D])

        lg = buf("lg", [P, NT, E0], F32)
        t8 = buf("t8", [P, 4, NT, E0], F32)
        oh = buf("oh", [P, 2, NT, E0], F32)
        t1 = buf("t1", [P, 8, NT], F32)
        rev = buf("rev", [P, E0], F32)
        ones = buf("ones", [P, P], F32)
        cnt = buf("cnt", [P, 2, E0], F32)
        actv = buf("actv", [P, 2, E0], F32)
        const3, dv3 = sem("const3"), sem("dve_step3")
        ex_ready, lm_ready, cnt_ready, cnt_done = sem("ex_ready"), sem("lm_ready"), sem("cnt_ready"), sem("cnt_done")
        router_step = sem("router_step")

        raw_loaded = sem("raw_loaded")
        whi_ready, wlo_ready = sem("whi_ready"), sem("wlo_ready")
        turns = sem("turns")

        def load_expert0(sp, e):
            sp.dma_start(raw[:, 0:2048].rearrange("p (k i) -> p k i", k=KT),
                         w1_in[e].rearrange("(k p) i -> p k i", p=P)).then_inc(raw_loaded, 16)
            sp.dma_start(raw[:, 2048:4096].rearrange("p (c d) -> p c d", c=C0),
                         w2_in[e].rearrange("(c p) d -> p c d", p=P)).then_inc(raw_loaded, 16)

        def expert_high(act, e):
            act.wait_ge(raw_loaded, 32 * e + 32)
            nc.scalar.activation(whi[:, e, :], raw[:, :], ACT.Copy).then_inc(whi_ready, 1)

        def expert_low(pool, e):
            pool.wait_ge(whi_ready, e + 1)
            nc.gpsimd.tensor_tensor(wlo[:, e, :], raw[:, :], whi[:, e, :].bitcast(F32), ALU.subtract
                                    ).then_inc(wlo_ready, 1)

        def split_keys(pool, keysT, kx, kx_ready, b, j):
            for k in range(KT):
                keys = keysT[:, k, ds(b * S, S)]
                nc.gpsimd.tensor_tensor(kx[:, j, k, :, :], rows(keys, HT), each(hmask[:, :], S), ALU.mult
                                        ).then_inc(kx_ready, 1)

        def over_tiles(engine, step):
            def body(it, last):
                for s in range(XR):
                    after = [(XR * it + s + d, (s + d) % XR) for d in range(3)]
                    step(*(None if last and s + d >= XR else after[d] for d in range(3)))
            with engine.Fori(0, NT // XR - 1) as it:
                body(it, False)
            body(NT // XR - 1, True)

        class Norm:

            var_ready, rstd_ready = sem("norm_var_ready"), sem("norm_rstd_ready")
            rows_ready, turned = sem("norm_rows_ready"), sem("norm_turned")

            def __init__(self, hn, norms, turns):
                self.hn, self.halves, self.tiles = hn, 2 * norms, NT * turns

            def tile_statistics(self, v, tiles, src):
                for t in tiles:
                    v(nc.vector.bn_stats(stats[:, t, :], src[:, t, :]))

            def statistics(self, dve, v, scale2=None, src=None, before=None, stats_done=False):
                src = x if src is None else src
                for half in range(2):
                    tiles = slice(half * NT // 2, (half + 1) * NT // 2)
                    if before is not None:
                        before(half)
                    if not stats_done:
                        self.tile_statistics(v, range(tiles.start, tiles.stop), src)
                    v.wait()
                    for t in range(tiles.start, tiles.stop):
                        v(nc.vector.bn_aggr(mv[:, t, :], stats[:, t, :]))
                    v.wait()
                    if scale2 is None:
                        nc.vector.tensor_scalar(var[:, tiles], mv[:, tiles, 1], EPS, None, ALU.add
                                                ).then_inc(self.var_ready, 1)
                    else:
                        nc.vector.tensor_scalar(var[:, tiles], mv[:, tiles, 1], scale2, EPS, ALU.mult,
                                                ALU.add).then_inc(self.var_ready, 1)

            def power(self, pool):
                for half in range(2):
                    tiles = slice(half * NT // 2, (half + 1) * NT // 2)
                    pool.wait_ge(self.var_ready, self.halves + half + 1)
                    nc.gpsimd.tensor_tensor(rstd[:, tiles], var[:, tiles], mhalf[:, tiles], ALU.pow
                                            ).then_inc(self.rstd_ready, 1)

            def normalise(self, dve, src=None):
                src = x if src is None else src
                for t in range(NT):
                    if t % (NT // 2) == 0:
                        dve.wait_ge(self.rstd_ready, self.halves + t // (NT // 2) + 1)
                    nc.vector.tensor_scalar(self.hn[:, t, :], src[:, t, :], mv[:, t, 0:1], rstd[:, t:t + 1],
                                            ALU.subtract, ALU.mult).then_inc(self.rows_ready, 1)

            def transpose(self, pe):
                for t in range(NT):
                    pe.wait_ge(self.rows_ready, self.tiles + t + 1)
                    for k in range(KT):
                        at = k * 2 * P + (t % 2) * P
                        last = nc.tensor.transpose(psum[t // 2][:, at:at + P], self.hn[:, t, k * P:(k + 1) * P],
                                                   ident[:, :])
                    last.then_inc(self.turned, 1)

            def turned_bank(self, engine, j):
                engine.wait_ge(self.turned, self.tiles + 2 * j + 2)
                return psum[j][:, :].rearrange("p (k t) -> p k t", k=KT)

        with ExitStack() as s1:
            def buf1(name, shape, dt=F32):
                return buf(name, shape, dt, s1)

            kT = buf1("kT", [P, KT, T])
            qT = buf1("qT", [P, KT, T])
            oT = buf1("oT", [P, KT, T])
            wo = buf1("wo", [P, KT, D])
            wv = buf1("wv", [P, KT, D])
            lrow = buf1("lrow", [P, 4, D])
            mcol = buf1("mcol", [P, 2, B])
            rs2 = buf1("rs2", [P, 2])
            hn = buf1("hn", [P, NT, D])

            kx = buf1("kx", [P, XC, KT, HT, S])
            kx_ready = sem("kx_ready")
            vx = buf1("vx", [P, XC, HP, 2 * VC])
            vx_zero = sem("vx_zero")

            ld = {n: sem(f"ld_{n}") for n in ("wk", "wqk", "rest", "small", "mask")}
            ld_x, ld_ctx = [sem(f"ld_x{h}") for h in range(2)], [sem(f"ld_ctx{h}") for h in range(2)]
            const_ready, cst_zero = sem("const_ready"), sem("cst_zero")
            pool_step, dve_step1, act_step = sem("pool_step1"), sem("dve_step1"), sem("act_step1")
            n1 = Norm(hn, 0, 0)
            k_done, q_done, h_ready = sem("k_done"), sem("q_done"), sem("h_ready")

            with ExitStack() as s1a:
                ctxT = buf("ctxT", [P, KT, T], F32, s1a)
                hT = buf("hT", [P, KT, T], F32, s1a)
                wq = buf("wq", [P, KT, D], F32, s1a)
                wk = buf("wk", [P, KT, D], F32, s1a)
                bqk = buf("bqk", [P, 2, KT], F32, s1a)
                g4 = buf("g4", [P, 4], F32, s1a)
                mraw = buf("mraw", [P, B], I32, s1a)
                mflt = buf("mflt", [P, B], F32, s1a)
                rsr = buf("rsr", [P, 1], F32, s1a)

                with nc.Block() as block:
                    @block.sync
                    def _(sp):
                        sp.dma_start(wk[:, :, :], wk_in.rearrange("(k p) d -> p k d", p=P)).then_inc(ld["wk"], 16)
                        for h in range(2):
                            sp.dma_start(x[:, h * 4:h * 4 + 4, :],
                                         x_in.rearrange("(t p) d -> p t d", p=P)[:, h * 4:h * 4 + 4, :]
                                         ).then_inc(ld_x[h], 16)
                        sp.dma_start(wq[:, :, :], wq_in.rearrange("(k p) d -> p k d", p=P)).then_inc(ld["wqk"], 16)
                        sp.dma_start(rsr[:, :], rs_in.partition_broadcast(P)).then_inc(ld["small"], 16)
                        sp.dma_start(g4[:, 0:2], gx_in.partition_broadcast(P)).then_inc(ld["small"], 16)
                        sp.dma_start(g4[:, 2:4], gf_in.partition_broadcast(P)).then_inc(ld["small"], 16)
                        sp.dma_start(wv[:, :, :], wv_in.rearrange("(k p) d -> p k d", p=P)).then_inc(ld["rest"], 16)
                        sp.dma_start(wo[:, :, :], wo_in.rearrange("(k p) d -> p k d", p=P)).then_inc(ld["rest"], 16)
                        sp.dma_start(lrow[:, :, :], rows_in.partition_broadcast(P)).then_inc(ld["rest"], 16)
                        for h in range(2):
                            sp.dma_start(mraw[h * S:(h + 1) * S, :], mask_in).then_inc(ld["mask"], 16)
                        sp.dma_start(b1[:, :], b1_in).then_inc(ld["rest"], 16)
                        sp.wait_ge(cst_zero, 1)
                        for j in (0, 2):
                            sp.dma_start(cst[j * E0:(j + 1) * E0, :], b2_in).then_inc(ld["rest"], 16)
                        load_expert0(sp, 0)
                        sp.wait_ge(ld["rest"], 96)

                    @block.gpsimd
                    def _(pool):
                        g = Steps(pool, pool_step)
                        nc.gpsimd.memset(cst[:, :], 0.0).then_inc(cst_zero, 1)
                        pool.wait_ge(cst_zero, 1)
                        nc.gpsimd.memset(mhalf[:, :], -0.5)
                        g(nc.gpsimd.memset(ident[:, :], 0.0))
                        g(nc.gpsimd.memset(hmask[:, :], 1.0))
                        g.wait()
                        nc.gpsimd.affine_select(out=ident[:, :], in_=ident[:, :], compare_op=ALU.not_equal, fill=1.0,
                                                base=0, pattern=[[-1, P]], channel_multiplier=1
                                                ).then_inc(const_ready, 1)
                        g(nc.gpsimd.affine_select(out=hmask[:, :], in_=hmask[:, :], compare_op=ALU.is_ge, fill=0.0,
                                                  base=0, pattern=[[-HD, HT]], channel_multiplier=1))
                        g.wait()
                        g(nc.gpsimd.affine_select(out=hmask[:, :], in_=hmask[:, :], compare_op=ALU.is_ge, fill=0.0,
                                                  base=HD - 1, pattern=[[HD, HT]], channel_multiplier=-1))
                        n1.power(pool)
                        nc.gpsimd.memset(vx[:, :, :, :], 0.0).then_inc(vx_zero, 1)
                        for h in range(2):
                            pool.wait_ge(vx_zero, h + 1)
                            nc.gpsimd.memset(vx[h * S:(h + 1) * S, :, :, h * VC + HD:h * VC + HD + 1], 1.0
                                             ).then_inc(vx_zero, 1)
                        pool.wait_ge(vx_zero, 3)
                        g.wait()
                        pool.wait_ge(act_step, 2 + KT)
                        for j in range(XC):
                            split_keys(pool, kT, kx, kx_ready, j, j)

                    @block.vector
                    def _(dve):
                        v = Steps(dve, dve_step1)
                        n1.statistics(dve, v, before=lambda half: dve.wait_ge(ld_x[half], 16))
                        dve.wait_ge(ld["mask"], 32)
                        v(nc.vector.tensor_copy(mflt[:, :], mraw[:, :]))
                        v.wait()
                        v(nc.vector.tensor_scalar(mcol[:, 0, :], mflt[:, :], 0.5, None, ALU.is_gt))
                        dve.wait_ge(ld["small"], 48)
                        v(nc.vector.tensor_scalar(rs2[:, 0:1], rsr[:, :], 0.0, RES_MAX, ALU.max, ALU.min))
                        v.wait()
                        v(nc.vector.tensor_scalar(mcol[:, 1, :], mcol[:, 0, :], -1.0, CLIP, ALU.add, ALU.mult))
                        v(nc.vector.tensor_tensor(rs2[:, 1:2], rs2[:, 0:1], rs2[:, 0:1], ALU.mult))
                        n1.normalise(dve)

                    @block.tensor
                    def _(pe):
                        pe.wait_ge(ld["wk"], 16)
                        for c in range(NCH):
                            pe.wait_ge(ld_ctx[c], 16)
                            for m in range(KT):
                                for k in range(KT):
                                    last = nc.tensor.matmul(psum[4 + m * NCH + c][:, :], wk[:, k, m * P:(m + 1) * P],
                                                            ctxT[:, k, c * CH:(c + 1) * CH], start=(k == 0),
                                                            stop=(k == KT - 1))
                                last.then_inc(k_done, 1)
                        pe.wait_ge(const_ready, 1)
                        n1.transpose(pe)
                        pe.wait_ge(ld["wqk"], 32)
                        pe.wait_ge(h_ready, 4)
                        for m in range(KT):
                            for c in range(NCH):
                                for k in range(KT):
                                    last = nc.tensor.matmul(psum[m * NCH + c][:, :], wq[:, k, m * P:(m + 1) * P],
                                                            hT[:, k, c * CH:(c + 1) * CH], start=(k == 0),
                                                            stop=(k == KT - 1))
                                last.then_inc(q_done, 1)

                    @block.scalar
                    def _(act):
                        a = Steps(act, act_step)
                        for c in range(NCH):
                            cols = slice(c * CH, (c + 1) * CH)
                            act.dma_start(ctxT[:, :, cols], ctxT_in.rearrange("(k p) t -> p k t", p=P)[:, :, cols]
                                          ).then_inc(ld_ctx[c], 16)
                        act.dma_start(bqk[:, :, :], bqk_in.rearrange("p (j k) -> p j k", j=2)
                                      ).then_inc(ld["wqk"], 16)
                        act.wait_ge(ld["small"], 48)
                        a(nc.scalar.activation(tg[:, :], g4[:, :], ACT.Tanh))
                        act.wait_ge(ld["wqk"], 32)
                        a(nc.scalar.mul(bqk[:, 0, :], bqk[:, 0, :], QSCALE))
                        a.wait()
                        for c in range(NCH):
                            for m in range(KT):
                                act.wait_ge(k_done, c * KT + m + 1)
                                a(nc.scalar.activation(kT[:, m, c * CH:(c + 1) * CH], psum[4 + m * NCH + c][:, :],
                                                       ACT.Identity, bias=bqk[:, 1, m:m + 1]))
                        for j in range(4):
                            nc.scalar.activation(hT[:, :, 2 * P * j:2 * P * (j + 1)], n1.turned_bank(act, j),
                                                 ACT.Copy).then_inc(h_ready, 1)
                        for m in range(KT):
                            for c in range(NCH):
                                act.wait_ge(q_done, m * NCH + c + 1)
                                nc.scalar.activation(qT[:, m, c * CH:(c + 1) * CH], psum[m * NCH + c][:, :],
                                                     ACT.Identity, bias=bqk[:, 0, m:m + 1], scale=QSCALE)

            with ExitStack() as s2:
                cv = buf("cv", [P, XR, KT, P], F32, s2)
                sc = buf("sc", [P, XC, CH], F32, s2)
                pt = buf("pt", [P, XC, CH], F32, s2)
                rc = buf("rc", [P, XR, NH], F32, s2)
                o = buf("o", [P, XR, NH, HD], F32, s2)
                cv_in = [sem(f"cv_in{j}") for j in range(XR)]
                v_done, vx_ready, s_done, sc_ready = sem("v_done"), sem("vx_ready"), sem("s_done"), sem("sc_ready")
                p_ready, pv_done, rc_ready, o_ready = sem("p_ready"), sem("pv_done"), sem("rc_ready"), sem("o_ready")
                o_turned, o_copied = sem("o_turned"), sem("o_copied")
                NI = B // XC

                with nc.Block() as block:
                    @block.sync
                    def _(sp):
                        with sp.Fori(0, NI) as it:
                            for j in range(XR):
                                sp.wait_ge(v_done, XR * it + j + 1)
                                sp.dma_start(cv[:, j, :, :],
                                             ctxTt_in[ds(XR * it + j, 1)].rearrange("o (k p) c -> p (o k) c", p=P)
                                             ).then_inc(cv_in[j], 16)

                    @block.gpsimd
                    def _(pool):
                        with pool.Fori(1, NI) as it:
                            for j in range(XC):
                                pool.wait_ge(s_done, XC * it + j + 1)
                                split_keys(pool, kT, kx, kx_ready, XC * it + j, j)

                    @block.tensor
                    def _(pe):
                        pe.sem_inc(v_done, XR)
                        pe.sem_inc(s_done, XC)

                        def values(tile):
                            n, s = tile
                            pe.wait_ge(o_copied, n + 1)
                            pe.wait_ge(cv_in[s], 16 * ((n - s) // XR) + 16 if isinstance(n, int)
                                       else (n - s) * (16 // XR) + 16)
                            for k in range(KT):
                                last = nc.tensor.matmul(psum[s][:, 0:D], cv[:, s, k, :], wv[:, k, :],
                                                        start=(k == 0), stop=(k == KT - 1))
                            last.then_inc(v_done, 1)

                        def scores(tile):
                            n, s = tile
                            for h in range(2):
                                j = 2 * s + h
                                pe.wait_ge(kx_ready, KT * (2 * n + h + 1))
                                pe.wait_ge(sc_ready, 2 * n + h + 1)
                                for hp in range(HP):
                                    k, q = hp // (HP // KT), 2 * (hp % (HP // KT))
                                    last = nc.tensor.matmul(psum[2 + j][:, hp * S:(hp + 1) * S],
                                                            kx[:, j, k, q:q + 2, :],
                                                            qT[:, k, ds((2 * n + h) * S, S)],
                                                            start=True, stop=True)
                                last.then_inc(s_done, 1)

                        def product(tile):
                            n, s = tile
                            pe.wait_ge(o_ready, n + 1)
                            pe.wait_ge(vx_ready, 2 * (2 * n + 2))
                            pe.wait_ge(p_ready, 2 * n + 2 + XC)
                            for hp in range(HP):
                                for h in range(2):
                                    j = 2 * s + h
                                    last = nc.tensor.matmul(psum[6 + s][h * S:(h + 1) * S, hp * 2 * VC:(hp + 1) * 2 * VC],
                                                            pt[:, j, hp * S:(hp + 1) * S], vx[:, j, hp, :],
                                                            start=True, stop=True)
                                    if hp == HP - 1:
                                        last.then_inc(pv_done, 1)

                        def turn(tile):
                            n, s = tile
                            pe.wait_ge(o_ready, n + 1 + XR)
                            for k in range(KT):
                                last = nc.tensor.transpose(psum[s][:, k * P:(k + 1) * P],
                                                           o[:, s, k * HT:(k + 1) * HT, :].rearrange(
                                                               "p h d -> p (h d)"), ident[:, :])
                            last.then_inc(o_turned, 1)

                        def step(tile, nxt, _):
                            if nxt is not None:
                                scores(nxt)
                            product(tile)
                            if nxt is not None:
                                values(nxt)
                            pe.wait_ge(vx_ready, 4 * (tile[0] + 1))
                            turn(tile)

                        scores((0, 0))
                        values((0, 0))
                        over_tiles(pe, step)

                    @block.vector
                    def _(dve):
                        dve.sem_inc(sc_ready, XC)
                        dve.sem_inc(o_ready, XR)

                        def values(tile):
                            n, s = tile
                            dve.wait_ge(v_done, n + 1 + XR)
                            dve.wait_ge(pv_done, 2 * n + 2)
                            for g in range(2):
                                bank = psum[s][:, 0:D].rearrange("p (q h d) -> p q h d", h=2, d=HD)
                                own = slice(g * S, (g + 1) * S)
                                for h in range(2):
                                    nc.vector.tensor_tensor(
                                        vx[h * S:(h + 1) * S, 2 * s + g, :, h * VC:h * VC + HD], bank[own, :, h, :],
                                        lrow[own, 0, :].rearrange("p (q h d) -> p q h d", h=2, d=HD)[:, :, h, :],
                                        ALU.add).then_inc(vx_ready, 1)

                        def clip(tile):
                            n, s = tile
                            for h in range(2):
                                dve.wait_ge(s_done, 2 * n + h + 1 + XC)
                                dve.wait_ge(p_ready, 2 * n + h + 1)
                                nc.vector.tensor_scalar(sc[:, 2 * s + h, :], psum[2 + 2 * s + h][:, :], CLIP, -CLIP,
                                                        ALU.min, ALU.max).then_inc(sc_ready, 1)

                        def divide(tile):
                            n, s = tile
                            dve.wait_ge(pv_done, 2 * n + 2 + XC)
                            dve.wait_ge(o_ready, n + 1)
                            heads = psum[6 + s][:, 0:HP * 2 * VC].rearrange("p (h c) -> p h c", c=VC)
                            nc.vector.reciprocal(rc[:, s, :], heads[:, :, HD]).then_inc(rc_ready, 1)
                            dve.wait_ge(rc_ready, n + 1)
                            dve.wait_ge(o_turned, n + 1)
                            nc.vector.tensor_tensor(o[:, s, :, :], heads[:, :, 0:HD], each(rc[:, s, :], HD),
                                                    ALU.mult).then_inc(o_ready, 1)

                        def step(tile, nxt, _):
                            if nxt is not None:
                                clip(nxt)
                            divide(tile)
                            if nxt is not None:
                                values(nxt)

                        clip((0, 0))
                        values((0, 0))
                        over_tiles(dve, step)

                    @block.scalar
                    def _(act):
                        nc.scalar.preload_act_table(ACT.Exp)
                        act.sem_inc(p_ready, XC)
                        act.sem_inc(pv_done, XC)
                        act.sem_inc(o_turned, XR)
                        act.sem_inc(o_copied, XR)

                        def exponentials(tile):
                            n, s = tile
                            for h in range(2):
                                b, j = 2 * n + h, 2 * s + h
                                act.wait_ge(sc_ready, b + 1 + XC)
                                act.wait_ge(pv_done, b + 1)
                                apart(act, turns)
                                nc.scalar.activation(pt[:, j, :], sc[:, j, :], ACT.Exp, bias=mcol[:, 1, ds(b, 1)],
                                                     scale=mcol[:, 0, ds(b, 1)]).then_inc(p_ready, 1)

                        def step(tile, nxt, _):
                            if nxt is not None:
                                exponentials(nxt)
                            n, s = tile
                            act.wait_ge(o_turned, n + 1 + XR)
                            apart(act, turns)
                            nc.scalar.activation(oT[:, :, ds(n * P, P)],
                                                 psum[s][:, 0:KT * P].rearrange("p (k t) -> p k t", k=KT),
                                                 ACT.Copy).then_inc(o_copied, 1)

                        exponentials((0, 0))
                        over_tiles(act, step)

            with ExitStack() as s3:
                dl = buf("dl", [P, NT, D], F32, s3)
                hT = buf("hT3", [P, KT, T], F32, s3)
                rw1 = buf("rw1", [P, KT, P], F32, s3)
                rw2 = buf("rw2", [P, E0], F32, s3)
                rg = buf("rg", [P, T], F32, s3)
                gm = buf("gm", [P, 2, D], F32, s3)
                rstd2 = buf("rstd2", [P, NT], F32, s3)
                ld3 = sem("ld_router")
                nhi_ready, wo_done = sem("nhi3_ready"), sem("wo_done")
                nd, n2 = Norm(dl, 1, 1), Norm(hn, 2, 1)
                hT_ready, r1_done, rg_ready, lg_done = sem("h3_ready"), sem("r1_done"), sem("rg_ready"), sem("lg_done")

                with nc.Block() as block:
                    @block.sync
                    def _(sp):
                        sp.dma_start(rw1[:, :, :], rw1_in.rearrange("(k p) m -> p k m", p=P)).then_inc(ld3, 16)
                        sp.dma_start(rw2[:, :], rw2_in).then_inc(ld3, 16)
                        sp.wait_ge(wlo_ready, 1)
                        load_expert0(sp, 1)

                    @block.gpsimd
                    def _(pool):
                        nc.gpsimd.memset(ones[:, :], 1.0)
                        nc.gpsimd.iota(rev[:, :], pattern=[[-1, E0]], base=E0, channel_multiplier=0,
                                       allow_small_or_imprecise_dtypes=True).then_inc(const3, 1)
                        expert_low(pool, 0)
                        nd.power(pool)
                        n2.power(pool)

                    @block.tensor
                    def _(pe):
                        for t in range(NT):
                            for k in range(KT):
                                last = nc.tensor.matmul(psum[t // 2][:, (t % 2) * D:(t % 2 + 1) * D],
                                                        oT[:, k, t * P:(t + 1) * P], wo[:, k, :], start=(k == 0),
                                                        stop=(k == KT - 1))
                            last.then_inc(wo_done, 1)
                        n2.transpose(pe)
                        pe.wait_ge(ld3, 32)
                        pe.wait_ge(hT_ready, 4)
                        for c in range(NCH):
                            for k in range(KT):
                                last = nc.tensor.matmul(psum[4 + c][:, :], rw1[:, k, :], hT[:, k, c * CH:(c + 1) * CH],
                                                        start=(k == 0), stop=(k == KT - 1))
                            last.then_inc(r1_done, 1)
                        for t in range(NT):
                            if t % TC == 0:
                                pe.wait_ge(rg_ready, t // TC + 1)
                            last = nc.tensor.matmul(psum[6][:, t * E0:(t + 1) * E0], rg[:, t * P:(t + 1) * P],
                                                    rw2[:, :], start=True, stop=True)
                        last.then_inc(lg_done, 1)

                    @block.vector
                    def _(dve):
                        v = Steps(dve, dv3)
                        v(nc.vector.tensor_scalar(gm[:, :, :], lrow[:, 2:4, :], tg[:, 0:1], None, ALU.mult))
                        v.wait()
                        v(nc.vector.tensor_tensor(x[:, :, :], x[:, :, :], rows(gm[:, 1, :], NT), ALU.add))
                        for j in range(NT // 2):
                            dve.wait_ge(wo_done, 2 * j + 2)
                            v(nc.vector.tensor_tensor(dl[:, 2 * j:2 * j + 2, :],
                                                      psum[j][:, :].rearrange("p (t d) -> p t d", t=2),
                                                      rows(lrow[:, 1, :], 2), ALU.add))
                            v.wait()
                            nd.tile_statistics(v, range(2 * j, 2 * j + 2), dl)
                        nd.statistics(dve, v, scale2=rs2[:, 1:2], stats_done=True)
                        for t in range(NT):
                            v(nc.vector.scalar_tensor_tensor(dl[:, t, :], dl[:, t, :], mv[:, t, 0:1], gm[:, 0, :],
                                                             ALU.subtract, ALU.mult))
                        dve.wait_ge(nd.rstd_ready, nd.halves + 2)
                        v(nc.vector.tensor_scalar(rstd2[:, :], rstd[:, :], rs2[:, 0:1], None, ALU.mult))
                        v.wait()

                        def onto_stream(half):
                            for t in range(half * NT // 2, (half + 1) * NT // 2):
                                v(nc.vector.scalar_tensor_tensor(x[:, t, :], dl[:, t, :], rstd2[:, t:t + 1],
                                                                 x[:, t, :], ALU.mult, ALU.add))
                            v.wait()

                        n2.statistics(dve, v, before=onto_stream)
                        n2.normalise(dve)
                        for j in range(4):
                            cols = slice(2 * P * j, 2 * P * (j + 1))
                            dve.wait_ge(nhi_ready, j + 1)
                            v(nc.vector.tensor_tensor(nlo[:, :, cols], hT[:, :, cols], nhi[:, :, cols].bitcast(F32),
                                                      ALU.subtract))

                    @block.scalar
                    def _(act):
                        expert_high(act, 0)
                        for j in range(4):
                            cols = slice(2 * P * j, 2 * P * (j + 1))
                            nc.scalar.activation(hT[:, :, cols], n2.turned_bank(act, j), ACT.Copy
                                                 ).then_inc(hT_ready, 1)
                        for j in range(4):
                            cols = slice(2 * P * j, 2 * P * (j + 1))
                            act.wait_ge(hT_ready, j + 1)
                            nc.scalar.activation(nhi[:, :, cols], hT[:, :, cols], ACT.Copy).then_inc(nhi_ready, 1)
                        for c in range(NCH):
                            act.wait_ge(r1_done, c + 1)
                            nc.scalar.activation(rg[:, c * CH:(c + 1) * CH], psum[4 + c][:, :], ACT.Gelu
                                                 ).then_inc(rg_ready, 1)

        with ExitStack() as s4:
            hhi = buf("hhi", [P, NCH, C0, CH], F32R, s4)
            hlo = buf("hlo", [P, NCH, C0, CH], F32R, s4)
            ga = buf("ga", [P, 4, CH], F32, s4)
            gb = buf("gb", [P, E0 * C0], F32, s4)
            gbp = buf("gbp", [P, E0 * (GB + 1)], F32R, s4)
            gbe = buf("gbe", [P, 2, GB], F32R, s4)
            gbd = gbp[:, :].rearrange("p (e q) -> p e q", q=GB + 1)[:, :, 0:GB].rearrange(
                "p e (m j) -> p e m j", j=4 * E0)
            gb_ready, gbz_ready, gbh_ready, gbs_ready = sem("gb_ready"), sem("gbz_ready"), sem("gbh_ready"), sem("gbs_ready")
            gbe_ready = sem("gbe_ready")
            hid_done, act_ready, hi_ready, split_ready = (sem("hid_done"), sem("act_ready"), sem("hi_ready"),
                                                          sem("split_ready"))
            y_done, acc_ready, c_done, c_read = sem("y_done"), sem("acc_ready"), sem("c_done"), sem("c_read")
            NPAIR = E0 // 2
            LAST = object()

            def items(it, last):
                seq = [(2 * it + s, s, c) for s in range(2) for c in range(NCH)]
                nxt = seq[1:] + [None if last else (2 * it + 2, 0, 0)]
                return list(zip(seq, nxt))

            def over_pairs(engine, body):
                with engine.Fori(0, NPAIR - 1) as it:
                    body(it, False)
                body(NPAIR - 1, True)

            def unit(item):
                return (item[0] * NCH + item[2]) * C0

            def tile(item):
                return (item[0] * NCH + item[2]) * TC

            with nc.Block() as block:
                @block.sync
                def _(sp):
                    with sp.Fori(2, E0) as e:
                        sp.wait_ge(wlo_ready, e)
                        sp.dma_start(raw[:, 0:2048].rearrange("p (k i) -> p k i", k=KT),
                                     w1_in[ds(e, 1)].rearrange("o (k p) i -> p (o k) i", p=P)).then_inc(raw_loaded, 16)
                        sp.dma_start(raw[:, 2048:4096].rearrange("p (c d) -> p c d", c=C0),
                                     w2_in[ds(e, 1)].rearrange("o (c p) d -> p (o c) d", p=P)).then_inc(raw_loaded, 16)

                @block.gpsimd
                def _(pool):
                    def low(e, s):
                        pool.wait_ge(whi_ready, e + 1)
                        nc.gpsimd.tensor_tensor(wlo[:, s, :], raw[:, :], whi[:, s, :].bitcast(F32), ALU.subtract
                                                ).then_inc(wlo_ready, 1)
                    nc.gpsimd.memset(gbp[:, :].bitcast(F32), 0.0).then_inc(gbz_ready, 1)
                    expert_low(pool, 1)
                    with pool.Fori(1, NPAIR) as it:
                        for s in range(2):
                            low(2 * it + s, s)

                @block.tensor
                def _(pe):
                    def hidden(item):
                        e, s, c = item
                        if c == 0:
                            pe.wait_ge(wlo_ready, e + 1)
                        for m in range(C0):
                            pe.wait_ge(act_ready, unit(item) + m + 1)
                            n = 0
                            for k in range(KT):
                                for w, a in ((wlo, nhi), (whi, nlo), (whi, nhi)):
                                    at = k * I0 + m * P
                                    last = nc.tensor.matmul(psum[m % 4][:, :], w[:, s, at:at + P],
                                                            a[:, k, c * CH:(c + 1) * CH], start=(n == 0),
                                                            stop=(n == 3 * KT - 1))
                                    n += 1
                            last.then_inc(hid_done, 1)

                    def output(item):
                        e, s, c = item
                        for t in range(TC):
                            pe.wait_ge(acc_ready, tile(item) + t - 2 + 1 + NT)
                            n = 0
                            for m in range(C0):
                                if t == 0:
                                    pe.wait_ge(split_ready, unit(item) + m + 1 + 4)
                                at = 2048 + m * D
                                for h, w in ((hlo, whi), (hhi, wlo), (hhi, whi)):
                                    last = nc.tensor.matmul(psum[4 + t % 2][:, 0:D], h[:, c, m, t * P:(t + 1) * P],
                                                            w[:, s, at:at + D], start=(n == 0),
                                                            stop=(n == 3 * C0 - 1))
                                    n += 1
                            last.then_inc(y_done, 1)

                    def constant(item):
                        e, s, c = item
                        pe.wait_ge(c_read, e + 1)
                        pe.wait_ge(gbe_ready, e + 1)
                        n = 0
                        for m in range(C0):
                            at = 2048 + m * D
                            for w, o_ in ((whi, 0), (wlo, 2 * E0)):
                                o_ += m * 4 * E0
                                last = nc.tensor.matmul(psum[6][0:2 * E0, 0:D], gbe[:, s, o_:o_ + 2 * E0],
                                                        w[:, s, at:at + D], start=(n == 0), stop=(n == 2 * C0 - 1))
                                n += 1
                        last.then_inc(c_done, 1)

                    def body(it, last):
                        for item, nxt in items(it, last):
                            if nxt is not None:
                                hidden(nxt)
                            output(item)
                            if item[2] == 0:
                                constant(item)
                    hidden((0, 0, 0))
                    pe.wait_ge(cnt_ready, 2)
                    nc.tensor.matmul(psum[7][:, 0:2 * E0], ones[:, :], cnt[:, :, :].rearrange("p k e -> p (k e)"),
                                     start=True, stop=True).then_inc(cnt_done, 1)
                    over_pairs(pe, body)

                @block.scalar
                def _(act):
                    act.wait_ge(lm_ready, 1)
                    nc.scalar.activation(lg[:, :, :], lg[:, :, :], ACT.Exp).then_inc(ex_ready, 1)
                    nc.scalar.activation(gb[:, :], b1[:, :], ACT.Gelu).then_inc(gb_ready, 1)
                    expert_high(act, 1)
                    act.sem_inc(act_ready, 4)
                    act.sem_inc(y_done, 2 * TC)

                    def gelu(item):
                        e, s, c = item
                        act.wait_ge(y_done, tile(item) + TC)
                        for m in range(C0):
                            act.wait_ge(hid_done, unit(item) + m + 1)
                            act.wait_ge(split_ready, unit(item) + m + 1)
                            apart(act, turns)
                            nc.scalar.activation(ga[:, m % 4, :], psum[m % 4][:, :], ACT.Gelu,
                                                 bias=b1[:, ds(e * C0 + m, 1)]).then_inc(act_ready, 1)
                            act.wait_ge(act_ready, unit(item) + m + 1 + 4)
                            nc.scalar.activation(hhi[:, c, m, :], ga[:, m % 4, :], ACT.Copy).then_inc(hi_ready, 1)

                    def body(it, last):
                        for item, nxt in items(it, last):
                            e, s, c = item
                            if c == 0:
                                nc.scalar.activation(gbe[:, s, :], gbp[:, ds(e * GB, GB)].bitcast(F32), ACT.Copy
                                                     ).then_inc(gbe_ready, 1)
                            if nxt is not None:
                                gelu(nxt)
                    gelu((0, 0, 0))
                    act.wait_ge(gbs_ready, 3)
                    over_pairs(act, body)

                @block.vector
                def _(dve):
                    dve.sem_inc(split_ready, 4)
                    dve.sem_inc(acc_ready, NT)

                    v = Steps(dve, router_step)

                    def choose():
                        logits = psum[6][:, 0:NT * E0].rearrange("p (t e) -> p t e", e=E0)
                        v(nc.vector.tensor_reduce(t1[:, 0, :], logits, AX.X, ALU.max))
                        v.wait()
                        nc.vector.tensor_tensor(lg[:, :, :], logits, each(t1[:, 0, :], E0), ALU.subtract
                                                ).then_inc(lm_ready, 1)
                        dve.wait_ge(lm_ready, 1)
                        dve.sem_inc(c_read, 1)
                        dve.wait_ge(ex_ready, 1)
                        v(nc.vector.tensor_reduce(t1[:, 1, :], lg[:, :, :], AX.X, ALU.add))
                        v.wait()
                        v(nc.vector.reciprocal(t1[:, 2, :], t1[:, 1, :]))
                        v.wait()
                        v(nc.vector.tensor_tensor(lg[:, :, :], lg[:, :, :], each(t1[:, 2, :], E0), ALU.mult))
                        v.wait()
                        dve.wait_ge(const3, 1)
                        for k in range(2):
                            v(nc.vector.tensor_reduce(t1[:, 3 + k, :], lg[:, :, :], AX.X, ALU.max))
                            v.wait()
                            v(nc.vector.tensor_tensor(t8[:, 0, :, :], lg[:, :, :], each(t1[:, 3 + k, :], E0),
                                                      ALU.is_equal))
                            v.wait()
                            v(nc.vector.tensor_tensor(t8[:, 1, :, :], t8[:, 0, :, :], rows(rev[:, :], NT), ALU.mult))
                            v.wait()
                            v(nc.vector.tensor_reduce(t1[:, 5, :], t8[:, 1, :, :], AX.X, ALU.max))
                            v.wait()
                            v(nc.vector.tensor_tensor(oh[:, k, :, :], t8[:, 1, :, :], each(t1[:, 5, :], E0),
                                                      ALU.is_equal))
                            v.wait()
                            nc.vector.tensor_reduce(cnt[:, k, :], oh[:, k, :, :].rearrange("p t e -> p e t"), AX.X,
                                                    ALU.add).then_inc(cnt_ready, 1)
                            if k == 0:
                                v(nc.vector.scalar_tensor_tensor(lg[:, :, :], oh[:, 0, :, :], -2.0, lg[:, :, :],
                                                                 ALU.mult, ALU.add))
                                v.wait()

                    def weigh():
                        dve.wait_ge(cnt_done, 1)
                        v(nc.vector.tensor_scalar(actv[:, :, :].rearrange("p k e -> p (k e)"), psum[7][:, 0:2 * E0],
                                                  0.5, None, ALU.is_gt))
                        v(nc.vector.tensor_scalar(t1[:, 6:8, :], t1[:, 3:5, :], tg[:, 2:3], None, ALU.mult))
                        v.wait()
                        for k in range(2):
                            w = each(t1[:, 6 + k, :], E0)
                            v(nc.vector.tensor_tensor(t8[:, 2 * k, :, :], oh[:, k, :, :], w, ALU.mult))
                            v(nc.vector.tensor_tensor(t8[:, 2 * k + 1, :, :], rows(actv[:, k, :], NT), oh[:, k, :, :],
                                                      ALU.subtract))
                            v.wait()
                            v(nc.vector.tensor_tensor(t8[:, 2 * k + 1, :, :], t8[:, 2 * k + 1, :, :], w, ALU.mult))
                            v.wait()
                        v(nc.vector.tensor_tensor(wts[:, :, 2, :], t8[:, 0, :, :], t8[:, 2, :, :], ALU.add))
                        for j in range(2):
                            v(nc.vector.tensor_tensor(wts[:, :, j, :], t8[:, 1, :, :], t8[:, 3, :, :], ALU.add))

                    def high(e, s):
                        dve.wait_ge(raw_loaded, 32 * e + 32)
                        nc.vector.tensor_copy(whi[:, s, :], raw[:, :]).then_inc(whi_ready, 1)

                    def split(item):
                        c = item[2]
                        dve.wait_ge(y_done, tile(item) + TC)
                        for m in range(C0):
                            dve.wait_ge(hi_ready, unit(item) + m + 1)
                            nc.vector.tensor_tensor(hlo[:, c, m, :], ga[:, m % 4, :],
                                                    hhi[:, c, m, :].bitcast(F32), ALU.subtract
                                                    ).then_inc(split_ready, 1)

                    def accumulate(item):
                        e, s, c = item
                        for t in range(TC):
                            g = c * TC + t
                            dve.wait_ge(y_done, tile(item) + t + 1 + 2 * TC)
                            dve.wait_ge(acc_ready, tile(item) + t + 1)
                            nc.vector.scalar_tensor_tensor(x[:, g, :], psum[4 + t % 2][:, 0:D],
                                                           wts[:, g, 2, ds(e, 1)], x[:, g, :], ALU.mult, ALU.add
                                                           ).then_inc(acc_ready, 1)

                    def body(it, last):
                        for item, nxt in items(it, last):
                            if nxt is not None:
                                split(nxt)
                            accumulate(item)
                            e, s, c = item
                            if c == 0:
                                dve.wait_ge(c_done, e + 1)
                                dve.wait_ge(c_read, e + 1)
                                nc.vector.tensor_tensor(cst[0:2 * E0, :], cst[0:2 * E0, :], psum[6][0:2 * E0, 0:D],
                                                        ALU.add).then_inc(c_read, 1)
                            if c == 1 and not last:
                                high(e + 2, s)
                    choose()
                    dve.wait_ge(gb_ready, 1)
                    dve.wait_ge(gbz_ready, 1)
                    g3 = gb[:, :].rearrange("p (e m) -> p e m", m=C0)
                    nc.vector.tensor_copy(gbd[:, :, :, 0], g3).then_inc(gbh_ready, 1)
                    nc.vector.tensor_copy(gbd[:, :, :, 2 * E0], g3).then_inc(gbs_ready, 1)
                    dve.wait_ge(gbh_ready, 1)
                    nc.vector.tensor_tensor(gbd[:, :, :, E0], g3, gbd[:, :, :, 0].bitcast(F32), ALU.subtract
                                            ).then_inc(gbs_ready, 2)
                    split((0, 0, 0))
                    weigh()
                    v.wait()
                    over_pairs(dve, body)

        with ExitStack() as s5:
            hn = buf("hn5", [P, NT, D], F32, s5)
            ctxT = buf("ctxT5", [P, KT, T], F32, s5)
            qT = buf("qT5", [P, KT, T], F32, s5)
            watT = buf("watT", [3 * E0, T], F32, s5)
            far = buf("far", [P, S], F32, s5)
            lo_b = buf("lo_b", [P, S], F32, s5)
            far_r = buf("far_r", [P, S], F32R, s5)
            ident_r = buf("ident_r", [P, P], F32R, s5)
            BOUND_STEPS = 6
            kx = buf("kx6", [P, XC, KT, HT, S], F32, s5)
            kx_ready = sem("kx6_ready")
            n5 = Norm(hn, 3, 2)
            ws_loaded, ws_ready, wsh_ready = sem("ws_loaded"), sem("ws_ready"), sem("wsh_ready")
            ld5, dv5, pl5, w_turned, w_copied = sem("ld5"), sem("dve_step5"), sem("pool_step5"), sem("w_turned"), sem("w_copied")
            add_done = sem("add_done")

            with nc.Block() as block:
                @block.sync
                def _(sp):
                    sp.dma_start(ctxT[:, :, :], ctxT_in.rearrange("(k p) t -> p k t", p=P)).then_inc(ld5, 16)
                    for h in range(NS):
                        sp.dma_start(raw[:, h * SN:(h + 1) * SN], ws_in[h]).then_inc(ws_loaded, 16)
                    sp.wait_ge(ld5, 16)

                @block.gpsimd
                def _(pool):
                    g = Steps(pool, pl5)
                    g(nc.gpsimd.memset(far[:, :], 0.0))
                    g(nc.gpsimd.memset(lo_b[:, :], -BIG))
                    g.wait()
                    for h in range(2):
                        for bound, fill in ((far, -FAR), (lo_b, MASKED)):
                            part = bound[h * S:(h + 1) * S, :]
                            g(nc.gpsimd.affine_select(out=part, in_=part, compare_op=ALU.is_ge, fill=fill, base=0,
                                                      pattern=[[-1, S]], channel_multiplier=1))
                            g.wait()
                    assert g.n == BOUND_STEPS
                    n5.power(pool)
                    pool.wait_ge(ld5, 16)
                    for j in range(2):
                        split_keys(pool, ctxT, kx, kx_ready, j, j)

                @block.tensor
                def _(pe):
                    for t in range(NT):
                        last = nc.tensor.transpose(psum[t // TC][0:3 * E0, (t % TC) * P:(t % TC + 1) * P],
                                                   wts[:, t, :, :].rearrange("p j e -> p (j e)"), ident[:, :])
                        if t % TC == TC - 1:
                            last.then_inc(w_turned, 1)
                    for t in range(NT):
                        if t % TC == 0:
                            pe.wait_ge(w_copied, 1 + t // TC)
                        last = nc.tensor.matmul(psum[4 + t // 2][:, (t % 2) * D:(t % 2 + 1) * D],
                                                watT[:, t * P:(t + 1) * P], cst[:, :], start=True, stop=True)
                        last.then_inc(add_done, 1)
                    n5.transpose(pe)

                @block.vector
                def _(dve):
                    v = Steps(dve, dv5)

                    def add(half):
                        for j in range(2 * half, 2 * half + 2):
                            dve.wait_ge(add_done, 2 * j + 2)
                            v(nc.vector.tensor_tensor(x[:, 2 * j:2 * j + 2, :], x[:, 2 * j:2 * j + 2, :],
                                                      psum[4 + j][:, :].rearrange("p (t d) -> p t d", t=2), ALU.add))
                        v.wait()

                    n5.statistics(dve, v, before=add)
                    n5.normalise(dve)

                @block.scalar
                def _(act):
                    nc.scalar.activation(ident_r[:, :], ident[:, :], ACT.Copy)
                    for c in range(NCH):
                        act.wait_ge(w_turned, c + 1)
                        nc.scalar.activation(watT[:, c * CH:(c + 1) * CH], psum[c][0:3 * E0, :], ACT.Copy
                                             ).then_inc(w_copied, 1)
                    act.wait_ge(pl5, BOUND_STEPS)
                    nc.scalar.activation(far_r[:, :], far[:, :], ACT.Copy)
                    for j in range(4):
                        nc.scalar.activation(qT[:, :, 2 * P * j:2 * P * (j + 1)], n5.turned_bank(act, j), ACT.Copy,
                                             scale=QSCALE)
                    for h in range(NS):
                        act.wait_ge(ws_loaded, 16 * NS)
                        nc.scalar.activation(whi[:, h, WN:WN + SN], raw[:, h * SN:(h + 1) * SN], ACT.Copy
                                             ).then_inc(wsh_ready, 1)

            with ExitStack() as s6:
                qs = buf("qs6", [P, XC, KT, S], F32, s6)
                cv = buf("cv6", [P, XC, D], F32, s6)
                vx = buf("vx6", [P, XC, HP, 2 * VC], F32, s6)
                sm = buf("sm6", [P, XR, KT, HT, S], F32, s6)
                mx = buf("mx6", [P, XR, KT, HT], F32, s6)
                pt = buf("pt6", [P, XR, HP, P], F32, s6)
                rc = buf("rc6", [P, XR, NH], F32, s6)
                o = buf("o6", [P, XR, NH, HD], F32, s6)
                cv_in = [sem(f"cv6_in{j}") for j in range(XC)]
                vx_zero, qs_ready, vx_ready = sem("vx6_zero"), sem("qs6_ready"), sem("vx6_ready")
                s_done, s_read, e_ready = sem("s6_done"), sem("s6_read"), sem("e6_ready")
                p_turned, pt_ready, pv_done, o_added = sem("p6_turned"), sem("pt6_ready"), sem("pv6_done"), sem("o6_added")
                mask_step, out_step = sem("mask_step"), sem("out_step")
                NI = B // XC

                with nc.Block() as block:
                    @block.sync
                    def _(sp):
                        with sp.Fori(0, NI) as it:
                            for j in range(XC):
                                sp.wait_ge(vx_ready, 2 * (XC * it + j + 1))
                                src = ctx2_in[ds(XC * it + j, 1)].rearrange("o s d -> (o s) d")
                                for h in range(2):
                                    sp.dma_start(cv[h * S:(h + 1) * S, j, :], src).then_inc(cv_in[j], 16)

                    @block.gpsimd
                    def _(pool):
                        for j in range(2, XC):
                            split_keys(pool, ctxT, kx, kx_ready, j, j)
                        with pool.Fori(1, NI) as it:
                            for j in range(XC):
                                pool.wait_ge(s_done, XC * it + 2 * (j // 2) + 2)
                                split_keys(pool, ctxT, kx, kx_ready, XC * it + j, j)
                        for h in range(NS):
                            pool.wait_ge(wsh_ready, h + 1)
                            nc.gpsimd.tensor_tensor(wlo[:, h, WN:WN + SN], raw[:, h * SN:(h + 1) * SN],
                                                    whi[:, h, WN:WN + SN].bitcast(F32), ALU.subtract
                                                    ).then_inc(ws_ready, 1)

                    @block.tensor
                    def _(pe):
                        pe.sem_inc(s_done, XC)
                        pe.sem_inc(pv_done, XC)

                        def scores(tile, k):
                            n, s = tile
                            if k == 0:
                                pe.wait_ge(kx_ready, KT * (2 * n + 2))
                                pe.wait_ge(qs_ready, 2 * n + 2)
                            pe.wait_ge(s_read, KT * n + k + 1)
                            nc.tensor.matmul(psum[KT * s + k][:, :], ident_r[:, :], rows(far_r[:, :], HT),
                                             start=True, stop=False)
                            for h in range(2):
                                last = nc.tensor.matmul(psum[KT * s + k][h * S:(h + 1) * S, :],
                                                        qs[:, 2 * s + h, k, :],
                                                        kx[:, 2 * s + h, k, :, :].rearrange("p h s -> p (h s)"),
                                                        start=False, stop=True)
                            last.then_inc(s_done, 1)

                        def step(tile, nxt, _):
                            if nxt is not None:
                                scores(nxt, 0)
                            n, s = tile
                            for k in range(KT):
                                pe.wait_ge(e_ready, KT * n + k + 1 + KT * XR)
                                pe.wait_ge(pt_ready, KT * n + k + 1)
                                for q in range(HP // KT):
                                    last = nc.tensor.transpose(psum[4 + k][:, q * P:(q + 1) * P],
                                                               sm[:, s, k, 2 * q:2 * q + 2, :].rearrange(
                                                                   "p h s -> p (h s)"), ident[:, :])
                                last.then_inc(p_turned, 1)
                            for k in range(1, KT):
                                if nxt is not None:
                                    scores(nxt, k)
                            pe.wait_ge(pt_ready, KT * (n + 1) + KT)
                            pe.wait_ge(o_added, n + 1)
                            pe.wait_ge(vx_ready, 2 * (2 * n + 2) + 2 * XC)
                            for hp in range(HP):
                                for h in range(2):
                                    last = nc.tensor.matmul(
                                        psum[6 + s][h * S:(h + 1) * S, hp * 2 * VC:(hp + 1) * 2 * VC],
                                        pt[:, s, hp, h * S:(h + 1) * S], vx[:, 2 * s + h, hp, :],
                                        start=True, stop=True)
                                    if hp == HP - 1:
                                        last.then_inc(pv_done, 1)

                        for k in range(KT):
                            scores((0, 0), k)
                        over_tiles(pe, step)

                    @block.vector
                    def _(dve):
                        dve.sem_inc(s_read, KT * XR)
                        dve.sem_inc(o_added, XR)
                        v = Steps(dve, vx_zero)
                        v(nc.vector.memset(vx[:, :, :, :], 0.0))
                        v.wait()
                        for h in range(2):
                            v(nc.vector.memset(vx[h * S:(h + 1) * S, :, :, h * VC + HD:h * VC + HD + 1], 1.0))

                        def masked(tile):
                            n, s = tile
                            v = Steps(dve, mask_step, n * 2 * KT)
                            dve.wait_ge(p_turned, KT * (n + 1))
                            for k in range(KT):
                                dve.wait_ge(s_done, 2 * n + k + 1 + XC)
                                bank = psum[KT * s + k][:, :].rearrange("p (h s) -> p h s", s=S)
                                part = sm[:, s, k, :, :]
                                nc.vector.tensor_tensor(part, bank, rows(lo_b[:, :], HT), ALU.max
                                                        ).then_inc(s_read, 1)
                                dve.wait_ge(s_read, KT * n + k + 1 + KT * XR)
                                v(nc.vector.tensor_reduce(mx[:, s, k, :], part, AX.X, ALU.max))
                                v.wait()
                                v(nc.vector.tensor_tensor(part, part, each(mx[:, s, k, :], S), ALU.subtract))

                        def step(tile, nxt, _):
                            if nxt is not None:
                                masked(nxt)
                            n, s = tile
                            v = Steps(dve, out_step, n * 2)
                            dve.wait_ge(pv_done, 2 * n + 2 + XC)
                            dve.wait_ge(o_added, n + XR)
                            heads = psum[6 + s][:, 0:HP * 2 * VC].rearrange("p (h c) -> p h c", c=VC)
                            v(nc.vector.reciprocal(rc[:, s, :], heads[:, :, HD]))
                            v.wait()
                            v(nc.vector.tensor_tensor(o[:, s, :, :], heads[:, :, 0:HD], each(rc[:, s, :], HD),
                                                      ALU.mult))
                            v.wait()
                            rows_x = x[:, ds(n, 1), :].rearrange("p o d -> p (o d)")
                            nc.vector.tensor_tensor(rows_x, rows_x, o[:, s, :, :].rearrange("p h d -> p (h d)"),
                                                    ALU.add).then_inc(o_added, 1)

                        masked((0, 0))
                        over_tiles(dve, step)

                    @block.scalar
                    def _(act):
                        act.sem_inc(e_ready, KT * XR)
                        act.sem_inc(pt_ready, KT)
                        act.sem_inc(p_turned, KT * XR)
                        act.sem_inc(vx_ready, 2 * XC)

                        def queries(tile):
                            n, s = tile
                            for h in range(2):
                                j = 2 * s + h
                                act.wait_ge(s_done, 2 * n + 2)
                                apart(act, turns)
                                nc.scalar.activation(qs[:, j, :, :], qT[:, :, ds((2 * n + h) * S, S)], ACT.Copy
                                                     ).then_inc(qs_ready, 1)

                        def values(tile):
                            n, s = tile
                            for g in range(2):
                                j = 2 * s + g
                                act.wait_ge(cv_in[j], 32 * ((n - s) // XR) + 32 if isinstance(n, int)
                                            else (n - s) * (32 // XR) + 32)
                                act.wait_ge(pv_done, 2 * n + g + 1)
                                for h in range(2):
                                    r = slice(h * S, (h + 1) * S)
                                    nc.scalar.activation(
                                        vx[r, j, :, h * VC:h * VC + HD],
                                        cv[r, j, :].rearrange("p (q h d) -> p q h d", h=2, d=HD)[:, :, h, :],
                                        ACT.Identity, scale=tg[r, 1:2]).then_inc(vx_ready, 1)

                        def exponentials(tile):
                            n, s = tile
                            for k in range(KT):
                                act.wait_ge(mask_step, 2 * (KT * n + k) + 2)
                                part = sm[:, s, k, :, :]
                                nc.scalar.activation(part, part, ACT.Exp).then_inc(e_ready, 1)

                        def step(tile, nxt, after):
                            n, s = tile
                            for k in range(KT):
                                act.wait_ge(p_turned, KT * n + k + 1 + KT * XR)
                                if k == 0:
                                    act.wait_ge(pv_done, 2 * n + 2)
                                nc.scalar.activation(pt[:, s, k * 4:k * 4 + 4, :].rearrange("p q t -> p (q t)"),
                                                     psum[4 + k][:, :], ACT.Copy).then_inc(pt_ready, 1)
                            if after is not None:
                                queries(after)
                                values(after)
                            if nxt is not None:
                                exponentials(nxt)

                        queries((0, 0))
                        queries((1, 1))
                        nc.scalar.preload_act_table(ACT.Exp)
                        act.wait_ge(vx_zero, 3)
                        values((0, 0))
                        values((1, 1))
                        exponentials((0, 0))
                        over_tiles(act, step)

        with ExitStack() as s7:
            hT = buf("hT7", [P, KT, T], F32, s7)
            wT = buf("wT", [4 * K1, G1, T], F32R, s7)
            scal = buf("scal", [P, NT, G1], F32, s7)
            selw = buf("selw", [4 * K1, P], F32R, s7)
            s1c = buf("s1c", [4 * K1, 2], F32, s7)
            scb = buf("scb", [P, NSC], F32, s7)
            mur = buf("mur", [MS, D], F32, s7)
            mus = buf("mus", [MS, 2, D], F32R, s7)
            muh = buf("muh", [MS, D], F32R, s7)
            mul_ = buf("mul", [MS, 2, D], F32, s7)
            w_loaded, scaled_ready, wh_ready = sem("w7_loaded"), sem("scaled_ready"), sem("wh_ready")
            mus_ready, prep_ready, prep_step = sem("mus_ready"), sem("prep_ready"), sem("prep_step")
            s1c_ready, turns_pool = sem("s1c_ready"), sem("turns_pool")
            WPARTS = ((0, WD), (WD, WN))
            PREP = 6

            def load_group(sp, g):
                sp.dma_start(raw[:, 0:WN], wf_in[ds(g, 1)].rearrange("o p c -> (o p) c")).then_inc(w_loaded, 16)
                for h in range(2):
                    sp.dma_start(scb[h * S:(h + 1) * S, :], sc_in[ds(g, 1), h, :].broadcast_to([S, NSC])
                                 ).then_inc(w_loaded, 16)
                sp.dma_start(mur[:, :], mu_in[ds(g, 1)].rearrange("o r d -> (o r) d")
                             ).then_inc(w_loaded, 16)

            def scale(pool, g):
                g_ = Steps(pool, prep_step, g * PREP)
                pool.wait_ge(w_loaded, 64 * g + 64)
                g_(nc.gpsimd.tensor_tensor(raw[:, WL:WD], raw[:, WL:WD], scb[:, 0:3 * P], ALU.mult))
                g_.wait()
                dn = raw[S:P, WD + D:WD + 2 * D]
                nc.gpsimd.tensor_tensor(dn, dn, scb[S:P, 3 * P:NSC], ALU.mult).then_inc(scaled_ready, 1)
                pool.wait_ge(scaled_ready, g + 1)

            def stack_mixing(pool, g, s):
                g_ = Steps(pool, prep_step, g * PREP + 1)
                apart(pool, turns_pool)
                g_(nc.gpsimd.tensor_copy(muh[:, :], mur[:, :]))
                g_.wait()
                g_(nc.gpsimd.tensor_tensor(mul_[:, 0, :], mur[:, :], muh[:, :].bitcast(F32), ALU.subtract))
                g_.wait()
                apart(pool, turns_pool)
                g_(nc.gpsimd.tensor_scalar(mul_[:, 0, :], mul_[:, 0, :], s1c[0:MS, 1:2], None, ALU.mult))
                g_(nc.gpsimd.tensor_scalar(mul_[:, 1, :], muh[:, :].bitcast(F32), s1c[0:MS, 0:1], None, ALU.mult))
                g_.wait()
                nc.gpsimd.tensor_tensor(mus[:, s, :], mul_[:, 0, :], mul_[:, 1, :], ALU.add
                                        ).then_inc(mus_ready, 1)
                pool.wait_ge(mus_ready, g + 1)

            def low_part(pool, g, s, part):
                a, b = WPARTS[part]
                pool.wait_ge(wh_ready, 2 * g + part + 1)
                to = prep_ready if part == 1 else prep_step
                nc.gpsimd.tensor_tensor(wlo[:, s, a:b], raw[:, a:b], whi[:, s, a:b].bitcast(F32), ALU.subtract
                                        ).then_inc(to, 1)

            def high_part(s, part):
                a, b = WPARTS[part]
                nc.scalar.activation(whi[:, s, a:b], raw[:, a:b], ACT.Copy).then_inc(wh_ready, 1)

            with ExitStack() as s7a:
                hn = buf("hn7", [P, NT, D], F32, s7a)
                gw = buf("gw", [P, KT, E1], F32, s7a)
                invb = buf("invb", [E1, E1], I32, s7a)
                invf = buf("invf", [E1, 2, E1], F32, s7a)
                eidx = buf("eidx", [E1, 1], F32, s7a)
                sel = buf("sel", [E1, E1], F32, s7a)
                pre = buf("pre", [P, NT, E1 + 8 - TOP1], F32, s7a)
                rep = buf("rep", [P, NT, E1 + 8 - TOP1], F32, s7a)
                pr = pre[:, :, 0:E1]
                big = buf("big", [P, 2, NT, E1], F32, s7a)
                top = buf("top", [P, NT, 8], F32, s7a)
                t1 = buf("t17", [P, 4, NT], F32, s7a)
                tg8 = buf("tg8", [P, 3, NT, G1], F32, s7a)
                wdT = buf("wdT", [E1, T], F32, s7a)
                wst = buf("wst", [P, NT, G1, 32], F32R, s7a)
                jk = buf("jk", [4 * K1, P], F32, s7a)
                pi = buf("pi", [4 * K1, 4], I32, s7a)
                pf = buf("pf", [4 * K1, 3], F32, s7a)
                n7 = Norm(hn, 4, 3)
                nlo_ready = sem("nlo7_ready")
                ld7, iota_ready, pl7, dv7 = sem("ld7"), sem("iota_ready"), sem("pool_step7"), sem("dve_step7")
                v7 = Steps(nc.vector, dv7)
                hT_ready, g_done, lm_ready, ex_ready = sem("h7_ready"), sem("g7_done"), sem("lm7_ready"), sem("ex7_ready")
                wd_ready, wd_turned, wdT_ready, f_done = sem("wd_ready"), sem("wd_turned"), sem("wdT_ready"), sem("f_done")
                z_ready, ez_ready, st_ready = sem("z_ready"), sem("ez_ready"), sem("st_ready")
                st_turned, hi_ready, nhi_ready = sem("st_turned"), sem("hi7_ready"), sem("nhi7_ready")

                with nc.Block() as block:
                    @block.sync
                    def _(sp):
                        sp.dma_start(gw[:, :, :], gw_in.rearrange("(k p) e -> p k e", p=P)).then_inc(ld7, 16)
                        sp.dma_start(invb[:, :], inv_in.partition_broadcast(E1)).then_inc(ld7, 16)
                        load_group(sp, 0)

                    @block.gpsimd
                    def _(pool):
                        g = Steps(pool, pl7)
                        exact = dict(allow_small_or_imprecise_dtypes=True)
                        g(nc.gpsimd.iota(eidx[:, :], pattern=[[0, 1]], base=0, channel_multiplier=1, **exact))
                        g(nc.gpsimd.iota(pi[:, 0:1], pattern=[[0, 1]], base=0, channel_multiplier=1))
                        g(nc.gpsimd.iota(jk[:, :], pattern=[[0, 2], [1, K1], [0, R1]], base=0, channel_multiplier=0,
                                         **exact))
                        g.wait()
                        g(nc.gpsimd.memset(pre[:, :, E1:], 2.0))
                        g(nc.gpsimd.memset(wst[:, :, :, 3 * K1:4 * K1].bitcast(F32), 0.0))
                        g.wait()
                        pool.sem_inc(iota_ready, 1)
                        n7.power(pool)
                    @block.tensor
                    def _(pe):
                        n7.transpose(pe)
                        pe.wait_ge(ld7, 32)
                        for t in range(NT):
                            if t % 2 == 0:
                                pe.wait_ge(hT_ready, t // 2 + 1)
                            for k in range(KT):
                                last = nc.tensor.matmul(psum[0][:, t * E1:(t + 1) * E1], hT[:, k, t * P:(t + 1) * P],
                                                        gw[:, k, :], start=(k == 0), stop=(k == KT - 1))
                        last.then_inc(g_done, 1)

                    @block.vector
                    def _(dve):
                        v = v7
                        n7.statistics(dve, v)
                        n7.normalise(dve)
                        dve.wait_ge(iota_ready, 1)
                        v(nc.vector.tensor_scalar(pi[:, 1:2], pi[:, 0:1], 7, None, ALU.bitwise_and))
                        v(nc.vector.tensor_scalar(pi[:, 2:3], pi[:, 0:1], 24, None, ALU.bitwise_and))
                        v.wait()
                        v(nc.vector.tensor_copy(pf[:, 0:2], pi[:, 1:3]))
                        v.wait()
                        v(nc.vector.tensor_scalar(s1c[:, 1:2], pf[:, 1:2], 8.0, None, ALU.is_equal))
                        v.wait()
                        nc.vector.tensor_scalar(s1c[:, 0:1], s1c[:, 1:2], -1.0, 1.0, ALU.mult, ALU.add
                                                ).then_inc(s1c_ready, 1)
                        dve.wait_ge(s1c_ready, 1)
                        v(nc.vector.tensor_scalar(selw[:, :], jk[:, :], pf[:, 0:1], s1c[:, 0:1], ALU.is_equal,
                                                  ALU.mult))
                        dve.wait_ge(ld7, 32)
                        v(nc.vector.tensor_copy(invf[:, 0, :], invb[:, :]))
                        v.wait()
                        v(nc.vector.tensor_scalar(invf[:, 1, :], invf[:, 0, :], 0.0, float(E1), ALU.is_lt, ALU.mult))
                        v.wait()
                        v(nc.vector.tensor_tensor(invf[:, 0, :], invf[:, 0, :], invf[:, 1, :], ALU.add))
                        v.wait()
                        v(nc.vector.tensor_scalar(sel[:, :], invf[:, 0, :], eidx[:, 0:1], None, ALU.is_equal))
                        for k in range(KT):
                            dve.wait_ge(nhi_ready, k + 1)
                            nc.vector.tensor_tensor(nlo[:, k, :], hT[:, k, :], nhi[:, k, :].bitcast(F32),
                                                    ALU.subtract).then_inc(nlo_ready, 1)

                    @block.scalar
                    def _(act):
                        for j in range(4):
                            nc.scalar.activation(hT[:, :, 2 * P * j:2 * P * (j + 1)], n7.turned_bank(act, j),
                                                 ACT.Copy).then_inc(hT_ready, 1)
                        act.wait_ge(hT_ready, 4)
                        for k in range(KT):
                            nc.scalar.activation(nhi[:, k, :], hT[:, k, :], ACT.Copy).then_inc(nhi_ready, 1)

                s_t, s_sg, s_hf, s_hi = sem("s_t_done"), sem("s_sg_ready"), sem("s_hf_ready"), sem("s_hi_ready")
                s_lo, s_dn, s_acc = sem("s_lo_ready"), sem("s_dn_done"), sem("s_acc_ready")
                spent = hn[:, :, :].rearrange("p (b j u) d -> p b j (u d)", b=2, j=2)
                sg = spent[:, 0]
                hf = spent[:, 1]
                hhi = buf("hhi7", [P, 2, 2, CH], F32R, s7a)
                hlo = buf("hlo7", [P, 2, 2, CH], F32R, s7a)
                ITEMS = NS * NCH
                UNITS = (P, IB)
                S_BANKS = (3, 7, 1, 2)
                ST_BANKS = (0, 4, 5, 6)

                with nc.Block() as block:
                    @block.sync
                    def _(sp):
                        sp.wait_ge(prep_ready, 1)
                        load_group(sp, 1)

                    @block.gpsimd
                    def _(pool):
                        scale(pool, 0)
                        stack_mixing(pool, 0, 0)
                        for part in range(2):
                            low_part(pool, 0, 0, part)
                        scale(pool, 1)
                        stack_mixing(pool, 1, 1)

                    @block.tensor
                    def _(pe):
                        def product(bank, n_terms, operands):
                            for n, (a, b) in enumerate(operands):
                                last = nc.tensor.matmul(bank, a, b, start=(n == 0), stop=(n == n_terms - 1))
                            return last

                        def hidden(q):
                            h, c = q // NCH, q % NCH
                            if q:
                                pe.wait_ge(s_sg, 2 * q)
                                pe.wait_ge(s_hf, 2 * q)
                            cols = slice(c * CH, (c + 1) * CH)
                            for j in range(3):
                                ops = []
                                for k in range(KT):
                                    at = WN + (k * 3 + j) * P
                                    ops += [(w[:, h, at:at + P], a[:, k, cols])
                                            for w, a in ((wlo, nhi), (whi, nlo), (whi, nhi))]
                                product(psum[4 + j][:, :], 3 * KT, ops).then_inc(s_t, 1)

                        def down(q):
                            h = q // NCH
                            pe.wait_ge(s_lo, 2 * q + 2)
                            for t in range(TC):
                                if q:
                                    pe.wait_ge(s_acc, TC * (q - 1) + t + 1)
                                tok = slice(t * P, (t + 1) * P)
                                ops = []
                                for m, r in enumerate(UNITS):
                                    at = WN + SD + m * D
                                    ops += [(a[0:r, q % 2, m, tok], w[0:r, h, at:at + D])
                                            for a, w in ((hlo, whi), (hhi, wlo), (hhi, whi))]
                                product(psum[S_BANKS[t]][:, 0:D], 6, ops).then_inc(s_dn, 1)

                        def by_place(c):
                            pe.wait_ge(wd_ready, c + 1)
                            for t in range(TC):
                                last = nc.tensor.transpose(psum[1 + c][0:E1, t * P:(t + 1) * P],
                                                           pr[:, c * TC + t, :], ident[:, :])
                            last.then_inc(wd_turned, 1)
                            pe.wait_ge(wdT_ready, c + 1)
                            for t in range(TC):
                                at = (c * TC + t) * P
                                last = nc.tensor.matmul(psum[7 * c][:, t * E1:(t + 1) * E1],
                                                        wdT[:, at:at + P], sel[:, :], start=True, stop=True)
                            last.then_inc(f_done, 1)

                        hidden(0)
                        by_place(0)
                        by_place(1)
                        hidden(1)
                        pe.wait_ge(z_ready, 2)
                        down(0)
                        hidden(2)
                        down(1)
                        hidden(3)
                        down(2)
                        pe.wait_ge(st_ready, 2 * NCH)
                        pe.wait_ge(s_hf, 2 * ITEMS)
                        for q in range(2):
                            for c in range(NCH):
                                for t in range(TC):
                                    last = nc.tensor.transpose(psum[ST_BANKS[q * NCH + c]][:, t * P:(t + 1) * P],
                                                               wst[:, c * TC + t, 4 * q:4 * q + 4, :].bitcast(F32
                                                                   ).rearrange("p g k -> p (g k)"), ident[:, :])
                                last.then_inc(st_turned, 1)
                        down(3)

                    @block.vector
                    def _(dve):
                        v = v7

                        def split(q):
                            if q > 1:
                                dve.wait_ge(s_dn, TC * (q - 1))
                            for m, r in enumerate(UNITS):
                                dve.wait_ge(s_t, 3 * q + 2 + m)
                                dve.wait_ge(s_sg, 2 * q + m + 1)
                                if q:
                                    dve.wait_ge(s_lo, 2 * q)
                                up = psum[5 + m][m * UB:m * UB + r, :]
                                nc.vector.tensor_tensor(hf[0:r, m, :], sg[0:r, m, :], up, ALU.mult
                                                        ).then_inc(s_hf, 1)
                            for m, r in enumerate(UNITS):
                                dve.wait_ge(s_hi, 2 * q + m + 1)
                                nc.vector.tensor_tensor(hlo[0:r, q % 2, m, :], hf[0:r, m, :],
                                                        hhi[0:r, q % 2, m, :].bitcast(F32), ALU.subtract
                                                        ).then_inc(s_lo, 1)

                        def accumulate(q):
                            for t in range(TC):
                                g = (q % NCH) * TC + t
                                dve.wait_ge(s_dn, TC * q + t + 1)
                                if q >= NCH:
                                    dve.wait_ge(s_acc, TC * (q - NCH) + t + 1)
                                nc.vector.scalar_tensor_tensor(x[:, g, :], psum[S_BANKS[t]][:, 0:D],
                                                               tg[:, 3:4], x[:, g, :], ALU.mult, ALU.add
                                                               ).then_inc(s_acc, 1)

                        logits = psum[0][:, :].rearrange("p (t e) -> p t e", e=E1)
                        halves = [slice(c * TC, (c + 1) * TC) for c in range(NCH)]
                        for h in halves:
                            v(nc.vector.tensor_reduce(t1[:, 0, h], logits[:, h, :], AX.X, ALU.max))
                            v.wait()
                            nc.vector.tensor_tensor(pr[:, h, :], logits[:, h, :], each(t1[:, 0, h], E1), ALU.subtract
                                                    ).then_inc(lm_ready, 1)
                        for c, h in enumerate(halves):
                            dve.wait_ge(ex_ready, c + 1)
                            v(nc.vector.tensor_reduce(t1[:, 1, h], pr[:, h, :], AX.X, ALU.add))
                            v.wait()
                            v(nc.vector.reciprocal(t1[:, 2, h], t1[:, 1, h]))
                            v.wait()
                            v(nc.vector.tensor_tensor(pr[:, h, :], pr[:, h, :], each(t1[:, 2, h], E1), ALU.mult))
                            v.wait()
                            for t in range(h.start, h.stop):
                                v(nc.vector.max(top[:, t, :], pre[:, t, :]))
                            v.wait()
                            for t in range(h.start, h.stop):
                                v(nc.vector.match_replace(rep[:, t, :], top[:, t, :], pre[:, t, :], -1.0))
                            v.wait()
                            nc.vector.scalar_tensor_tensor(pr[:, h, :], rep[:, h, 0:E1], 0.0, pr[:, h, :], ALU.is_lt,
                                                           ALU.mult).then_inc(wd_ready, 1)
                        split(0)

                        def views(h):
                            flat, z = big[:, 0, h, :], big[:, 1, h, :]
                            f3, z3 = (a.rearrange("p t (g k) -> p t g k", k=K1) for a in (flat, z))
                            return flat, z, f3, z3, z.rearrange("p t (g k) -> p (t g) k", k=K1)

                        for c, h in enumerate(halves):
                            flat, z, f3, z3, zg = views(h)
                            dve.wait_ge(f_done, c + 1)
                            v(nc.vector.tensor_copy(flat, psum[7 * c][:, 0:TC * E1].rearrange(
                                "p (t e) -> p t e", e=E1)))
                            v.wait()
                            v(nc.vector.tensor_reduce(tg8[:, 0, h, :], f3, AX.X, ALU.add))
                            v(nc.vector.tensor_scalar(z, flat, 0.0, -1.0e9, ALU.is_equal, ALU.mult))
                            v.wait()
                            v(nc.vector.tensor_scalar(scal[:, h, 0:G1], tg8[:, 0, h, :], tg[:, 3:4], None, ALU.mult))
                            v(nc.vector.tensor_tensor(z, z, flat, ALU.add))
                            v.wait()
                            v(nc.vector.tensor_reduce(tg8[:, 1, h, :], z3, AX.X, ALU.max))
                            v.wait()
                            nc.vector.tensor_tensor(zg, zg, each(tg8[:, 1, h, :].rearrange("p t g -> p (t g)"), K1),
                                                    ALU.subtract).then_inc(z_ready, 1)
                        split(1)
                        accumulate(0)
                        for c, h in enumerate(halves):
                            flat, z, f3, z3, zg = views(h)
                            dve.wait_ge(ez_ready, c + 1)
                            v(nc.vector.tensor_reduce(tg8[:, 2, h, :], z3, AX.X, ALU.add))
                            v.wait()
                            v(nc.vector.reciprocal(tg8[:, 0, h, :], tg8[:, 2, h, :]))
                            v.wait()
                            v(nc.vector.tensor_tensor(zg, zg, each(tg8[:, 0, h, :].rearrange("p t g -> p (t g)"), K1),
                                                      ALU.mult))
                            v.wait()
                            nc.vector.tensor_copy(wst[:, h, :, 0:K1], z3).then_inc(hi_ready, 1)
                            dve.wait_ge(hi_ready, c + 1)
                            nc.vector.tensor_tensor(wst[:, h, :, 2 * K1:3 * K1], z3,
                                                    wst[:, h, :, 0:K1].bitcast(F32), ALU.subtract
                                                    ).then_inc(st_ready, 1)
                        split(2)
                        accumulate(1)
                        split(3)
                        accumulate(2)
                        dve.wait_ge(st_turned, 2)
                        for g in range(4):
                            nc.vector.tensor_copy(wT[:, g, CH:2 * CH],
                                                  psum[ST_BANKS[1]][g * 4 * K1:(g + 1) * 4 * K1, :])
                        accumulate(3)

                    @block.scalar
                    def _(act):
                        def silu(q):
                            if q:
                                act.wait_ge(s_hf, 2 * q)
                            act.wait_ge(s_t, 3 * q + 1)
                            nc.scalar.activation(sg[:, 0, :], psum[4][:, :], ACT.Silu).then_inc(s_sg, 1)
                            act.wait_ge(s_t, 3 * q + 3)
                            nc.scalar.activation(sg[0:IB, 1, :], psum[6][0:IB, :], ACT.Silu).then_inc(s_sg, 1)

                        def high(q):
                            for m, r in enumerate(UNITS):
                                act.wait_ge(s_hf, 2 * q + m + 1)
                                nc.scalar.activation(hhi[0:r, q % 2, m, :], hf[0:r, m, :], ACT.Copy
                                                     ).then_inc(s_hi, 1)

                        halves = [slice(c * TC, (c + 1) * TC) for c in range(NCH)]
                        for c, h in enumerate(halves):
                            act.wait_ge(lm_ready, c + 1)
                            nc.scalar.activation(pr[:, h, :], pr[:, h, :], ACT.Exp).then_inc(ex_ready, 1)
                        silu(0)
                        for c in range(NCH):
                            act.wait_ge(wd_turned, c + 1)
                            nc.scalar.activation(wdT[:, c * CH:(c + 1) * CH], psum[1 + c][0:E1, :], ACT.Copy
                                                 ).then_inc(wdT_ready, 1)
                        high(0)
                        silu(1)
                        for c, h in enumerate(halves):
                            act.wait_ge(z_ready, c + 1)
                            nc.scalar.activation(big[:, 1, h, :], big[:, 1, h, :], ACT.Exp).then_inc(ez_ready, 1)
                        high(1)
                        act.wait_ge(scaled_ready, 1)
                        high_part(0, 0)
                        high_part(0, 1)
                        for c, h in enumerate(halves):
                            act.wait_ge(hi_ready, c + 1)
                            nc.scalar.activation(wst[:, h, :, K1:2 * K1], wst[:, h, :, 0:K1].bitcast(F32), ACT.Copy
                                                 ).then_inc(st_ready, 1)
                        silu(2)
                        high(2)
                        silu(3)
                        high(3)
                        for n in (0, 2, 3):
                            act.wait_ge(st_turned, n + 1)
                            for g in range(4):
                                nc.scalar.activation(wT[:, n // NCH * 4 + g, (n % NCH) * CH:(n % NCH + 1) * CH],
                                                     psum[ST_BANKS[n]][g * 4 * K1:(g + 1) * 4 * K1, :], ACT.Copy)

            with ExitStack() as s8:
                xef = buf("xef", [P, KT, CH], F32, s8)
                xhi = buf("xhi", [P, NCH, KT, CH], F32R, s8)
                xlo = buf("xlo", [P, NCH, KT, CH], F32R, s8)
                we = buf("we", [P, NCH, CH], F32, s8)
                spare = raw[:, WN:WN + 3 * CH].rearrange("p (j c) -> p j c", j=3)
                waf = spare[:, 0, :]
                wahi = buf("wahi", [P, CH], F32R, s8)
                walo = buf("walo", [P, CH], F32R, s8)
                sg0 = spare[:, 1, :]
                sg1 = buf("sg1", [IB, CH], F32, s8)
                h0f = spare[:, 2, :]
                h1f = buf("h1f", [P, CH], F32, s8)
                h0hi = buf("h0hi", [P, NCH, CH], F32R, s8)
                h0lo = buf("h0lo", [P, NCH, CH], F32R, s8)
                h1hi = buf("h1hi", [P, NCH, CH], F32R, s8)
                h1lo = buf("h1lo", [P, NCH, CH], F32R, s8)
                names = ("mu_done qa_done we_done dq_done t_done dn_done we_ready wahi_ready xhi_ready sg_ready "
                         "hhi_ready wadhi_ready xef_ready xlo_ready waf_ready walo_ready wadf_ready wadlo_ready "
                         "hf_ready hlo_ready acc_ready zero_ready turns_pe")
                q8 = {n: sem("m_" + n) for n in names.split()}
                out_written = sem("out_written")
                DOWN_BANKS = (7, 3, 0, 1)

                def wait(engine, name, value):
                    if not isinstance(value, int) or value > 0:
                        engine.wait_ge(q8[name], value)

                def item_of(g, s, c):
                    return dict(g=g, s=s, c=c, n=g * NCH + c)

                def pair(it, first=False, last=False):
                    seq = [item_of(2 * it + s, s, c) for s in range(2) for c in range(NCH)]
                    before = None if first else item_of(2 * it - 1, 1, NCH - 1)
                    after = None if last else item_of(2 * it + 2, 0, 0)
                    return list(zip([before] + seq[:-1], seq, seq[1:] + [after]))

                def over_items(engine, body):
                    for p, i, n in pair(0, first=True):
                        body(p, i, n)
                    with engine.Fori(1, G1 // 2 - 1) as it:
                        for p, i, n in pair(it):
                            body(p, i, n)
                    for p, i, n in pair(G1 // 2 - 1, last=True):
                        body(p, i, n)
                    body(item_of(G1 - 1, 1, NCH - 1), None, None)

                def cols(i):
                    return slice(i["c"] * CH, (i["c"] + 1) * CH)

                with nc.Block() as block:
                    @block.sync
                    def _(sp):
                        with sp.Fori(2, G1) as g:
                            sp.wait_ge(prep_ready, g)
                            load_group(sp, g)
                        for c in range(NCH):
                            for t in range(TC):
                                wait(sp, "acc_ready", TC * (G1 * NCH - NCH + c) + t + 1)
                                sp.dma_start(out.rearrange("(t p) d -> p t d", p=P)[:, c * TC + t, :],
                                             x[:, c * TC + t, :]).then_inc(out_written, 16)
                        sp.wait_ge(out_written, NT * 16)

                    @block.gpsimd
                    def _(pool):
                        for n, rest in enumerate((h1hi, h1lo)):
                            nc.gpsimd.memset(rest[32:UB, :, :].bitcast(F32), 0.0).then_inc(q8["zero_ready"], 1)
                            pool.wait_ge(q8["zero_ready"], n + 1)

                        for part in range(2):
                            low_part(pool, 1, 1, part)
                        with pool.Fori(1, G1 // 2) as it:
                            for s in range(2):
                                g = 2 * it + s
                                scale(pool, g)
                                wait(pool, "mu_done", (g - 1) * NCH * KT)
                                stack_mixing(pool, g, s)
                                for part in range(2):
                                    low_part(pool, g, s, part)

                    @block.tensor
                    def _(pe):
                        def split_product(bank, terms, first, last):
                            n = 0
                            for w, a in terms:
                                for i, j in ((1, 0), (0, 1), (0, 0)):
                                    done = nc.tensor.matmul(bank, w[i], a[j], start=first and n == 0,
                                                            stop=last and n == 3 * len(terms) - 1)
                                    n += 1
                            return done

                        def weights(s, a, b, r=slice(0, P)):
                            return whi[r, s, a:b], wlo[r, s, a:b]

                        def mixed(i):
                            pe.wait_ge(mus_ready, i["g"] + 1)
                            wait(pe, "xef_ready", KT * i["n"])
                            apart(pe, q8["turns_pe"])
                            for k in range(KT):
                                nc.tensor.matmul(psum[k][:, :], mus[:, i["s"], k * P:(k + 1) * P],
                                                 wT[0:MS, ds(i["g"], 1), cols(i)].rearrange("r o t -> r (o t)"),
                                                 start=True, stop=True).then_inc(q8["mu_done"], 1)

                        def stream(i, j, src):
                            terms = [(weights(i["s"], k * 512 + j * P, k * 512 + (j + 1) * P),
                                      (src[0][:, k, :], src[1][:, k, :])) for k in range(KT)]
                            split_product(psum[4 + j][:, :], terms, True, False)

                        def body(prev, i, nxt):
                            if i is not None:
                                s, c, n = i["s"], i["c"], i["n"]
                                src = (xhi[:, c], xlo[:, c])
                                pe.wait_ge(prep_ready, i["g"] + 1)
                            if i is not None:
                                wait(pe, "xlo_ready", KT * (n + 1))
                                wait(pe, "waf_ready", n)
                                terms = [(weights(s, k * 512 + 384, k * 512 + 512), (src[0][:, k, :], src[1][:, k, :]))
                                         for k in range(KT)]
                                split_product(psum[2][:, :], terms, True, True).then_inc(q8["qa_done"], 1)
                                wait(pe, "acc_ready", TC * (n - 1))
                                apart(pe, q8["turns_pe"])
                                nc.tensor.matmul(psum[3][:, :], selw[0:MS, :],
                                                 wT[0:MS, ds(i["g"], 1), cols(i)].rearrange("r o t -> r (o t)"),
                                                 start=True, stop=True).then_inc(q8["we_done"], 1)
                            if nxt is not None:
                                mixed(nxt)
                            if i is not None:
                                wait(pe, "sg_ready", 2 * n)
                                wait(pe, "hf_ready", 2 * n)
                                stream(i, 0, src)
                                stream(i, 1, src)
                            if prev is not None:
                                wait(pe, "hlo_ready", 2 * prev["n"] + 2)
                                if i is None:
                                    wait(pe, "acc_ready", TC * prev["n"])
                                sp_, cp = prev["s"], prev["c"]
                                terms = [(weights(sp_, WA, WA + P), (h0hi[:, cp, :], h0lo[:, cp, :])),
                                         (weights(sp_, WA + P, WA + 2 * P, slice(0, IB)),
                                          (h1hi[0:IB, cp, :], h1lo[0:IB, cp, :]))]
                                split_product(psum[7][:, :], terms, True, True).then_inc(q8["dq_done"], 1)
                            if i is not None:
                                stream(i, 2, src)
                            if i is not None:
                                wait(pe, "walo_ready", n + 1)
                                for f, (w, a) in enumerate(((wlo, wahi), (whi, walo), (whi, wahi))):
                                    for j in range(2):
                                        r, at = slice(j * KR, (j + 1) * KR), WL + j * P
                                        last = nc.tensor.matmul(psum[4 + j][:, :], w[r, s, at:at + P], a[r, :],
                                                                start=False, stop=(f == 2))
                                        if f == 2:
                                            last.then_inc(q8["t_done"], 1)
                                split_product(psum[6][:, :], [(weights(s, WL + 2 * P, WD), (wahi[:, :], walo[:, :]))],
                                              False, True).then_inc(q8["t_done"], 1)
                            if prev is not None:
                                sp_, cp, m = prev["s"], prev["c"], prev["n"]
                                wait(pe, "hlo_ready", 2 * m + 2)
                                wait(pe, "wadlo_ready", m + 1)
                                if i is not None:
                                    wait(pe, "we_ready", n + 1)
                                for t in range(TC):
                                    wait(pe, "acc_ready", TC * (m - 1) + t + 1)
                                    if t == 2 and nxt is not None:
                                        wait(pe, "xef_ready", KT * nxt["n"] + KT)
                                    tok = slice(t * P, (t + 1) * P)
                                    terms = [((h0hi[:, cp, tok], h0lo[:, cp, tok]), weights(sp_, WD, WD + D)),
                                             ((h1hi[:, cp, tok], h1lo[:, cp, tok]), weights(sp_, WD + D, WD + 2 * D))]
                                    split_product(psum[DOWN_BANKS[t]][:, 0:D], terms, True, True
                                                  ).then_inc(q8["dn_done"], 1)

                        mixed(item_of(0, 0, 0))
                        over_items(pe, body)

                    @block.vector
                    def _(dve):
                        def mix(i):
                            n = i["n"]
                            for k in range(KT):
                                wait(dve, "mu_done", KT * n + k + 1)
                                wait(dve, "xhi_ready", KT * (n - 1) + k + 1)
                                wait(dve, "xlo_ready", KT * (n - 1) + k + 1)
                                nc.vector.tensor_tensor(xef[:, k, :], psum[k][:, :], hT[:, k, cols(i)], ALU.add
                                                        ).then_inc(q8["xef_ready"], 1)
                            for k in range(KT):
                                wait(dve, "xhi_ready", KT * n + k + 1)
                                nc.vector.tensor_tensor(xlo[:, i["c"], k, :], xef[:, k, :], xhi[:, i["c"], k, :].bitcast(F32),
                                                        ALU.subtract).then_inc(q8["xlo_ready"], 1)

                        def accumulate(prev, ts):
                            m = prev["n"]
                            col = prev["g"]
                            for t in ts:
                                g = prev["c"] * TC + t
                                wait(dve, "dn_done", TC * m + t + 1)
                                wait(dve, "acc_ready", TC * (m - NCH) + t + 1)
                                nc.vector.scalar_tensor_tensor(x[:, g, :], psum[DOWN_BANKS[t]][:, 0:D],
                                                               scal[:, g, ds(col, 1)], x[:, g, :], ALU.mult, ALU.add
                                                               ).then_inc(q8["acc_ready"], 1)

                        def body(prev, i, nxt):
                            if i is not None:
                                n, c = i["n"], i["c"]
                                wait(dve, "qa_done", n + 1)
                                wait(dve, "we_ready", n + 1)
                                nc.vector.tensor_tensor(waf, psum[2][:, :], we[:, c, :], ALU.mult
                                                        ).then_inc(q8["waf_ready"], 1)
                                wait(dve, "wahi_ready", n + 1)
                                nc.vector.tensor_tensor(walo[:, :], waf, wahi[:, :].bitcast(F32), ALU.subtract
                                                        ).then_inc(q8["walo_ready"], 1)
                            if nxt is not None:
                                mix(nxt)
                            if prev is not None:
                                m, cp = prev["n"], prev["c"]
                                wait(dve, "dq_done", m + 1)
                                nc.vector.tensor_tensor(h1f[UB:P, :], psum[7][UB:P, :], we[UB:P, cp, :], ALU.mult
                                                        ).then_inc(q8["wadf_ready"], 1)
                                wait(dve, "wadhi_ready", m + 1)
                                nc.vector.tensor_tensor(h1lo[UB:P, cp, :], h1f[UB:P, :],
                                                        h1hi[UB:P, cp, :].bitcast(F32), ALU.subtract
                                                        ).then_inc(q8["wadlo_ready"], 1)
                            if i is not None:
                                n, c = i["n"], i["c"]
                                wait(dve, "dn_done", TC * (n - 1))
                                wait(dve, "t_done", 3 * n + 2)
                                wait(dve, "sg_ready", 2 * n + 1)
                                wait(dve, "hlo_ready", 2 * n)
                                nc.vector.tensor_tensor(h0f, sg0, psum[5][:, :], ALU.mult
                                                        ).then_inc(q8["hf_ready"], 1)
                            if prev is not None:
                                accumulate(prev, [0])
                            if i is not None:
                                wait(dve, "t_done", 3 * n + 3)
                                wait(dve, "sg_ready", 2 * n + 2)
                                nc.vector.tensor_tensor(h1f[0:IB, :], sg1[:, :], psum[6][UB:UB + IB, :], ALU.mult
                                                        ).then_inc(q8["hf_ready"], 1)
                            if prev is not None:
                                accumulate(prev, range(1, TC))
                            if i is not None:
                                wait(dve, "hhi_ready", 2 * n + 1)
                                nc.vector.tensor_tensor(h0lo[:, c, :], h0f, h0hi[:, c, :].bitcast(F32),
                                                        ALU.subtract).then_inc(q8["hlo_ready"], 1)
                                wait(dve, "hhi_ready", 2 * n + 2)
                                nc.vector.tensor_tensor(h1lo[0:IB, c, :], h1f[0:IB, :],
                                                        h1hi[0:IB, c, :].bitcast(F32), ALU.subtract
                                                        ).then_inc(q8["hlo_ready"], 1)

                        mix(item_of(0, 0, 0))
                        wait(dve, "zero_ready", 2)
                        over_items(dve, body)

                    @block.scalar
                    def _(act):
                        def mix(i):
                            for k in range(KT):
                                wait(act, "xef_ready", KT * i["n"] + k + 1)
                                nc.scalar.activation(xhi[:, i["c"], k, :], xef[:, k, :], ACT.Copy
                                                     ).then_inc(q8["xhi_ready"], 1)

                        def high(i, part):
                            g = i["g"]
                            if isinstance(g, int) and g == G1 - 1:
                                return
                            act.wait_ge(scaled_ready, g + 2)
                            if part == 0:
                                wait(act, "t_done", 3 * NCH * g)
                            else:
                                wait(act, "dn_done", TC * NCH * g)
                            high_part(1 - i["s"], part)

                        def body(prev, i, nxt):
                            if i is not None:
                                n, c = i["n"], i["c"]
                                wait(act, "we_done", n + 1)
                                wait(act, "wadf_ready", n - 1)
                                nc.scalar.activation(we[:, c, :], psum[3][:, :], ACT.Copy).then_inc(q8["we_ready"], 1)
                                wait(act, "waf_ready", n + 1)
                                nc.scalar.activation(wahi[:, :], waf, ACT.Copy).then_inc(q8["wahi_ready"], 1)
                            if i is not None and i["c"] == 1:
                                high(i, 1)
                            if nxt is not None:
                                mix(nxt)
                            if prev is not None:
                                m, cp = prev["n"], prev["c"]
                                wait(act, "wadf_ready", m + 1)
                                nc.scalar.activation(h1hi[UB:P, cp, :], h1f[UB:P, :], ACT.Copy
                                                     ).then_inc(q8["wadhi_ready"], 1)
                            if i is not None:
                                n, c = i["n"], i["c"]
                                wait(act, "t_done", 3 * n + 1)
                                wait(act, "hf_ready", 2 * n)
                                nc.scalar.activation(sg0, psum[4][:, :], ACT.Silu).then_inc(q8["sg_ready"], 1)
                                wait(act, "t_done", 3 * n + 3)
                                nc.scalar.activation(sg1[:, :], psum[6][0:IB, :], ACT.Silu).then_inc(q8["sg_ready"], 1)
                                wait(act, "hf_ready", 2 * n + 1)
                                nc.scalar.activation(h0hi[:, c, :], h0f, ACT.Copy).then_inc(q8["hhi_ready"], 1)
                                wait(act, "hf_ready", 2 * n + 2)
                                nc.scalar.activation(h1hi[0:IB, c, :], h1f[0:IB, :], ACT.Copy
                                                     ).then_inc(q8["hhi_ready"], 1)
                                if c == 0:
                                    high(i, 0)

                        mix(item_of(0, 0, 0))
                        nc.scalar.preload_act_table(ACT.Silu)
                        act.wait_ge(q8["zero_ready"], 2)
                        over_items(act, body)


def layouts(i):
    import numpy as np

    def T_(a):
        return np.ascontiguousarray(np.swapaxes(a, -1, -2))

    ctx = i["ctx_2048"]
    r = {}
    r["x_in"] = i["x"].reshape(T, D)
    r["ctxT_in"] = T_(ctx.reshape(T, D))
    r["ctxTt_in"] = T_(ctx.reshape(NT, P, D))
    r["ctx2_in"] = ctx
    r["mask_in"] = T_(i["mask_BxS2_ik0"])
    r["gx_in"] = i["g_xattn"]
    r["gf_in"] = i["g_ffn"]
    for n in "qkvo":
        r[f"w{n}_in"] = T_(i[f"L0_xattn_W{n}"])
    r["bqk_in"] = T_(np.stack([i["L0_xattn_bq"], i["L0_xattn_bk"]]).reshape(2 * KT, P))
    r["rows_in"] = np.stack([i[f"L0_xattn_{n}"] for n in ("bv", "bo", "ln_gamma", "ln_beta")])
    r["rs_in"] = np.reshape(i["L0_xattn_residual_scale"], (1,))
    r["rw1_in"] = i["L0_ffn_rw1"]
    r["rw2_in"] = i["L0_ffn_rw2"]
    r["w1_in"] = i["L0_ffn_w1"]
    r["b1_in"] = T_(i["L0_ffn_b1"].reshape(E0 * C0, P))
    r["w2_in"] = i["L0_ffn_w2"]
    r["b2_in"] = i["L0_ffn_b2"]
    r["gw_in"] = T_(i["L1_ffn_gate_weight"])
    r["inv_in"] = i["L1_ffn_inv_mapping"].reshape(E1)
    mu = T_(i["L1_ffn_mask_up_W"])
    r["mu_in"] = np.concatenate([mu, mu, mu], axis=1)

    def three(gate, up):
        gap = np.zeros(gate.shape[:-1] + (UB - IB,), gate.dtype)
        return np.concatenate([gate[..., :P], up[..., :P], gate[..., P:], gap, up[..., P:], gap], axis=-1)

    def by_slice(a):
        n, _, c = a.shape
        return a.reshape(n, KT, P, c).transpose(0, 2, 1, 3).reshape(n, P, KT * c)

    def down(a, tail):
        n = a.shape[0]
        gap = np.zeros((n, UB - IB, a.shape[2]), a.dtype)
        rest = np.concatenate([a[:, P:], gap, tail], axis=1)
        return np.concatenate([a[:, :P], rest], axis=2)

    g = {k: i["L1_ffn_" + k] for k in ("gate_W", "gate_qa", "gate_qb", "gate_scale", "up_W", "up_qa", "up_qb",
                                       "up_scale", "down_W", "down_qa", "down_qb", "down_scale")}
    inner = [T_(g[k].reshape(G1, KR, -1)) for k in ("gate_qa", "up_qa")]
    wx = by_slice(np.concatenate([three(T_(g["gate_W"]), T_(g["up_W"]))] + inner, axis=2))
    outer = [g[k].transpose(0, 1, 3, 2).reshape(G1, KR, -1) for k in ("gate_qb", "up_qb", "down_qb")]
    z = np.zeros_like(outer[0])
    wl = np.concatenate([three(outer[0], z), three(z, outer[1])], axis=1)
    wd = down(T_(g["down_W"]), outer[2])
    qa = T_(g["down_qa"].reshape(G1, KR, I1))
    qa = np.concatenate([np.zeros_like(qa), qa], axis=2)
    wa = down(qa, np.zeros((G1, KR, P), qa.dtype))
    r["wf_in"] = np.concatenate([wx, wl, wd, wa], axis=2)
    zs = np.zeros_like(g["gate_scale"])
    r["sc_in"] = np.stack([np.concatenate([three(g["gate_scale"], zs), np.zeros_like(g["down_scale"])], axis=1),
                           np.concatenate([three(zs, g["up_scale"]), g["down_scale"]], axis=1)], axis=1)
    sg, su = (i[f"L1_ffn_sh_{n}_W"].reshape(NS, I1, D) for n in ("gate", "up"))
    sd = T_(i["L1_ffn_sh_down_W"]).reshape(NS, I1, D)
    tail = np.zeros((NS, KR, D), sd.dtype)
    r["ws_in"] = np.concatenate([by_slice(three(T_(sg), T_(su))), down(sd, tail)], axis=2)
    return {k: np.ascontiguousarray(v) for k, v in r.items()}


ORDER = ["x_in", "ctxT_in", "ctxTt_in", "ctx2_in", "mask_in", "gx_in", "gf_in", "wq_in", "wk_in", "wv_in", "wo_in",
         "bqk_in", "rows_in", "rs_in", "rw1_in", "rw2_in", "w1_in", "b1_in", "w2_in", "b2_in", "gw_in", "inv_in",
         "mu_in", "wf_in", "sc_in", "ws_in"]


def kernel(**inputs):
    import numpy as np
    from concourse import bacc
    from concourse.bass_utils import run_bass_kernel_spmd

    nc = bacc.Bacc("TRN2", target_bir_lowering=False, num_devices=1)
    arrays = layouts({k: np.asarray(v) for k, v in inputs.items()})
    args = [nc.dram_tensor(n, arrays[n].shape, mybir.dt.from_np(arrays[n].dtype), kind="ExternalInput").ap()
            for n in ORDER]
    out = nc.dram_tensor("out", (T, D), F32, kind="ExternalOutput").ap()
    build(nc, *args, out)
    r = run_bass_kernel_spmd(nc, [arrays], core_ids=[0])
    return r.results[0]["out"].reshape(B, S, D)
```
